# Optimizing a Trainium2 kernel written in Bass

```python
import numpy as np
import jax
import jax.numpy as jnp

def _softmax(x, axis=-1):
    return jax.nn.softmax(x, axis=axis)

def _gelu(x):
    return jax.nn.gelu(x, approximate=True)

def _silu(x):
    return jax.nn.silu(x)

def _sigmoid(x):
    return jax.nn.sigmoid(x)

def _layernorm(x, axis=-1, eps=1e-05):
    m = jnp.mean(x, axis=axis, keepdims=True)
    v = jnp.var(x, axis=axis, keepdims=True)
    return (x - m) / jnp.sqrt(v + eps)

def _scatter_add(tgt, idx, src, axis=0):
    return tgt.at[idx].add(src)

def _segment_sum(src, seg, n):
    return jax.ops.segment_sum(src, seg, n)
kernel_name = 'mk_flamingo_gated_d4_seqx_r4_955b7f'

def setup_inputs(seed: int=0):
    np.random.seed(seed)
    _w = jnp.asarray

    def _rec_inputs():
        import jax
        import jax.numpy as jnp
        _rk = jax.random.key(seed)
        x = -0.0002928 + 1 * jax.random.normal(jax.random.fold_in(_rk, 1), (8, 256, 256), jnp.float32)
        _lenS = 256 - jax.random.randint(jax.random.fold_in(_rk, 7), (8,), 0, max(1, 256 // 4) + 1, jnp.int32)
        _lenS2 = 256 - jax.random.randint(jax.random.fold_in(_rk, 8), (8,), 0, max(1, 256 // 4) + 1, jnp.int32)
        _ctx_1024P = jax.random.normal(jax.random.fold_in(_rk, 11), (8, 16, 256), jnp.float32)
        _ctx_1024c = jax.random.dirichlet(jax.random.fold_in(_rk, 511), 0.3 * jnp.ones((16,), jnp.float32), (8, 256))
        _ctx_1024t = jnp.einsum('bsk,bkd->bsd', _ctx_1024c, _ctx_1024P)
        _ctx_1024t = _ctx_1024t * jax.lax.rsqrt(jnp.mean(jnp.square(_ctx_1024t)) + 1e-12) * 0.953939
        ctx_1024 = -1.39393e-06 + 0.999914 * (_ctx_1024t + 0.3 * jax.random.normal(jax.random.fold_in(_rk, 611), (8, 256, 256), jnp.float32))
        _validS = jnp.arange(256)[None, :] < _lenS[:, None]
        _validS2 = jnp.arange(256)[None, :] < _lenS2[:, None]
        _causal = jnp.tril(jnp.ones((256, 256), dtype=bool))
        mask_BxSxS2_ff0 = jnp.where(jnp.ones((8, 256, 256), dtype=bool), 0.0, -1000000000.0).astype(jnp.float32)
        _g = jax.random.normal(jax.random.fold_in(_rk, 9001), (2, 4), jnp.float32)
        _g = jnp.sign(_g) * jnp.maximum(jnp.abs(_g), 1.0) + (_g == 0) * 1.0
        g_xattn = _g[0]
        g_ffn = _g[1]
        return (x, ctx_1024, mask_BxSxS2_ff0, g_xattn, g_ffn)
    x, ctx_1024, mask_BxSxS2_ff0, g_xattn, g_ffn = _rec_inputs()

    def _L0_xattn_setup():
        import jax, jax.numpy as jnp
        import numpy as np
        _NEG_INF_FP32 = -1000000000.0
        B, L, D, H = (2, 512, 256, 16)

        def _split_heads(t, heads):
            b, l, d = t.shape
            return t.reshape(b, l, heads, d // heads).transpose(0, 2, 1, 3)
        key = jax.random.key(seed)
        ks = jax.random.split(key, 6)
        s = 0.02
        return {'x': jax.random.normal(ks[0], (B, L, D), jnp.float32), 'y': jax.random.normal(ks[1], (B, L, D), jnp.float32), 'bias': jnp.zeros((B, L, L), jnp.float32), 'Wq': jax.random.normal(ks[2], (D, D), jnp.float32) * s, 'Wk': jax.random.normal(ks[3], (D, D), jnp.float32) * s, 'Wv': jax.random.normal(ks[4], (D, D), jnp.float32) * s, 'Wo': jax.random.normal(ks[5], (D, D), jnp.float32) * s}
    _L0_xattn_all = _L0_xattn_setup()
    _L0_xattn_in = {k: v for k, v in _L0_xattn_all.items() if k in ('Wq', 'Wk', 'Wv', 'Wo')}
    del _L0_xattn_all

    def _L0_ffn_setup():
        import jax, jax.numpy as jnp
        import numpy as np
        HIDDEN = 256
        INNER = 1024

        def _weight_quant(w):
            scale = 1.0 / jnp.clip(jnp.mean(jnp.abs(w)), 1e-05)
            wq = jnp.clip(jnp.round(w * scale), -1.0, 1.0) / scale
            return w + jax.lax.stop_gradient(wq - w)

        def _act_quant(x):
            scale = 127.0 / jnp.clip(jnp.max(jnp.abs(x), axis=-1, keepdims=True), 1e-05)
            xq = jnp.clip(jnp.round(x * scale), -128.0, 127.0) / scale
            return x + jax.lax.stop_gradient(xq - x)

        def _bitlinear(x, w):
            return jnp.einsum('bsi,oi->bso', _act_quant(x), _weight_quant(w))
        key = jax.random.key(seed)
        k0, k1, k2, k3 = jax.random.split(key, 4)
        x = jax.random.normal(k0, (4, 512, HIDDEN), dtype=jnp.float32)
        w_gate = jax.random.normal(k1, (INNER, HIDDEN), dtype=jnp.float32) / np.sqrt(HIDDEN)
        w_up = jax.random.normal(k2, (INNER, HIDDEN), dtype=jnp.float32) / np.sqrt(HIDDEN)
        w_down = jax.random.normal(k3, (HIDDEN, INNER), dtype=jnp.float32) / np.sqrt(INNER)
        return {'x': x, 'w_gate': w_gate, 'w_up': w_up, 'w_down': w_down}
    _L0_ffn_all = _L0_ffn_setup()
    _L0_ffn_in = {k: v for k, v in _L0_ffn_all.items() if k in ('w_gate', 'w_up', 'w_down')}
    del _L0_ffn_all

    def _L1_xattn_setup():
        import jax, jax.numpy as jnp
        import numpy as np
        B, S, E, NH = (1, 512, 256, 8)
        DH = E // NH
        EPS = 1e-06
        LN_EPS = 1e-05
        key = jax.random.key(seed)
        ks = jax.random.split(key, 8)
        q = jax.random.normal(ks[0], (B, S, E), dtype=jnp.float32)
        k = jax.random.normal(ks[1], (B, S, E), dtype=jnp.float32)
        v = jax.random.normal(ks[2], (B, S, E), dtype=jnp.float32)
        scale = 1.0 / np.sqrt(3 * E)
        igate_w = jax.random.normal(ks[3], (NH, 3 * E), dtype=jnp.float32) * scale
        igate_b = jax.random.normal(ks[4], (NH,), dtype=jnp.float32) * 0.1
        fgate_w = jax.random.normal(ks[5], (NH, 3 * E), dtype=jnp.float32) * scale
        fgate_b = jnp.linspace(3.0, 6.0, NH, dtype=jnp.float32)
        out_w = 1.0 + 0.1 * jax.random.normal(ks[6], (E,), dtype=jnp.float32)
        return {'q': q, 'k': k, 'v': v, 'igate_w': igate_w, 'igate_b': igate_b, 'fgate_w': fgate_w, 'fgate_b': fgate_b, 'out_w': out_w}
    _L1_xattn_all = _L1_xattn_setup()
    _L1_xattn_in = {k: v for k, v in _L1_xattn_all.items() if k in ('igate_w', 'igate_b', 'fgate_w', 'fgate_b', 'out_w')}
    del _L1_xattn_all

    def _L1_ffn_setup():
        import jax, jax.numpy as jnp
        import numpy as np
        DIM = 256
        HID = 1024
        NUM_EXPERTS = 8
        TOP_K = 2
        ALPHA = 2.0
        B, S = (4, 512)

        def _swiglu(x, wu, wg, wd):
            up = x @ wu
            g = x @ wg
            gate = jax.nn.sigmoid(g) * g
            return up * gate @ wd
        key = jax.random.key(seed)
        ks = jax.random.split(key, 8)
        x = jax.random.normal(ks[0], (B, S, DIM), dtype=jnp.float32)
        Wr = jax.random.normal(ks[1], (DIM, NUM_EXPERTS), dtype=jnp.float32) * 0.02
        Wu = jax.random.normal(ks[2], (NUM_EXPERTS - 1, DIM, HID), dtype=jnp.float32) * 0.02
        Wg = jax.random.normal(ks[3], (NUM_EXPERTS - 1, DIM, HID), dtype=jnp.float32) * 0.02
        Wd = jax.random.normal(ks[4], (NUM_EXPERTS - 1, HID, DIM), dtype=jnp.float32) * 0.002
        Wu_s = jax.random.normal(ks[5], (DIM, HID), dtype=jnp.float32) * 0.02
        Wg_s = jax.random.normal(ks[6], (DIM, HID), dtype=jnp.float32) * 0.02
        Wd_s = jax.random.normal(ks[7], (HID, DIM), dtype=jnp.float32) * 0.002
        return {'x': x, 'Wr': Wr, 'Wu': Wu, 'Wg': Wg, 'Wd': Wd, 'Wu_s': Wu_s, 'Wg_s': Wg_s, 'Wd_s': Wd_s}
    _L1_ffn_all = _L1_ffn_setup()
    _L1_ffn_in = {k: v for k, v in _L1_ffn_all.items() if k in ('Wr', 'Wu', 'Wg', 'Wd', 'Wu_s', 'Wg_s', 'Wd_s')}
    del _L1_ffn_all

    def _L2_xattn_setup():
        import jax, jax.numpy as jnp
        import numpy as np
        EMBED = 256
        HEADS = 16
        HEAD_DIM = EMBED // HEADS
        key = jax.random.key(seed)
        ks = jax.random.split(key, 11)
        B, T, E = (2, 512, EMBED)
        s = 1.0 / np.sqrt(E)
        return {'query': jax.random.normal(ks[0], (B, T, E), jnp.float32), 'key': jax.random.normal(ks[1], (B, T, E), jnp.float32), 'value': jax.random.normal(ks[2], (B, T, E), jnp.float32), 'wq': jax.random.normal(ks[3], (E, E), jnp.float32) * s, 'bq': jnp.zeros((E,), jnp.float32), 'wk': jax.random.normal(ks[4], (E, E), jnp.float32) * s, 'bk': jnp.zeros((E,), jnp.float32), 'wv': jax.random.normal(ks[5], (E, E), jnp.float32) * s, 'bv': jnp.zeros((E,), jnp.float32), 'wo': jax.random.normal(ks[6], (E, E), jnp.float32) * s, 'bo': jnp.zeros((E,), jnp.float32)}
    _L2_xattn_all = _L2_xattn_setup()
    _L2_xattn_in = {k: v for k, v in _L2_xattn_all.items() if k in ('wq', 'bq', 'wk', 'bk', 'wv', 'bv', 'wo', 'bo')}
    del _L2_xattn_all

    def _L2_ffn_setup():
        import jax, jax.numpy as jnp
        import numpy as np
        B, S, H, E, DFF = (4, 1024, 256, 8, 1024)
        key = jax.random.key(seed)
        k0, k1, k2, k3 = jax.random.split(key, 4)
        hidden_states = jax.random.normal(k0, (B, S, H), dtype=jnp.float32)
        gate_w = jax.random.normal(k1, (E, H), dtype=jnp.float32) * 0.02
        w1 = jax.random.normal(k2, (E, H, DFF), dtype=jnp.float32) * 0.02
        b1 = jnp.zeros((E, DFF), dtype=jnp.float32)
        w2 = jax.random.normal(k3, (E, DFF, H), dtype=jnp.float32) * 0.02
        b2 = jnp.zeros((E, H), dtype=jnp.float32)
        return {'hidden_states': hidden_states, 'gate_w': gate_w, 'w1': w1, 'b1': b1, 'w2': w2, 'b2': b2}
    _L2_ffn_all = _L2_ffn_setup()
    _L2_ffn_in = {k: v for k, v in _L2_ffn_all.items() if k in ('gate_w', 'w1', 'b1', 'w2', 'b2')}
    del _L2_ffn_all

    def _L3_xattn_setup():
        import math
        import jax, jax.numpy as jnp
        import numpy as np
        B, S, H, NH = (2, 512, 256, 4)
        DH = H // NH

        def _mlstm_parallel(qh, kh, vh, ig, fg, eps=1e-06):
            b, nh, s, dh = qh.shape
            log_f = jax.nn.log_sigmoid(fg)
            pcs = jnp.pad(jnp.cumsum(log_f, axis=-1), ((0, 0), (0, 0), (1, 0)))
            mat = pcs[..., :, None] - pcs[..., None, :]
            ltr = jnp.tril(jnp.ones((s, s), dtype=bool))
            log_fg_matrix = jnp.where(ltr, mat[..., 1:, 1:], -jnp.inf)
            log_D = log_fg_matrix + ig[..., None, :]
            max_log_D = jnp.max(log_D, axis=-1, keepdims=True)
            D = jnp.exp(log_D - max_log_D)
            qk = jnp.einsum('bhsd,bhtd->bhst', qh, kh) / math.sqrt(dh)
            C = qk * D
            normalizer = jnp.maximum(jnp.abs(C.sum(axis=-1, keepdims=True)), jnp.exp(-max_log_D))
            Cn = C / (normalizer + eps)
            return jnp.einsum('bhst,bhtd->bhsd', Cn, vh)
        key = jax.random.key(seed)
        ks = jax.random.split(key, 8)
        gate_std = 1.0 / math.sqrt(3 * H)
        return {'q': jax.random.normal(ks[0], (B, S, H), jnp.float32), 'k': jax.random.normal(ks[1], (B, S, H), jnp.float32), 'v': jax.random.normal(ks[2], (B, S, H), jnp.float32), 'w_igate': jax.random.normal(ks[3], (NH, 3 * H), jnp.float32) * gate_std, 'b_igate': jax.random.normal(ks[4], (NH,), jnp.float32) * 0.1, 'w_fgate': jax.random.normal(ks[5], (NH, 3 * H), jnp.float32) * gate_std, 'b_fgate': jnp.linspace(3.4, 6.0, NH, dtype=jnp.float32), 'ln_weight': jnp.zeros((H,), jnp.float32)}
    _L3_xattn_all = _L3_xattn_setup()
    _L3_xattn_in = {k: v for k, v in _L3_xattn_all.items() if k in ('w_igate', 'b_igate', 'w_fgate', 'b_fgate', 'ln_weight')}
    del _L3_xattn_all

    def _L3_ffn_setup():
        import jax, jax.numpy as jnp
        import numpy as np
        E = 8
        K = 2
        C = 256
        F = 512
        EPS = 1e-05
        key = jax.random.key(seed)
        ks = jax.random.split(key, 6)
        x = jax.random.normal(ks[0], (2, 256, C), dtype=jnp.float32)
        ln_gamma = 1.0 + 0.02 * jax.random.normal(ks[1], (C,), dtype=jnp.float32)
        ln_beta = 0.02 * jax.random.normal(ks[2], (C,), dtype=jnp.float32)
        gate_w = jax.random.normal(ks[3], (E, C), dtype=jnp.float32) / np.sqrt(C)
        w1 = jax.random.normal(ks[4], (E, F, C), dtype=jnp.float32) / np.sqrt(C)
        w2 = jax.random.normal(ks[5], (E, C, F), dtype=jnp.float32) / np.sqrt(F)
        return {'x': x, 'ln_gamma': ln_gamma, 'ln_beta': ln_beta, 'gate_w': gate_w, 'w1': w1, 'w2': w2}
    _L3_ffn_all = _L3_ffn_setup()
    _L3_ffn_in = {k: v for k, v in _L3_ffn_all.items() if k in ('ln_gamma', 'ln_beta', 'gate_w', 'w1', 'w2')}
    del _L3_ffn_all
    return {'x': x, 'ctx_1024': ctx_1024, 'mask_BxSxS2_ff0': mask_BxSxS2_ff0, 'g_xattn': g_xattn, 'g_ffn': g_ffn, 'L0_xattn_Wq': _L0_xattn_in['Wq'], 'L0_xattn_Wk': _L0_xattn_in['Wk'], 'L0_xattn_Wv': _L0_xattn_in['Wv'], 'L0_xattn_Wo': _L0_xattn_in['Wo'], 'L0_ffn_w_gate': _L0_ffn_in['w_gate'], 'L0_ffn_w_up': _L0_ffn_in['w_up'], 'L0_ffn_w_down': _L0_ffn_in['w_down'], 'L1_xattn_igate_w': _L1_xattn_in['igate_w'], 'L1_xattn_igate_b': _L1_xattn_in['igate_b'], 'L1_xattn_fgate_w': _L1_xattn_in['fgate_w'], 'L1_xattn_fgate_b': _L1_xattn_in['fgate_b'], 'L1_xattn_out_w': _L1_xattn_in['out_w'], 'L1_ffn_Wr': _L1_ffn_in['Wr'], 'L1_ffn_Wu': _L1_ffn_in['Wu'], 'L1_ffn_Wg': _L1_ffn_in['Wg'], 'L1_ffn_Wd': _L1_ffn_in['Wd'], 'L1_ffn_Wu_s': _L1_ffn_in['Wu_s'], 'L1_ffn_Wg_s': _L1_ffn_in['Wg_s'], 'L1_ffn_Wd_s': _L1_ffn_in['Wd_s'], 'L2_xattn_wq': _L2_xattn_in['wq'], 'L2_xattn_bq': _L2_xattn_in['bq'], 'L2_xattn_wk': _L2_xattn_in['wk'], 'L2_xattn_bk': _L2_xattn_in['bk'], 'L2_xattn_wv': _L2_xattn_in['wv'], 'L2_xattn_bv': _L2_xattn_in['bv'], 'L2_xattn_wo': _L2_xattn_in['wo'], 'L2_xattn_bo': _L2_xattn_in['bo'], 'L2_ffn_gate_w': _L2_ffn_in['gate_w'], 'L2_ffn_w1': _L2_ffn_in['w1'], 'L2_ffn_b1': _L2_ffn_in['b1'], 'L2_ffn_w2': _L2_ffn_in['w2'], 'L2_ffn_b2': _L2_ffn_in['b2'], 'L3_xattn_w_igate': _L3_xattn_in['w_igate'], 'L3_xattn_b_igate': _L3_xattn_in['b_igate'], 'L3_xattn_w_fgate': _L3_xattn_in['w_fgate'], 'L3_xattn_b_fgate': _L3_xattn_in['b_fgate'], 'L3_xattn_ln_weight': _L3_xattn_in['ln_weight'], 'L3_ffn_ln_gamma': _L3_ffn_in['ln_gamma'], 'L3_ffn_ln_beta': _L3_ffn_in['ln_beta'], 'L3_ffn_gate_w': _L3_ffn_in['gate_w'], 'L3_ffn_w1': _L3_ffn_in['w1'], 'L3_ffn_w2': _L3_ffn_in['w2']}

def reference(x, ctx_1024, mask_BxSxS2_ff0, g_xattn, g_ffn, L0_xattn_Wq, L0_xattn_Wk, L0_xattn_Wv, L0_xattn_Wo, L0_ffn_w_gate, L0_ffn_w_up, L0_ffn_w_down, L1_xattn_igate_w, L1_xattn_igate_b, L1_xattn_fgate_w, L1_xattn_fgate_b, L1_xattn_out_w, L1_ffn_Wr, L1_ffn_Wu, L1_ffn_Wg, L1_ffn_Wd, L1_ffn_Wu_s, L1_ffn_Wg_s, L1_ffn_Wd_s, L2_xattn_wq, L2_xattn_bq, L2_xattn_wk, L2_xattn_bk, L2_xattn_wv, L2_xattn_bv, L2_xattn_wo, L2_xattn_bo, L2_ffn_gate_w, L2_ffn_w1, L2_ffn_b1, L2_ffn_w2, L2_ffn_b2, L3_xattn_w_igate, L3_xattn_b_igate, L3_xattn_w_fgate, L3_xattn_b_fgate, L3_xattn_ln_weight, L3_ffn_ln_gamma, L3_ffn_ln_beta, L3_ffn_gate_w, L3_ffn_w1, L3_ffn_w2):
    import jax
    import jax.numpy as jnp

    def _L0_xattn_ref(x, y, bias, Wq, Wk, Wv, Wo):
        import jax, jax.numpy as jnp
        import numpy as np
        _NEG_INF_FP32 = -1000000000.0
        B, L, D, H = (2, 512, 256, 16)

        def _split_heads(t, heads):
            b, l, d = t.shape
            return t.reshape(b, l, heads, d // heads).transpose(0, 2, 1, 3)
        q = _split_heads(x @ Wq, H)
        k = _split_heads(y @ Wk, H)
        v = _split_heads(y @ Wv, H)
        depth = k.shape[-1]
        scale = jnp.asarray(depth, q.dtype) ** (-0.5)
        logits = jnp.einsum('bhqd,bhkd->bhqk', q, k) * scale
        logits = logits + bias[:, None, :, :] * _NEG_INF_FP32
        weights = jax.nn.softmax(logits, axis=-1)
        out = jnp.einsum('bhqk,bhkd->bhqd', weights, v)
        out = out.transpose(0, 2, 1, 3).reshape(x.shape[0], x.shape[1], D)
        return out @ Wo

    def _L0_ffn_ref(x, w_gate, w_up, w_down):
        import jax, jax.numpy as jnp
        import numpy as np
        HIDDEN = 256
        INNER = 1024

        def _weight_quant(w):
            scale = 1.0 / jnp.clip(jnp.mean(jnp.abs(w)), 1e-05)
            wq = jnp.clip(jnp.round(w * scale), -1.0, 1.0) / scale
            return w + jax.lax.stop_gradient(wq - w)

        def _act_quant(x):
            scale = 127.0 / jnp.clip(jnp.max(jnp.abs(x), axis=-1, keepdims=True), 1e-05)
            xq = jnp.clip(jnp.round(x * scale), -128.0, 127.0) / scale
            return x + jax.lax.stop_gradient(xq - x)

        def _bitlinear(x, w):
            return jnp.einsum('bsi,oi->bso', _act_quant(x), _weight_quant(w))
        gate = jax.nn.silu(_bitlinear(x, w_gate))
        up = _bitlinear(x, w_up)
        return _bitlinear(gate * up, w_down)

    def _L1_xattn_ref(q, k, v, igate_w, igate_b, fgate_w, fgate_b, out_w):
        import jax, jax.numpy as jnp
        import numpy as np
        B, S, E, NH = (1, 512, 256, 8)
        DH = E // NH
        EPS = 1e-06
        LN_EPS = 1e-05
        Bq, Sq, Eq = q.shape
        nh = igate_b.shape[0]
        dh = Eq // nh
        gi = jnp.concatenate([q, k, v], axis=-1)
        ig = (gi @ igate_w.T + igate_b).transpose(0, 2, 1)
        fg = (gi @ fgate_w.T + fgate_b).transpose(0, 2, 1)
        qh = q.reshape(Bq, Sq, nh, dh).transpose(0, 2, 1, 3)
        kh = k.reshape(Bq, Sq, nh, dh).transpose(0, 2, 1, 3)
        vh = v.reshape(Bq, Sq, nh, dh).transpose(0, 2, 1, 3)
        log_f = jax.nn.log_sigmoid(fg)
        cs = jnp.cumsum(log_f, axis=-1)
        diff = cs[..., :, None] - cs[..., None, :]
        mask = jnp.tril(jnp.ones((Sq, Sq), dtype=bool))
        log_fg_mat = jnp.where(mask, diff, -jnp.inf)
        log_D = log_fg_mat + ig[..., None, :]
        max_log_D = jnp.max(log_D, axis=-1, keepdims=True)
        D = jnp.exp(log_D - max_log_D)
        qk = jnp.einsum('bhsd,bhtd->bhst', qh, kh) / jnp.sqrt(jnp.float32(dh))
        C = qk * D
        normalizer = jnp.maximum(jnp.abs(C.sum(-1, keepdims=True)), jnp.exp(-max_log_D))
        h = jnp.einsum('bhst,bhtd->bhsd', C / (normalizer + EPS), vh)
        mean = h.mean(-1, keepdims=True)
        var = ((h - mean) ** 2).mean(-1, keepdims=True)
        hn = (h - mean) / jnp.sqrt(var + LN_EPS)
        hn = hn * out_w.reshape(nh, dh)[None, :, None, :]
        return hn.transpose(0, 2, 1, 3).reshape(Bq, Sq, Eq)

    def _L1_ffn_ref(x, Wr, Wu, Wg, Wd, Wu_s, Wg_s, Wd_s):
        import jax, jax.numpy as jnp
        import numpy as np
        DIM = 256
        HID = 1024
        NUM_EXPERTS = 8
        TOP_K = 2
        ALPHA = 2.0
        B, S = (4, 512)

        def _swiglu(x, wu, wg, wd):
            up = x @ wu
            g = x @ wg
            gate = jax.nn.sigmoid(g) * g
            return up * gate @ wd
        logits = x @ Wr
        probs = jax.nn.softmax(logits, axis=-1)
        topk_vals, topk_idx = jax.lax.top_k(probs, TOP_K)
        out = jnp.zeros_like(x)
        for i in range(TOP_K - 1):
            p = topk_vals[..., i:i + 1]
            ind = topk_idx[..., i]
            acc = jnp.zeros_like(x)
            for j in range(NUM_EXPERTS - 1):
                mask = (ind == j).astype(x.dtype)[..., None]
                acc = acc + _swiglu(x, Wu[j], Wg[j], Wd[j]) * mask
            out = out + ALPHA * p * acc
        out = out + _swiglu(x, Wu_s, Wg_s, Wd_s)
        return out

    def _L2_xattn_ref(query, key, value, wq, bq, wk, bk, wv, bv, wo, bo):
        import jax, jax.numpy as jnp
        import numpy as np
        EMBED = 256
        HEADS = 16
        HEAD_DIM = EMBED // HEADS
        B, T, E = query.shape
        H, D = (HEADS, HEAD_DIM)
        q = (query @ wq + bq).reshape(B, T, H, D)
        k = (key @ wk + bk).reshape(B, T, H, D)
        v = (value @ wv + bv).reshape(B, T, H, D)
        scale = 1.0 / jnp.sqrt(jnp.asarray(D * H, q.dtype))
        scores = jnp.einsum('btnh,blnh->btnl', q, k) * scale
        attn = jax.nn.softmax(scores, axis=-1)
        attended = jnp.einsum('btnl,blnh->btnh', attn, v).reshape(B, T, H * D)
        return attended @ wo + bo

    def _L2_ffn_ref(hidden_states, gate_w, w1, b1, w2, b2):
        import jax, jax.numpy as jnp
        import numpy as np
        B, S, H, E, DFF = (4, 1024, 256, 8, 1024)
        b, s, h = hidden_states.shape
        x = hidden_states.reshape(-1, h)
        gate_logits = x @ gate_w.T
        gate_probs = jax.nn.softmax(gate_logits, axis=-1)
        expert_idx = jnp.argmax(gate_probs, axis=-1)
        expert_w = jnp.take_along_axis(gate_probs, expert_idx[:, None], axis=1)[:, 0]
        out = jnp.zeros_like(x)
        n_experts = w1.shape[0]
        for e in range(n_experts):
            ye = jax.nn.relu(x @ w1[e] + b1[e]) @ w2[e] + b2[e]
            sel = (expert_idx == e)[:, None]
            out = out + jnp.where(sel, ye * expert_w[:, None], 0.0)
        return out.reshape(b, s, h)

    def _L3_xattn_ref(q, k, v, w_igate, b_igate, w_fgate, b_fgate, ln_weight):
        import math
        import jax, jax.numpy as jnp
        import numpy as np
        B, S, H, NH = (2, 512, 256, 4)
        DH = H // NH

        def _mlstm_parallel(qh, kh, vh, ig, fg, eps=1e-06):
            b, nh, s, dh = qh.shape
            log_f = jax.nn.log_sigmoid(fg)
            pcs = jnp.pad(jnp.cumsum(log_f, axis=-1), ((0, 0), (0, 0), (1, 0)))
            mat = pcs[..., :, None] - pcs[..., None, :]
            ltr = jnp.tril(jnp.ones((s, s), dtype=bool))
            log_fg_matrix = jnp.where(ltr, mat[..., 1:, 1:], -jnp.inf)
            log_D = log_fg_matrix + ig[..., None, :]
            max_log_D = jnp.max(log_D, axis=-1, keepdims=True)
            D = jnp.exp(log_D - max_log_D)
            qk = jnp.einsum('bhsd,bhtd->bhst', qh, kh) / math.sqrt(dh)
            C = qk * D
            normalizer = jnp.maximum(jnp.abs(C.sum(axis=-1, keepdims=True)), jnp.exp(-max_log_D))
            Cn = C / (normalizer + eps)
            return jnp.einsum('bhst,bhtd->bhsd', Cn, vh)
        b, s, h = q.shape
        nh = b_igate.shape[0]
        dh = h // nh
        gin = jnp.concatenate([q, k, v], axis=-1)
        ig = jnp.einsum('bsd,hd->bhs', gin, w_igate) + b_igate[None, :, None]
        fg = jnp.einsum('bsd,hd->bhs', gin, w_fgate) + b_fgate[None, :, None]
        qh = q.reshape(b, s, nh, dh).transpose(0, 2, 1, 3)
        kh = k.reshape(b, s, nh, dh).transpose(0, 2, 1, 3)
        vh = v.reshape(b, s, nh, dh).transpose(0, 2, 1, 3)
        hst = _mlstm_parallel(qh, kh, vh, ig, fg)
        mean = hst.mean(axis=-1, keepdims=True)
        var = hst.var(axis=-1, keepdims=True)
        hn = (hst - mean) / jnp.sqrt(var + 1e-05)
        scale = (1.0 + ln_weight).reshape(nh, dh)
        hn = hn * scale[None, :, None, :]
        return hn.transpose(0, 2, 1, 3).reshape(b, s, h)

    def _L3_ffn_ref(x, ln_gamma, ln_beta, gate_w, w1, w2):
        import jax, jax.numpy as jnp
        import numpy as np
        E = 8
        K = 2
        C = 256
        F = 512
        EPS = 1e-05
        B, T, Cc = x.shape
        xf = x.reshape(-1, Cc)
        mu = jnp.mean(xf, axis=-1, keepdims=True)
        var = jnp.var(xf, axis=-1, keepdims=True)
        rn = (xf - mu) * jax.lax.rsqrt(var + EPS) * ln_gamma + ln_beta
        logits = rn @ gate_w.T
        probs = jax.nn.softmax(logits, axis=-1)
        rw, sel = jax.lax.top_k(probs, K)
        comb = jnp.sum(jax.nn.one_hot(sel, E, dtype=xf.dtype) * rw[..., None], axis=1)
        h = jax.nn.gelu(jnp.einsum('nc,efc->enf', xf, w1), approximate=False)
        y = jnp.einsum('enf,ecf->enc', h, w2)
        out = jnp.einsum('enc,ne->nc', y, comb)
        return out.reshape(B, T, Cc)
    x = x + jnp.tanh(g_xattn[0]) * _L0_xattn_ref(_layernorm(x, axis=-1), ctx_1024, mask_BxSxS2_ff0, L0_xattn_Wq, L0_xattn_Wk, L0_xattn_Wv, L0_xattn_Wo)
    x = x + jnp.tanh(g_ffn[0]) * _L0_ffn_ref(_layernorm(x, axis=-1), L0_ffn_w_gate, L0_ffn_w_up, L0_ffn_w_down)
    x = x + jnp.tanh(g_xattn[1]) * _L1_xattn_ref(_layernorm(x, axis=-1), ctx_1024, ctx_1024, L1_xattn_igate_w, L1_xattn_igate_b, L1_xattn_fgate_w, L1_xattn_fgate_b, L1_xattn_out_w)
    x = x + jnp.tanh(g_ffn[1]) * _L1_ffn_ref(_layernorm(x, axis=-1), L1_ffn_Wr, L1_ffn_Wu, L1_ffn_Wg, L1_ffn_Wd, L1_ffn_Wu_s, L1_ffn_Wg_s, L1_ffn_Wd_s)
    x = x + jnp.tanh(g_xattn[2]) * _L2_xattn_ref(_layernorm(x, axis=-1), ctx_1024, ctx_1024, L2_xattn_wq, L2_xattn_bq, L2_xattn_wk, L2_xattn_bk, L2_xattn_wv, L2_xattn_bv, L2_xattn_wo, L2_xattn_bo)
    x = x + jnp.tanh(g_ffn[2]) * _L2_ffn_ref(_layernorm(x, axis=-1), L2_ffn_gate_w, L2_ffn_w1, L2_ffn_b1, L2_ffn_w2, L2_ffn_b2)
    x = x + jnp.tanh(g_xattn[3]) * _L3_xattn_ref(_layernorm(x, axis=-1), ctx_1024, ctx_1024, L3_xattn_w_igate, L3_xattn_b_igate, L3_xattn_w_fgate, L3_xattn_b_fgate, L3_xattn_ln_weight)
    x = x + jnp.tanh(g_ffn[3]) * _L3_ffn_ref(_layernorm(x, axis=-1), L3_ffn_ln_gamma, L3_ffn_ln_beta, L3_ffn_gate_w, L3_ffn_w1, L3_ffn_w2)
    return x

_drawn_inputs = setup_inputs


def setup_inputs(seed=0):
    import zlib

    import numpy as np

    out = dict(_drawn_inputs(seed))
    spreads = {'L2_xattn_bq': (0.0, 2.0),
     'L2_xattn_bk': (0.0, 2.0),
     'L2_xattn_bv': (0.0, 0.312),
     'L2_xattn_bo': (0.0, 0.319),
     'L2_ffn_b1': (0.0, 2.0),
     'L2_ffn_b2': (0.0, 1.203),
     'L3_xattn_ln_weight': (0.0, 0.315)}
    factors = {'g_ffn': 48.784,
     'L0_xattn_Wq': 5.08,
     'L0_xattn_Wk': 4.744,
     'L1_xattn_igate_b': 64.0,
     'L1_ffn_Wr': 8.0,
     'L1_ffn_Wu': 8.0,
     'L1_ffn_Wg': 8.0,
     'L1_ffn_Wd': 8.0,
     'L1_ffn_Wu_s': 7.155,
     'L1_ffn_Wg_s': 6.994,
     'L1_ffn_Wd_s': 7.152,
     'L3_xattn_b_igate': 64.0,
     'L3_ffn_ln_gamma': 26.424,
     'L3_ffn_ln_beta': 23.204,
     'L2_xattn_wq': 4.58,
     'L2_xattn_wk': 3.727,
     'L2_ffn_w1': 6.214,
     'L2_ffn_w2': 3.202}
    for name, (base, spread) in spreads.items():
        noise = np.random.default_rng([zlib.crc32(name.encode()), seed]).standard_normal(out[name].shape)
        drawn = base * np.exp(spread * noise) if base else spread * noise
        out[name] = jnp.asarray(drawn.astype(out[name].dtype))
    for name, factor in factors.items():
        out[name] = (out[name] * factor).astype(out[name].dtype)
    return out
```

```python
from contextlib import ExitStack

import numpy as np

import concourse.bass as bass
from concourse import mybir

ALU = mybir.AluOpType
ACT = mybir.ActivationFunctionType
AX = mybir.AxisListType
F32 = mybir.dt.float32
BF16 = mybir.dt.bfloat16
I32 = mybir.dt.int32
U32 = mybir.dt.uint32

P = 128
B = 8
S = 256
D = 256
TB = S // P
KC = D // P
LN_EPS = 1e-5
MASK_FACTOR = 1e9


class Space:

    def __init__(self, nc, ctx, name, sems=None):
        self.nc, self.ctx, self.name = nc, ctx, name
        self.sems = [] if sems is None else sems

    def sb(self, name, shape, dt=F32):
        return self.ctx.enter_context(self.nc.sbuf_tensor(f"{self.name}_{name}", shape, dt))

    def psum(self, name, shape, dt=F32):
        return self.ctx.enter_context(self.nc.psum_tensor(f"{self.name}_{name}", shape, dt))

    def sem(self, name):
        sem = self.ctx.enter_context(self.nc.semaphore(f"{self.name}_{name}"))
        self.sems.append(sem)
        return sem

    def block(self):
        self.ctx.callback(self.clear)
        return self.ctx.enter_context(self.nc.Block())

    def clear(self):
        with self.nc.Block() as block:
            @block.sync
            def _(sp):
                for sem in self.sems:
                    sp.sem_clear(sem)


class Tally:

    def __init__(self, sem, per, first=0):
        self.sem, self.per, self.first = sem, per, first

    def wait(self, engine, b, k):
        engine.wait_ge(self.sem, b * self.per + (self.first + k))

    def wait_apart(self, engine, b, k, passed):
        self.wait(engine, b, k)
        engine.sem_inc(passed, 1)


def rows(dram, b):
    return dram[b].rearrange("(t p) d -> p t d", p=P)


def batches(engine, turn):
    turn(0, 0, first=True)
    with engine.Fori(0, B // 2 - 1) as pair:
        turn(2 * pair + 1, 1)
        turn(2 * pair + 2, 0)
    turn(B - 1, 1, last=True)


def load_times(b, par, per):
    return (b - par) * (8 * per) + 16 * per


H = 16
DH = D // H
QG = 4
HG = H // QG


def attention_phase(nc, name, x_src, x_dst, ctx_dram, consts, w, gate_col, score_scale, mask_dram=None):
    masked = mask_dram is not None
    biased = "bq" in w
    q_scale = -score_scale if masked else score_scale
    exp_scale = -1.0 if masked else 1.0
    nload = 3 if masked else 2
    with ExitStack() as ctx:
        m = Space(nc, ctx, name)
        wq = m.sb("wq", [P, KC, HG * P])
        wk = m.sb("wk", [P, KC, HG * P])
        wv = m.sb("wv", [P, KC, D])
        wo = m.sb("wo", [P, KC, D])
        bq = m.sb("bq", [P, HG])
        bqs = m.sb("bqs", [P, HG])
        bk = m.sb("bk", [P, HG])
        bv = m.sb("bv", [1, D])
        ones_row = m.sb("ones_row", [1, P])
        bo = m.sb("bo", [P, D])
        xin = m.sb("xin", [P, 2, TB, D])
        cin = m.sb("cin", [P, 2, TB, D])
        xres = m.sb("xres", [P, 2, TB, D])
        mask = m.sb("mask", [P, 2, TB, S]) if masked else None
        stats = m.sb("stats", [P, TB, 6])
        mv = m.sb("mv", [P, TB, 2])
        veps = m.sb("veps", [P, TB])
        rstd = m.sb("rstd", [P, TB])
        xn = m.sb("xn", [P, TB, D])
        xnT = m.sb("xnT", [P, KC, S])
        cT = m.sb("cT", [P, KC, S])
        qT = m.sb("qT", [P, 2, HG, S])
        kT = m.sb("kT", [P, 2, HG, S])
        v = m.sb("v", [P, 2, TB, D])
        sm = m.sb("sm", [P, 2, TB, S]) if masked else None
        shift = m.sb("shift", [P, 2, TB, 1])
        probs = m.sb("probs", [P, 2, TB, S])
        probsT = m.sb("probsT", [P, 2, TB, S])
        rsum = m.sb("rsum", [P, 2, TB, H])
        rinv = m.sb("rinv", [P, TB, H])
        o_sb = m.sb("o_sb", [P, TB, D])
        oT = m.sb("oT", [P, KC, S])
        yb = m.sb("yb", [P, TB, D])

        ps_s = m.psum("ps_s", [P, 2, TB, S])
        ps_t = m.psum("ps_t", [P, 2, TB, S])
        ps_o = m.psum("ps_o", [P, TB, D])
        ps_w = m.psum("ps_w", [P, 2, TB, S])
        ps_y = m.psum("ps_y", [P, TB, D])

        weights_in = m.sem("weights_in")
        bias_scaled = m.sem("bias_scaled")
        ones_set = m.sem("ones_set")
        loaded = [m.sem("loaded0"), m.sem("loaded1")]
        xres_in = [m.sem("xres_in0"), m.sem("xres_in1")]
        mask_scaled = Tally(m.sem("mask_scaled"), 1)
        stored = Tally(m.sem("stored"), 16, 16)
        stats_done = Tally(m.sem("stats_done"), 1)
        mv_ready = Tally(m.sem("mv_ready"), 1)
        eps_added = Tally(m.sem("eps_added"), 1)
        rstd_ready = Tally(m.sem("rstd_ready"), 1)
        xn_ready = Tally(m.sem("xn_ready"), 1)
        work_filled = Tally(m.sem("work_filled"), 7)
        work_drained = Tally(m.sem("work_drained"), 7, 2)
        scores_ready = Tally(m.sem("scores_ready"), H)
        shift_ready = Tally(m.sem("shift_ready"), H, 2)
        probs_ready = Tally(m.sem("probs_ready"), H, 2)
        probsT_ready = Tally(m.sem("probsT_ready"), H, 2)
        probsT_copied = Tally(m.sem("probsT_copied"), H, 2)
        heads_done = Tally(m.sem("heads_done"), 1, 1)
        rinv_ready = Tally(m.sem("rinv_ready"), 1)
        o_ready = Tally(m.sem("o_ready"), 1, 1)
        oT_ready = Tally(m.sem("oT_ready"), 1)
        oT_copied = Tally(m.sem("oT_copied"), 1)
        y_ready = Tally(m.sem("y_ready"), 1)
        y_drained = Tally(m.sem("y_drained"), 2, 2)
        passed = m.sem("passed")
        ident = consts["ident"]
        minus_half = consts["minus_half"]
        gate = consts["gates"][:, gate_col:gate_col + 1]
        nweights = 4 + (4 if biased else 0)

        block = m.block()

        @block.sync
        def _(sp):
            sp.dma_start(wq[:], w["wq"]).then_inc(weights_in, 16)
            sp.dma_start(wk[:], w["wk"]).then_inc(weights_in, 16)
            sp.dma_start(wv[:], w["wv"]).then_inc(weights_in, 16)
            sp.dma_start(wo[:], w["wo"]).then_inc(weights_in, 16)
            if biased:
                sp.dma_start(bq[:], w["bq"]).then_inc(weights_in, 16)
                sp.dma_start(bk[:], w["bk"]).then_inc(weights_in, 16)
                sp.dma_start(bv[:], w["bv"]).then_inc(weights_in, 16)
                sp.dma_start(bo[:], w["bo"].broadcast_to([P, D])).then_inc(weights_in, 16)

            def load(b, par):
                sp.dma_start(xin[:, par], rows(x_src, b)).then_inc(loaded[par], 16)
                sp.dma_start(cin[:, par], rows(ctx_dram, b)).then_inc(loaded[par], 16)
                if masked:
                    sp.dma_start(mask[:, par], rows(mask_dram, b)).then_inc(loaded[par], 16)

            def store(b, par):
                y_drained.wait(sp, b, 2)
                sp.dma_start(rows(x_dst, b), xres[:, par]).then_inc(stored.sem, 16)

            def turn(b, par, first=False, last=False):
                if first:
                    load(0, 0)
                if not last:
                    heads_done.wait(sp, b, 0)
                    load(b + 1, 1 - par)
                if not first:
                    stored.wait(sp, b, -16)
                sp.dma_start(xres[:, par], rows(x_src, b)).then_inc(xres_in[par], 16)
                if not first:
                    store(b - 1, 1 - par)

            sp.sem_inc(stored.sem, 16)
            batches(sp, turn)
            store(B - 1, 1)
            stored.wait(sp, B - 1, 16)

        @block.tensor
        def _(pe):
            pe.sem_inc(probsT_ready.sem, 2)
            pe.sem_inc(heads_done.sem, 1)

            def transposes(dst, src):
                for k in range(KC):
                    for t in range(TB):
                        last = pe.transpose(dst[:, k, t * P:(t + 1) * P], src[:, t, k * P:(k + 1) * P], ident[:])
                return last

            def fill(b, par, j):
                bank = ps_w[:, (par + j) % 2]
                work_drained.wait(pe, b, j - 1)
                if j == 0:
                    xn_ready.wait(pe, b, 1)
                    last = transposes(bank, xn)
                elif j == 1:
                    pe.wait_ge(loaded[par], load_times(b, par, nload))
                    last = transposes(bank, cin[:, par])
                else:
                    if j == 2:
                        work_drained.wait(pe, b, 2)
                    if j < 6:
                        weight, act = (wq, xnT) if j < 4 else (wk, cT)
                        for g in range(2):
                            gg = 2 * (j % 2) + g
                            for k in range(KC):
                                last = pe.matmul(bank[:, g, :], weight[:, k, gg * P:(gg + 1) * P], act[:, k, :],
                                                 start=(k == 0), stop=(k == KC - 1))
                    else:
                        for t in range(TB):
                            if biased:
                                pe.matmul(bank[:, t, :], ones_row[:], bv[:], start=True, stop=False)
                            for k in range(KC):
                                last = pe.matmul(bank[:, t, :], cT[:, k, t * P:(t + 1) * P], wv[:, k, :],
                                                 start=(k == 0 and not biased), stop=(k == KC - 1))
                last.then_inc(work_filled.sem, 1)

            def scores(b, par, h):
                if h == 0:
                    work_drained.wait(pe, b, 7)
                (shift_ready if masked else probs_ready).wait(pe, b, h - 1)
                g, r = h // QG, 32 * (h % QG)
                for t in range(TB):
                    last = pe.matmul(ps_s[:, h % 2, t, :], qT[r:r + DH, par, g, t * P:(t + 1) * P],
                                     kT[r:r + DH, par, g, :], start=True, stop=True)
                last.then_inc(scores_ready.sem, 1)

            def turn_probs(b, par, h):
                probs_ready.wait(pe, b, h + 1)
                probsT_copied.wait(pe, b, h - 1)
                transposes(ps_t[:, h % 2], probs[:, h % 2]).then_inc(probsT_ready.sem, 1)

            def weigh(b, par, h):
                probsT_copied.wait(pe, b, h + 1)
                if h == 0:
                    o_ready.wait(pe, b, 0)
                for t in range(TB):
                    for lb in range(TB):
                        last = pe.matmul(ps_o[:, t, h * DH:(h + 1) * DH], probsT[:, h % 2, lb, t * P:(t + 1) * P],
                                         v[:, par, lb, h * DH:(h + 1) * DH], start=(lb == 0), stop=(lb == TB - 1))
                if h == H - 1:
                    last.then_inc(heads_done.sem, 1)

            def turn_out(b):
                o_ready.wait(pe, b, 1)
                y_drained.wait(pe, b, 0)
                transposes(ps_y, o_sb).then_inc(oT_ready.sem, 1)

            def project_out(b):
                oT_copied.wait(pe, b, 1)
                for t in range(TB):
                    for k in range(KC):
                        last = pe.matmul(ps_y[:, t, :], oT[:, k, t * P:(t + 1) * P], wo[:, k, :],
                                         start=(k == 0), stop=(k == KC - 1))
                last.then_inc(y_ready.sem, 1)

            def turn(b, par, first=False, last=False):
                for h in range(H):
                    if h < H - 1:
                        scores(b, par, h + 1)
                    elif not last:
                        scores(b + 1, 1 - par, 0)
                    turn_probs(b, par, h)
                    if h:
                        weigh(b, par, h - 1)
                    if h == 2 and not first:
                        turn_out(b - 1)
                    if h == 4 and not first:
                        project_out(b - 1)
                    if h >= 7 and h < 14 and not last:
                        fill(b + 1, 1 - par, h - 7)
                weigh(b, par, H - 1)

            pe.wait_ge(weights_in, 16 * nweights)
            if biased:
                pe.wait_ge(ones_set, 1)
            for j in range(7):
                fill(0, 0, j)
            scores(0, 0, 0)
            batches(pe, turn)
            turn_out(B - 1)
            project_out(B - 1)

        @block.scalar
        def _(act):
            act.sem_inc(work_drained.sem, 2)
            act.sem_inc(probs_ready.sem, 2)

            def drain(b, par, j):
                bank = ps_w[:, (par + j) % 2]
                work_filled.wait(act, b, j + 1)
                if j < 2:
                    act.activation((xnT if j == 0 else cT)[:], bank, ACT.Copy).then_inc(work_drained.sem, 1)
                elif j < 6:
                    dst, scale, bias = (qT, q_scale, bqs) if j < 4 else (kT, 1.0, bk)
                    g = 2 * (j % 2)
                    if not biased:
                        act.activation(dst[:, par, g:g + 2, :], bank, ACT.Copy,
                                       scale=scale).then_inc(work_drained.sem, 1)
                    else:
                        act.activation(dst[:, par, g, :], bank[:, 0, :], ACT.Identity,
                                       bias=bias[:, g:g + 1], scale=scale)
                        act.activation(dst[:, par, g + 1, :], bank[:, 1, :], ACT.Identity,
                                       bias=bias[:, g + 1:g + 2], scale=scale).then_inc(work_drained.sem, 1)
                else:
                    act.activation(v[:, par], bank, ACT.Copy).then_inc(work_drained.sem, 1)

            def copy_oT(b):
                oT_ready.wait(act, b, 1)
                act.activation(oT[:], ps_y[:], ACT.Copy).then_inc(oT_copied.sem, 1)

            def exponent(b, par, h):
                shift_ready.wait(act, b, h + 1)
                probsT_ready.wait(act, b, h - 1)
                for t in range(TB):
                    src = sm[:, h % 2, t, :] if masked else ps_s[:, h % 2, t, :]
                    last = act.activation(probs[:, h % 2, t, :], src, ACT.Exp, bias=shift[:, h % 2, t, :],
                                          scale=exp_scale, accum_out=rsum[:, par, t, h:h + 1])
                last.then_inc(probs_ready.sem, 1)

            def turn(b, par, first=False, last=False):
                for h in range(H):
                    exponent(b, par, h)
                    if h == 3 and not first:
                        copy_oT(b - 1)
                    if h >= 7 and h < 14 and not last:
                        drain(b + 1, 1 - par, h - 7)

            if biased:
                act.wait_ge(weights_in, 16 * nweights)
                act.activation(bqs[:], bq[:], ACT.Copy, scale=q_scale).then_inc(bias_scaled, 1)
                act.wait_ge(bias_scaled, 1)
            for j in range(7):
                drain(0, 0, j)
            batches(act, turn)
            copy_oT(B - 1)

        @block.gpsimd
        def _(pool):
            with pool.Fori(0, B) as b:
                mv_ready.wait_apart(pool, b, 1, passed)
                pool.tensor_scalar(veps[:], mv[:, :, 1], LN_EPS, None, ALU.add).then_inc(eps_added.sem, 1)
                eps_added.wait(pool, b, 1)
                pool.tensor_tensor(rstd[:], veps[:], minus_half[:, 0:TB], ALU.pow).then_inc(rstd_ready.sem, 1)

        @block.vector
        def _(dve):
            dve.sem_inc(shift_ready.sem, 2)
            dve.sem_inc(probsT_copied.sem, 2)
            dve.sem_inc(o_ready.sem, 1)
            dve.sem_inc(y_drained.sem, 2)

            def statistics(b, par):
                dve.wait_ge(loaded[par], load_times(b, par, nload))
                for t in range(TB):
                    last = dve.bn_stats(stats[:, t, :], xin[:, par, t, :])
                last.then_inc(stats_done.sem, 1)
                stats_done.wait_apart(dve, b, 1, passed)
                for t in range(TB):
                    last = dve.bn_aggr(mv[:, t, :], stats[:, t, :])
                last.then_inc(mv_ready.sem, 1)
                if masked:
                    dve.tensor_scalar(mask[:, par], mask[:, par], MASK_FACTOR, None,
                                      ALU.mult).then_inc(mask_scaled.sem, 1)

            def normalise(b, par):
                rstd_ready.wait(dve, b, 1)
                for t in range(TB):
                    last = dve.tensor_scalar(xn[:, t, :], xin[:, par, t, :], mv[:, t, 0:1], rstd[:, t:t + 1],
                                             ALU.subtract, ALU.mult)
                last.then_inc(xn_ready.sem, 1)

            def shifts(b, par, h):
                scores_ready.wait(dve, b, h + 1)
                if masked and h == 0:
                    mask_scaled.wait(dve, b, 1)
                probs_ready.wait_apart(dve, b, h - 1, passed)
                if masked:
                    for t in range(TB):
                        last = dve.tensor_tensor_reduce(sm[:, h % 2, t, :], ps_s[:, h % 2, t, :], mask[:, par, t, :],
                                                        1.0, 3.0e38, ALU.add, ALU.min, shift[:, h % 2, t, :])
                else:
                    last = dve.tensor_reduce(shift[:, h % 2, :, :], ps_s[:, h % 2], AX.X, ALU.max, negate=True)
                last.then_inc(shift_ready.sem, 1)

            def copy_probsT(b, par, h):
                probsT_ready.wait(dve, b, h + 1)
                dve.tensor_copy(probsT[:, h % 2], ps_t[:, h % 2]).then_inc(probsT_copied.sem, 1)

            def divide(b, par):
                probs_ready.wait(dve, b, H)
                dve.reciprocal(rinv[:], rsum[:, par]).then_inc(rinv_ready.sem, 1)
                rinv_ready.wait(dve, b, 1)
                heads_done.wait(dve, b, 1)
                dve.tensor_tensor(o_sb[:].rearrange("p t (h d) -> p (t h) d", d=DH),
                                  ps_o[:].rearrange("p t (h d) -> p (t h) d", d=DH),
                                  rinv[:].rearrange("p t h -> p (t h)").unsqueeze(2).broadcast_to([P, TB * H, DH]),
                                  ALU.mult).then_inc(o_ready.sem, 1)

            def add_residual(b, par):
                y_ready.wait(dve, b, 1)
                dve.wait_ge(xres_in[par], load_times(b, par, 1))
                if biased:
                    for t in range(TB):
                        last = dve.tensor_tensor(yb[:, t, :], ps_y[:, t, :], bo[:], ALU.add)
                    last.then_inc(y_drained.sem, 1)
                    y_drained.wait(dve, b, 1)
                    src = yb
                else:
                    dve.sem_inc(y_drained.sem, 1)
                    src = ps_y
                dve.scalar_tensor_tensor(xres[:, par], src[:], gate, xres[:, par], ALU.mult,
                                         ALU.add).then_inc(y_drained.sem, 1)

            def turn(b, par, first=False, last=False):
                for h in range(H):
                    if h < H - 1:
                        shifts(b, par, h + 1)
                    elif not last:
                        shifts(b + 1, 1 - par, 0)
                    copy_probsT(b, par, h)
                    if h == 1 and not first:
                        divide(b - 1, 1 - par)
                    if h == 5 and not first:
                        add_residual(b - 1, 1 - par)
                    if h == 5 and not last:
                        statistics(b + 1, 1 - par)
                    if h == 6 and not last:
                        normalise(b + 1, 1 - par)

            if biased:
                dve.memset(ones_row[:], 1.0).then_inc(ones_set, 1)
                dve.wait_ge(weights_in, 16 * nweights)
            statistics(0, 0)
            normalise(0, 0)
            shifts(0, 0, 0)
            batches(dve, turn)
            divide(B - 1, 1)
            add_residual(B - 1, 1)


NT = B * TB
MAGIC = 1.5 * 2.0 ** 23


def tile_rows(dram, n):
    return dram.rearrange("b (t p) d -> (b t) p d", p=P)[n]


def tiles(engine, turn, count=NT):
    turn(0, 0, first=True)
    with engine.Fori(0, count // 2 - 1) as pair:
        turn(2 * pair + 1, 1)
        turn(2 * pair + 2, 0)
    turn(count - 1, 1, last=True)


def tile_times(n, par, per):
    return (n - par) * (8 * per) + 16 * per


class Norm:

    def __init__(self, m, consts):
        self.stats = m.sb("ln_stats", [P, 6])
        self.mv = m.sb("ln_mv", [P, 2])
        self.veps = m.sb("ln_veps", [P, 1])
        self.rstd = m.sb("ln_rstd", [P, 1])
        self.minus_half = consts["minus_half"]
        self.stats_done = Tally(m.sem("ln_stats_done"), 1)
        self.mv_ready = Tally(m.sem("ln_mv_ready"), 1)
        self.eps_added = Tally(m.sem("ln_eps_added"), 1)
        self.rstd_ready = Tally(m.sem("ln_rstd_ready"), 1)
        self.passed = m.sem("ln_passed")

    def statistics(self, dve, x, n):
        dve.bn_stats(self.stats[:], x).then_inc(self.stats_done.sem, 1)
        self.stats_done.wait_apart(dve, n, 1, self.passed)
        dve.bn_aggr(self.mv[:], self.stats[:]).then_inc(self.mv_ready.sem, 1)

    def on_pool(self, pool, n):
        self.mv_ready.wait_apart(pool, n, 1, self.passed)
        pool.tensor_scalar(self.veps[:], self.mv[:, 1:2], LN_EPS, None, ALU.add).then_inc(self.eps_added.sem, 1)
        self.eps_added.wait(pool, n, 1)
        pool.tensor_tensor(self.rstd[:], self.veps[:], self.minus_half[:, 0:1],
                           ALU.pow).then_inc(self.rstd_ready.sem, 1)

    def apply(self, dve, out, x, n):
        self.rstd_ready.wait(dve, n, 1)
        return dve.tensor_scalar(out, x, self.mv[:, 0:1], self.rstd[:], ALU.subtract, ALU.mult)


F0 = 1024
FC0 = F0 // P
HALF = 512


def quantised_ffn_phase(nc, name, x_src, x_dst, consts, w, gate_col):
    with ExitStack() as ctx:
        m = Space(nc, ctx, name)
        wraw = m.sb("wraw", [P, 3, KC * F0])
        wround = m.sb("wround", [P, KC * F0])
        wt = m.sb("wt", [P, 3, KC * F0], BF16)
        wsum = m.sb("wsum", [P, 3])
        wmean = m.sb("wmean", [P, 3])
        winv = m.sb("winv", [P, 3])
        wfac = m.sb("wfac", [P, 3])
        ones = m.sb("ones", [P, P])
        identb = m.sb("identb", [P, P], BF16)
        xin = m.sb("xin", [P, 2, D])
        xres = m.sb("xres", [P, 2, D])
        xn = m.sb("xn", [P, D])
        amax = m.sb("amax", [P, 2, 1])
        clipped = m.sb("clipped", [P, 2, 1])
        inv = m.sb("inv", [P, 2, 1])
        sc = m.sb("sc", [P, 2, 1])
        fac = m.sb("fac", [P, 2, 2])
        qa = m.sb("qa", [P, D])
        qb = m.sb("qb", [P, D])
        xq = m.sb("xq", [P, D], BF16)
        xqT = m.sb("xqT", [P, KC, P], BF16)
        silu = m.sb("silu", [P, 2, HALF])
        h = m.sb("h", [P, F0])
        ha = m.sb("ha", [P, F0])
        hq = m.sb("hq", [P, F0], BF16)
        hqT = m.sb("hqT", [P, FC0, P], BF16)
        hmax = m.sb("hmax", [P, 1])
        hclip = m.sb("hclip", [P, 1])
        hinv = m.sb("hinv", [P, 1])
        hsc = m.sb("hsc", [P, 1])
        hfac = m.sb("hfac", [P, 2])
        norm = Norm(m, consts)

        ps_g = m.psum("ps_g", [P, 2, HALF])
        ps_u = m.psum("ps_u", [P, 2, HALF])
        ps_x = m.psum("ps_x", [P, 2 * HALF], BF16)
        ps_h = m.psum("ps_h", [P, FC0, P], BF16)
        ps_y = m.psum("ps_y", [P, HALF])
        ps_m = m.psum("ps_m", [P, HALF])

        weights_in = m.sem("weights_in")
        sums_ready = m.sem("sums_ready")
        mean_ready = m.sem("mean_ready")
        wstep = m.sem("wstep")
        weights_ready = m.sem("weights_ready")
        loaded = [m.sem("loaded0"), m.sem("loaded1")]
        xres_in = [m.sem("xres_in0"), m.sem("xres_in1")]
        stored = Tally(m.sem("stored"), 16, 16)
        xstep = Tally(m.sem("xstep"), 7)
        xq_ready = Tally(m.sem("xq_ready"), 1)
        xqT_ready = Tally(m.sem("xqT_ready"), 1)
        xqT_copied = Tally(m.sem("xqT_copied"), 1)
        fac_ready = Tally(m.sem("fac_ready"), 1)
        gate_ready = Tally(m.sem("gate_ready"), 2)
        up_ready = Tally(m.sem("up_ready"), 2)
        silu_ready = Tally(m.sem("silu_ready"), 2, 2)
        h_ready = Tally(m.sem("h_ready"), 2, 2)
        hstep = Tally(m.sem("hstep"), 6)
        hq_ready = Tally(m.sem("hq_ready"), 1, 1)
        hqT_ready = Tally(m.sem("hqT_ready"), 1, 1)
        hqT_copied = Tally(m.sem("hqT_copied"), 1)
        y_ready = Tally(m.sem("y_ready"), 1)
        sum_ready = Tally(m.sem("sum_ready"), 1, 1)
        identb_ready = m.sem("identb_ready")
        gate = consts["gates"][:, gate_col:gate_col + 1]
        block = m.block()

        @block.sync
        def _(sp):
            for i, k in enumerate(("gate", "up", "down")):
                sp.dma_start(wraw[:, i], w[k].rearrange("p k n -> p (k n)")).then_inc(weights_in, 16)

            def turn(n, par, first=False, last=False):
                if first:
                    sp.dma_start(xin[:, 0], tile_rows(x_src, 0)).then_inc(loaded[0], 16)
                if not last:
                    if not first:
                        xq_ready.wait(sp, n - 1, 1)
                    sp.dma_start(xin[:, 1 - par], tile_rows(x_src, n + 1)).then_inc(loaded[1 - par], 16)
                if not first:
                    stored.wait(sp, n, -16)
                sp.dma_start(xres[:, par], tile_rows(x_src, n)).then_inc(xres_in[par], 16)
                if not first:
                    store(n - 1, 1 - par)

            def store(n, par):
                sum_ready.wait(sp, n, 1)
                sp.dma_start(tile_rows(x_dst, n), xres[:, par]).then_inc(stored.sem, 16)

            sp.sem_inc(stored.sem, 16)
            tiles(sp, turn)
            store(NT - 1, 1)
            stored.wait(sp, NT - 1, 16)

        @block.gpsimd
        def _(pool):
            with pool.Fori(0, NT) as n:
                norm.on_pool(pool, n)

        @block.tensor
        def _(pe):
            pe.sem_inc(hqT_ready.sem, 1)
            pe.wait_ge(sums_ready, 1)
            pe.matmul(ps_m[:, 0:3], ones[:], wsum[:], start=True, stop=True).then_inc(mean_ready, 1)
            pe.wait_ge(weights_ready, 1)
            pe.wait_ge(identb_ready, 1)

            def turn_x(n):
                xq_ready.wait(pe, n, 1)
                for k in range(KC):
                    last = pe.transpose(ps_x[:, k * P:(k + 1) * P], xq[:, k * P:(k + 1) * P], identb[:])
                last.then_inc(xqT_ready.sem, 1)

            def gate_up(n):
                xqT_copied.wait(pe, n, 1)
                h_ready.wait(pe, n, 0)
                for c in range(2):
                    for i, bank, ready in ((0, ps_g, gate_ready), (1, ps_u, up_ready)):
                        for k in range(KC):
                            last = pe.matmul(bank[:, c, :], xqT[:, k, :],
                                             wt[:, i, k * F0 + c * HALF:k * F0 + (c + 1) * HALF],
                                             start=(k == 0), stop=(k == KC - 1))
                        last.then_inc(ready.sem, 1)

            def down(n):
                hq_ready.wait(pe, n, 1)
                for f in range(FC0):
                    last = pe.transpose(ps_h[:, f, :], hq[:, f * P:(f + 1) * P], identb[:])
                last.then_inc(hqT_ready.sem, 1)
                hqT_copied.wait(pe, n, 1)
                sum_ready.wait(pe, n, 0)
                for f in range(FC0):
                    last = pe.matmul(ps_y[:, 0:D], hqT[:, f, :], wt[:, 2, f * D:(f + 1) * D],
                                     start=(f == 0), stop=(f == FC0 - 1))
                last.then_inc(y_ready.sem, 1)

            def turn(n, par, first=False, last=False):
                if first:
                    turn_x(0)
                gate_up(n)
                if not last:
                    turn_x(n + 1)
                if not first:
                    down(n - 1)

            tiles(pe, turn)
            down(NT - 1)

        @block.scalar
        def _(act):
            act.sem_inc(silu_ready.sem, 2)
            act.activation(identb[:], consts["ident"][:], ACT.Copy).then_inc(identb_ready, 1)

            def copy_x(n):
                xqT_ready.wait(act, n, 1)
                act.activation(xqT[:].rearrange("p k n -> p (k n)"), ps_x[:, 0:D], ACT.Copy).then_inc(xqT_copied.sem, 1)

            def silus(n, par):
                fac_ready.wait(act, n, 1)
                for c in range(2):
                    gate_ready.wait(act, n, c + 1)
                    h_ready.wait(act, n, c + 1 - 2)
                    act.activation(silu[:, c], ps_g[:, c], ACT.Silu, scale=fac[:, par, 0:1]).then_inc(silu_ready.sem, 1)

            def copy_h(n):
                hqT_ready.wait(act, n, 1)
                act.activation(hqT[:], ps_h[:], ACT.Copy).then_inc(hqT_copied.sem, 1)

            def turn(n, par, first=False, last=False):
                if first:
                    copy_x(0)
                silus(n, par)
                if not last:
                    copy_x(n + 1)
                if not first:
                    copy_h(n - 1)

            tiles(act, turn)
            copy_h(NT - 1)

        @block.vector
        def _(dve):
            dve.sem_inc(h_ready.sem, 2)
            dve.sem_inc(hq_ready.sem, 1)
            dve.sem_inc(sum_ready.sem, 1)
            done = [0]

            def step(ins):
                done[0] += 1
                ins.then_inc(wstep, 1)
                dve.wait_ge(wstep, done[0])

            step(dve.memset(ones[:], 1.0))
            dve.wait_ge(weights_in, 48)
            for i in range(3):
                last = dve.tensor_reduce(wsum[:, i:i + 1], wraw[:, i], AX.X, ALU.add, apply_absolute_value=True)
            last.then_inc(sums_ready, 1)
            dve.wait_ge(mean_ready, 1)
            step(dve.tensor_scalar(wmean[:], ps_m[:, 0:3], 1.0 / (D * F0), 1e-5, ALU.mult, ALU.max))
            step(dve.reciprocal(winv[:], wmean[:]))
            step(dve.tensor_scalar(wfac[:], wmean[:], 1.0 / 127.0, None, ALU.mult))
            step(dve.tensor_scalar(wfac[:, 2:3], wfac[:, 2:3], gate, None, ALU.mult))
            for i in range(3):
                step(dve.tensor_scalar(wround[:], wraw[:, i], winv[:, i:i + 1], 1.0, ALU.mult, ALU.min))
                step(dve.tensor_scalar(wround[:], wround[:], -1.0, MAGIC, ALU.max, ALU.add))
                step(dve.tensor_scalar(wt[:, i], wround[:], MAGIC, None, ALU.subtract))
            dve.sem_inc(weights_ready, 1)

            def prepare(n, par):
                dve.wait_ge(loaded[par], tile_times(n, par, 1))
                norm.statistics(dve, xin[:, par], n)
                norm.apply(dve, xn[:], xin[:, par], n).then_inc(xstep.sem, 1)
                xstep.wait(dve, n, 1)
                dve.tensor_reduce(amax[:, par], xn[:], AX.X, ALU.max, apply_absolute_value=True).then_inc(xstep.sem, 1)
                xstep.wait(dve, n, 2)
                dve.tensor_scalar(clipped[:, par], amax[:, par], 1e-5, None, ALU.max).then_inc(xstep.sem, 1)
                xstep.wait(dve, n, 3)
                dve.reciprocal(inv[:, par], clipped[:, par]).then_inc(xstep.sem, 1)
                dve.tensor_scalar(fac[:, par], wfac[:, 0:2], clipped[:, par], None, ALU.mult).then_inc(fac_ready.sem, 1)
                xstep.wait(dve, n, 4)
                dve.tensor_scalar(sc[:, par], inv[:, par], 127.0, None, ALU.mult).then_inc(xstep.sem, 1)
                xstep.wait(dve, n, 5)
                dve.tensor_scalar(qa[:], xn[:], sc[:, par], 127.0, ALU.mult, ALU.min).then_inc(xstep.sem, 1)
                xstep.wait(dve, n, 6)
                dve.tensor_scalar(qb[:], qa[:], -128.0, MAGIC, ALU.max, ALU.add).then_inc(xstep.sem, 1)
                xstep.wait(dve, n, 7)
                dve.tensor_scalar(xq[:], qb[:], MAGIC, None, ALU.subtract).then_inc(xq_ready.sem, 1)

            def hidden(n, par):
                for c in range(2):
                    up_ready.wait(dve, n, c + 1)
                    silu_ready.wait(dve, n, c + 1)
                    dve.scalar_tensor_tensor(h[:, c * HALF:(c + 1) * HALF], ps_u[:, c], fac[:, par, 1:2], silu[:, c],
                                             ALU.mult, ALU.mult).then_inc(h_ready.sem, 1)
                h_ready.wait(dve, n, 2)
                dve.tensor_reduce(hmax[:], h[:], AX.X, ALU.max, apply_absolute_value=True).then_inc(hstep.sem, 1)
                hstep.wait(dve, n, 1)
                dve.tensor_scalar(hclip[:], hmax[:], 1e-5, None, ALU.max).then_inc(hstep.sem, 1)
                hstep.wait(dve, n, 2)
                dve.reciprocal(hinv[:], hclip[:]).then_inc(hstep.sem, 1)
                dve.tensor_scalar(hfac[:, par:par + 1], wfac[:, 2:3], hclip[:], None, ALU.mult)
                hstep.wait(dve, n, 3)
                dve.tensor_scalar(hsc[:], hinv[:], 127.0, None, ALU.mult).then_inc(hstep.sem, 1)
                hstep.wait(dve, n, 4)
                dve.tensor_scalar(ha[:], h[:], hsc[:], 127.0, ALU.mult, ALU.min).then_inc(hstep.sem, 1)
                hstep.wait(dve, n, 5)
                dve.tensor_scalar(ha[:], ha[:], -128.0, MAGIC, ALU.max, ALU.add).then_inc(hstep.sem, 1)
                hstep.wait(dve, n, 6)
                hqT_ready.wait(dve, n, 0)
                dve.tensor_scalar(hq[:], ha[:], MAGIC, None, ALU.subtract).then_inc(hq_ready.sem, 1)

            def add_residual(n, par):
                y_ready.wait(dve, n, 1)
                dve.wait_ge(xres_in[par], tile_times(n, par, 1))
                dve.scalar_tensor_tensor(xres[:, par], ps_y[:, 0:D], hfac[:, par:par + 1], xres[:, par], ALU.mult,
                                         ALU.add).then_inc(sum_ready.sem, 1)

            def turn(n, par, first=False, last=False):
                if first:
                    prepare(0, 0)
                if not last:
                    xqT_ready.wait(dve, n, 1)
                    prepare(n + 1, 1 - par)
                hidden(n, par)
                if not first:
                    add_residual(n - 1, 1 - par)

            tiles(dve, turn)
            add_residual(NT - 1, 1)


FG_ROW = 32
GN_EPS = 1e-5
NORMALISER_EPS = 1e-6
LOWEST = -3.0e38


def mlstm_phase(nc, name, x_src, x_dst, ctx_dram, consts, w, gate_col, nh, plus_one):
    dh = D // nh
    kh = P // dh
    W = S + P
    G = TB * nh
    slots = 8 // nh
    qk_scale = 1.0 / float(np.sqrt(dh))
    with ExitStack() as ctx:
        m = Space(nc, ctx, name)
        wg = m.sb("wg", [P, 6, 64])
        ib = m.sb("ib", [nh, 1])
        fb = m.sb("fb", [nh, 1])
        ow = m.sb("ow", [P, D])
        owg = m.sb("owg", [P, D])
        sel = m.sb("sel", [nh, nh * P])
        identb = m.sb("identb", [P, P], BF16)
        lower = m.sb("lower", [P, P])
        lowerb = m.sb("lowerb", [P, P], BF16)
        ones = m.sb("ones", [nh, S])
        xin = m.sb("xin", [P, 2, TB, D])
        cin = m.sb("cin", [P, 2, TB, D])
        xres = m.sb("xres", [P, 2, TB, D])
        stats = m.sb("stats", [P, TB, 6])
        mv = m.sb("mv", [P, TB, 2])
        veps = m.sb("veps", [P, TB])
        rstd = m.sb("rstd", [P, TB])
        xn = m.sb("xn", [P, TB, D])
        xnT = m.sb("xnT", [P, 2, KC, S])
        cT = m.sb("cT", [P, 2, KC, S])
        va = m.sb("va", [P, 2, TB, nh, dh + 1])
        igr = m.sb("igr", [nh, S])
        fgr = m.sb("fgr", [nh, S])
        z = m.sb("z", [nh, S])
        zabs = m.sb("zabs", [nh, S])
        zmin = m.sb("zmin", [nh, S])
        ex = m.sb("ex", [nh, S])
        lg = m.sb("lg", [nh, S])
        logf = m.sb("logf", [nh, S])
        cs = m.sb("cs", [nh, S])
        a = m.sb("a", [nh, S])
        mx = m.sb("mx", [nh, S])
        mlog = m.sb("mlog", [nh, S])
        negm = m.sb("negm", [nh, 2, S])
        e = m.sb("e", [nh, S])
        aT = m.sb("aT", [P, 2, 2, TB, nh])
        decay = m.sb("decay", [P, 2, W])
        c = m.sb("c", [P, 2, W])
        den = m.sb("den", [P, TB, nh])
        rden = m.sb("rden", [P, TB, nh])
        hn = m.sb("hn", [P, TB, nh, dh])
        sq = m.sb("sq", [P, TB, nh, dh])
        msum = m.sb("msum", [P, G])
        mean = m.sb("mean", [P, G])
        vsum = m.sb("vsum", [P, G])
        gveps = m.sb("gveps", [P, G])
        grstd = m.sb("grstd", [P, G])

        ps_q = m.psum("ps_q", [P, 2, 512])
        ps_m = m.psum("ps_m", [P, 2, 512])
        ps_o = m.psum("ps_o", [P, TB, 512])
        ps_w = m.psum("ps_w", [P, 2, TB, S])

        weights_in = m.sem("weights_in")
        wstep = m.sem("wstep")
        constants_ready = m.sem("constants_ready")
        loaded = [m.sem("loaded0"), m.sem("loaded1")]
        xres_in = [m.sem("xres_in0"), m.sem("xres_in1")]
        stored = Tally(m.sem("stored"), 16, 16)
        stats_done = Tally(m.sem("stats_done"), 1)
        mv_ready = Tally(m.sem("mv_ready"), 1)
        eps_added = Tally(m.sem("eps_added"), 1)
        rstd_ready = Tally(m.sem("rstd_ready"), 1)
        xn_ready = Tally(m.sem("xn_ready"), 1)
        va_ready = Tally(m.sem("va_ready"), 1)
        work_filled = Tally(m.sem("work_filled"), 4)
        act_drained = Tally(m.sem("act_drained"), 3)
        z_ready = Tally(m.sem("z_ready"), 1)
        ex_ready = Tally(m.sem("ex_ready"), 1)
        lg_ready = Tally(m.sem("lg_ready"), 1)
        gstep = Tally(m.sem("gstep"), 6)
        mlog_ready = Tally(m.sem("mlog_ready"), 1)
        e_ready = Tally(m.sem("e_ready"), 1)
        aT_ready = Tally(m.sem("aT_ready"), 1, 1)
        scores_ready = Tally(m.sem("scores_ready"), nh)
        m_ready = Tally(m.sem("m_ready"), nh)
        decay_ready = Tally(m.sem("decay_ready"), nh, 2)
        c_ready = Tally(m.sem("c_ready"), nh, 2)
        head_done = Tally(m.sem("head_done"), nh, 2)
        estep = Tally(m.sem("estep"), 10)
        out_read = Tally(m.sem("out_read"), 1, 1)
        vsum_ready = Tally(m.sem("vsum_ready"), 1)
        geps_added = Tally(m.sem("geps_added"), 1)
        grstd_ready = Tally(m.sem("grstd_ready"), 1)
        sum_ready = Tally(m.sem("sum_ready"), 1)
        passed = m.sem("passed")
        ident = consts["ident"]
        minus_half = consts["minus_half"]
        gate = consts["gates"][:, gate_col:gate_col + 1]
        block = m.block()

        @block.sync
        def _(sp):
            sp.dma_start(wg[:], w["gates"]).then_inc(weights_in, 16)
            sp.dma_start(ib[:], w["ib"]).then_inc(weights_in, 16)
            sp.dma_start(fb[:], w["fb"]).then_inc(weights_in, 16)
            sp.dma_start(ow[:], w["ow"].broadcast_to([P, D])).then_inc(weights_in, 16)
            sp.dma_start(sel[:], w["sel"]).then_inc(weights_in, 16)
            sp.dma_start(lower[:], w["lower"]).then_inc(weights_in, 16)

            def load(b, par):
                sp.dma_start(xin[:, par], rows(x_src, b)).then_inc(loaded[par], 16)
                sp.dma_start(cin[:, par], rows(ctx_dram, b)).then_inc(loaded[par], 16)

            def store(b, par):
                sum_ready.wait(sp, b, 1)
                sp.dma_start(rows(x_dst, b), xres[:, par]).then_inc(stored.sem, 16)

            def turn(b, par, first=False, last=False):
                if first:
                    load(0, 0)
                if not last:
                    head_done.wait(sp, b, 0)
                    load(b + 1, 1 - par)
                if not first:
                    stored.wait(sp, b, -16)
                sp.dma_start(xres[:, par], rows(x_src, b)).then_inc(xres_in[par], 16)
                if not first:
                    store(b - 1, 1 - par)

            sp.sem_inc(stored.sem, 16)
            batches(sp, turn)
            store(B - 1, 1)
            stored.wait(sp, B - 1, 16)

        @block.gpsimd
        def _(pool):
            def layer(b):
                mv_ready.wait_apart(pool, b, 1, passed)
                pool.tensor_scalar(veps[:], mv[:, :, 1], LN_EPS, None, ALU.add).then_inc(eps_added.sem, 1)
                eps_added.wait(pool, b, 1)
                pool.tensor_tensor(rstd[:], veps[:], minus_half[:, 0:TB], ALU.pow).then_inc(rstd_ready.sem, 1)

            def group(b):
                vsum_ready.wait_apart(pool, b, 1, passed)
                pool.tensor_scalar(gveps[:], vsum[:], 1.0 / dh, GN_EPS, ALU.mult,
                                   ALU.add).then_inc(geps_added.sem, 1)
                geps_added.wait(pool, b, 1)
                pool.tensor_tensor(grstd[:], gveps[:], minus_half[:, 0:G], ALU.pow).then_inc(grstd_ready.sem, 1)

            layer(0)
            layer(1)
            with pool.Fori(0, B - 2) as b:
                layer(b + 2)
                group(b)
            group(B - 2)
            group(B - 1)

        @block.tensor
        def _(pe):
            pe.sem_inc(head_done.sem, 2)
            pe.wait_ge(weights_in, 96)
            pe.wait_ge(constants_ready, 1)

            def transposes(dst, src):
                for k in range(KC):
                    for t in range(TB):
                        last = pe.transpose(dst[:, k, t * P:(t + 1) * P], src[:, t, k * P:(k + 1) * P], ident[:])
                return last

            def prepare(b, par, j):
                if j == 1:
                    xn_ready.wait(pe, b, 1)
                    act_drained.wait(pe, b, 0)
                    transposes(ps_w[:, 0], xn).then_inc(work_filled.sem, 1)
                if j == 2:
                    pe.wait_ge(loaded[par], load_times(b, par, 2))
                    aT_ready.wait(pe, b, 0)
                    transposes(ps_w[:, 1], cin[:, par]).then_inc(work_filled.sem, 1)
                if j == 3:
                    act_drained.wait(pe, b, 2)
                    for k in range(6):
                        src = xnT[:, par, k, :] if k < KC else cT[:, par, k % KC, :]
                        last = pe.matmul(ps_w[0:64, 0, 0, :], wg[:, k, :], src, start=(k == 0), stop=(k == 5))
                    last.then_inc(work_filled.sem, 1)
                if j == 6:
                    e_ready.wait_apart(pe, b, 1, passed)
                    for i, src in enumerate((a, e)):
                        for t in range(TB):
                            at = (i * TB + t) * nh
                            last = pe.transpose(ps_w[:, 1, 0, at:at + nh], src[:, t * P:(t + 1) * P],
                                                ident[0:nh, 0:nh])
                    last.then_inc(work_filled.sem, 1)

            def scores(b, par, h):
                if h == 0:
                    mlog_ready.wait(pe, b, 1)
                k, r = h // kh, dh * (h % kh)
                c_ready.wait(pe, b, h - 1)
                pe.matmul(ps_q[:, h % 2, 0:S], cT[r:r + dh, par, k, 0:P], xnT[r:r + dh, par, k, :],
                          start=True, stop=True)
                pe.matmul(ps_q[:, h % 2, S:W], cT[r:r + dh, par, k, P:S], xnT[r:r + dh, par, k, P:S],
                          start=True, stop=True).then_inc(scores_ready.sem, 1)
                decay_ready.wait(pe, b, h - 1)
                row = sel[:, h * P:(h + 1) * P]
                pe.matmul(ps_m[:, h % 2, 0:S], row, negm[:, par, :], start=True, stop=False, skip_group_check=True)
                pe.matmul(ps_m[:, h % 2, S:W], row, negm[:, par, P:S], start=False, stop=False,
                          skip_group_check=True)
                for at in (0, S):
                    last = pe.matmul(ps_m[:, h % 2, at:at + P], identb[:], lowerb[:], start=False, stop=True,
                                     skip_group_check=True)
                last.then_inc(m_ready.sem, 1)

            def weigh(b, par, h):
                c_ready.wait(pe, b, h + 1)
                if h == 0:
                    out_read.wait(pe, b, 0)
                    va_ready.wait(pe, b, 1)
                cols = slice(h * (dh + 1), (h + 1) * (dh + 1))
                pe.matmul(ps_o[:, 0, cols], c[:, h % 2, 0:P], va[:, par, 0, h, :], start=True, stop=True)
                pe.matmul(ps_o[:, 1, cols], c[:, h % 2, P:S], va[:, par, 0, h, :], start=True, stop=False)
                pe.matmul(ps_o[:, 1, cols], c[:, h % 2, S:W], va[:, par, 1, h, :], start=False,
                          stop=True).then_inc(head_done.sem, 1)

            def turn(b, par, first=False, last=False):
                for h in range(nh):
                    if h < nh - 1:
                        scores(b, par, h + 1)
                    if h:
                        weigh(b, par, h - 1)
                    if not last:
                        for j in range(h * slots, (h + 1) * slots):
                            prepare(b + 1, 1 - par, j)
                if not last:
                    scores(b + 1, 1 - par, 0)
                weigh(b, par, nh - 1)

            for j in range(8):
                prepare(0, 0, j)
            scores(0, 0, 0)
            batches(pe, turn)

        @block.scalar
        def _(act):
            act.sem_inc(decay_ready.sem, 2)
            act.wait_ge(weights_in, 96)
            act.activation(identb[:], ident[:], ACT.Copy)
            act.activation(lowerb[:], lower[:], ACT.Copy).then_inc(constants_ready, 1)

            def prepare(b, par, j):
                if j == 1 or j == 2:
                    work_filled.wait(act, b, j)
                    dst = xnT if j == 1 else cT
                    act.activation(dst[:, par], ps_w[:, j - 1], ACT.Copy).then_inc(act_drained.sem, 1)
                if j == 3:
                    work_filled.wait(act, b, 3)
                    act.activation(igr[:], ps_w[0:nh, 0, 0, :], ACT.Copy)
                    act.activation(fgr[:], ps_w[FG_ROW:FG_ROW + nh, 0, 0, :], ACT.Copy).then_inc(act_drained.sem, 1)
                if j == 4:
                    z_ready.wait(act, b, 1)
                    act.activation(ex[:], zabs[:], ACT.Exp).then_inc(ex_ready.sem, 1)
                    ex_ready.wait(act, b, 1)
                    act.activation(lg[:], ex[:], ACT.Ln, bias=1.0).then_inc(lg_ready.sem, 1)
                if j == 5:
                    mlog_ready.wait(act, b, 1)
                    act.activation(e[:], mlog[:], ACT.Exp, scale=-1.0).then_inc(e_ready.sem, 1)

            def decays(b, par, h):
                m_ready.wait(act, b, h + 1)
                if h == 0:
                    aT_ready.wait(act, b, 1)
                c_ready.wait(act, b, h - 1)
                act.activation(decay[:, h % 2, 0:S], ps_m[:, h % 2, 0:S], ACT.Exp, bias=aT[:, par, 0, 0, h:h + 1])
                act.activation(decay[:, h % 2, S:W], ps_m[:, h % 2, S:W], ACT.Exp,
                               bias=aT[:, par, 0, 1, h:h + 1]).then_inc(decay_ready.sem, 1)

            def turn(b, par, first=False, last=False):
                for h in range(nh):
                    decays(b, par, h)
                    if not last:
                        for j in range(h * slots, (h + 1) * slots):
                            prepare(b + 1, 1 - par, j)

            for j in range(8):
                prepare(0, 0, j)
            batches(act, turn)

        @block.vector
        def _(dve):
            dve.sem_inc(c_ready.sem, 2)
            dve.sem_inc(out_read.sem, 1)
            dve.sem_inc(aT_ready.sem, 1)
            dve.memset(ones[:], 1.0)
            dve.memset(va[:], 1.0).then_inc(wstep, 1)
            dve.wait_ge(weights_in, 96)
            dve.wait_ge(wstep, 1)
            dve.tensor_scalar(owg[:], ow[:], 1.0 if plus_one else 0.0, gate, ALU.add,
                              ALU.mult).then_inc(wstep, 1)
            dve.wait_ge(wstep, 2)

            def prepare(b, par, j):
                if j == 0:
                    dve.wait_ge(loaded[par], load_times(b, par, 2))
                    for t in range(TB):
                        last = dve.bn_stats(stats[:, t, :], xin[:, par, t, :])
                    last.then_inc(stats_done.sem, 1)
                    stats_done.wait_apart(dve, b, 1, passed)
                    for t in range(TB):
                        last = dve.bn_aggr(mv[:, t, :], stats[:, t, :])
                    last.then_inc(mv_ready.sem, 1)
                    dve.tensor_copy(va[:, par, :, :, 0:dh],
                                    cin[:, par].rearrange("p t (h d) -> p t h d", d=dh)).then_inc(va_ready.sem, 1)
                if j == 1:
                    rstd_ready.wait(dve, b, 1)
                    for t in range(TB):
                        last = dve.tensor_scalar(xn[:, t, :], xin[:, par, t, :], mv[:, t, 0:1], rstd[:, t:t + 1],
                                                 ALU.subtract, ALU.mult)
                    last.then_inc(xn_ready.sem, 1)
                if j == 3:
                    act_drained.wait(dve, b, 3)
                    dve.tensor_scalar(z[:], fgr[:], fb[:], None, ALU.add).then_inc(gstep.sem, 1)
                    dve.tensor_scalar(zmin[:], fgr[:], fb[:], 0.0, ALU.add, ALU.min).then_inc(gstep.sem, 1)
                    gstep.wait(dve, b, 2)
                    dve.scalar_tensor_tensor(zabs[:], zmin[:], 2.0, z[:], ALU.mult,
                                             ALU.subtract).then_inc(z_ready.sem, 1)
                if j == 4:
                    lg_ready.wait(dve, b, 1)
                    dve.tensor_tensor(logf[:], zmin[:], lg[:], ALU.subtract).then_inc(gstep.sem, 1)
                    gstep.wait(dve, b, 3)
                    dve.tensor_tensor_scan(cs[:], ones[:], logf[:], 0.0, ALU.mult, ALU.add).then_inc(gstep.sem, 1)
                    gstep.wait(dve, b, 4)
                    aT_ready.wait(dve, b, 0)
                    dve.scalar_tensor_tensor(a[:], igr[:], ib[:], cs[:], ALU.add, ALU.subtract).then_inc(gstep.sem, 1)
                    gstep.wait(dve, b, 5)
                    dve.tensor_tensor_scan(mx[:], a[:], a[:], LOWEST, ALU.max, ALU.max).then_inc(gstep.sem, 1)
                    gstep.wait(dve, b, 6)
                    dve.tensor_scalar(negm[:, par], mx[:], -1.0, None, ALU.mult)
                    dve.tensor_tensor(mlog[:], mx[:], cs[:], ALU.add).then_inc(mlog_ready.sem, 1)
                if j == 7:
                    work_filled.wait(dve, b, 4)
                    dve.tensor_copy(aT[:, par].rearrange("p i t h -> p (i t h)"),
                                    ps_w[:, 1, 0, 0:2 * G]).then_inc(aT_ready.sem, 1)

            def combine(b, par, h):
                scores_ready.wait(dve, b, h + 1)
                decay_ready.wait(dve, b, h + 1)
                head_done.wait(dve, b, h - 1)
                dve.scalar_tensor_tensor(c[:, h % 2, :], ps_q[:, h % 2, 0:W], qk_scale, decay[:, h % 2, :],
                                         ALU.mult, ALU.mult).then_inc(c_ready.sem, 1)

            def spread(x):
                return x.unsqueeze(2).broadcast_to([P, G, dh])

            def divide(b, par):
                head_done.wait(dve, b, nh)
                outs = ps_o[:, :, 0:nh * (dh + 1)].rearrange("p t (h d) -> p t h d", d=dh + 1)
                total = outs[:, :, :, dh]
                dve.scalar_tensor_tensor(den[:], total, -1.0, aT[:, par, 1], ALU.mult, ALU.max).then_inc(estep.sem, 1)
                estep.wait(dve, b, 1)
                dve.tensor_tensor(den[:], total, den[:], ALU.max).then_inc(estep.sem, 1)
                estep.wait(dve, b, 2)
                dve.tensor_scalar(den[:], den[:], NORMALISER_EPS, None, ALU.add).then_inc(estep.sem, 1)
                estep.wait(dve, b, 3)
                dve.reciprocal(rden[:], den[:]).then_inc(estep.sem, 1)
                estep.wait(dve, b, 4)
                dve.tensor_tensor(hn[:], outs[:, :, :, 0:dh], rden[:].unsqueeze(3).broadcast_to([P, TB, nh, dh]),
                                  ALU.mult).then_inc(out_read.sem, 1)

            def group_statistics(b):
                flat = hn[:].rearrange("p t h d -> p (t h) d")
                out_read.wait(dve, b, 1)
                dve.tensor_reduce(msum[:], flat, AX.X, ALU.add).then_inc(estep.sem, 1)
                estep.wait(dve, b, 5)
                dve.tensor_scalar(mean[:], msum[:], 1.0 / dh, None, ALU.mult).then_inc(estep.sem, 1)
                estep.wait(dve, b, 6)
                dve.tensor_tensor(flat, flat, spread(mean[:]), ALU.subtract).then_inc(estep.sem, 1)
                estep.wait(dve, b, 7)
                dve.tensor_tensor(sq[:], hn[:], hn[:], ALU.mult).then_inc(estep.sem, 1)
                estep.wait(dve, b, 8)
                dve.tensor_reduce(vsum[:], sq[:].rearrange("p t h d -> p (t h) d"), AX.X,
                                  ALU.add).then_inc(vsum_ready.sem, 1)

            def add_residual(b, par):
                flat = hn[:].rearrange("p t h d -> p (t h) d")
                rowsv = hn[:].rearrange("p t h d -> p t (h d)")
                grstd_ready.wait(dve, b, 1)
                dve.tensor_tensor(flat, flat, spread(grstd[:]), ALU.mult).then_inc(estep.sem, 1)
                estep.wait(dve, b, 9)
                dve.tensor_tensor(rowsv, rowsv, owg[:].unsqueeze(1).broadcast_to([P, TB, D]),
                                  ALU.mult).then_inc(estep.sem, 1)
                dve.wait_ge(xres_in[par], load_times(b, par, 1))
                estep.wait(dve, b, 10)
                dve.tensor_tensor(xres[:, par], rowsv, xres[:, par], ALU.add).then_inc(sum_ready.sem, 1)

            def finish(b, par, j):
                if j == 1:
                    divide(b, par)
                if j == 2:
                    group_statistics(b)
                if j == 5:
                    add_residual(b, par)

            def turn(b, par, first=False, last=False):
                for h in range(nh):
                    combine(b, par, h)
                    for j in range(h * slots, (h + 1) * slots):
                        if not first:
                            finish(b - 1, 1 - par, j)
                        if not last:
                            prepare(b + 1, 1 - par, j)

            for j in range(8):
                prepare(0, 0, j)
            batches(dve, turn)
            for j in range(8):
                finish(B - 1, 1, j)


E = 8


def sorted_tiles(choices):
    return (choices * B * S + E * (P - 1)) // P


MAX_TILES = sorted_tiles(2)


class Running:

    def __init__(self, m, name):
        self.sem, self.before = m.sem(name), 0

    def target(self, dmas):
        self.before += 16 * dmas
        return self.before


class Routing:

    def __init__(self, m, choices):
        self.slot = m.sb("slot", [P, choices * NT], U32)
        self.weight = m.sb("weight", [P, choices, NT])
        self.expert = m.sb("expert", [P, MAX_TILES], I32)


def route_phase(nc, name, x_src, xn_dst, sorted_dst, consts, w, routing, choices, tiles_used, experts,
                alpha, none_expert, second_norm):
    J = choices * NT
    with ExitStack() as ctx:
        m = Space(nc, ctx, name)
        wr = m.sb("wr", [P, KC, E])
        eidx = m.sb("eidx", [P, E])
        before = m.sb("before", [P, P])
        tidx = m.sb("tidx", [P, MAX_TILES])
        least = m.sb("least", [P, MAX_TILES])
        gamma = m.sb("gamma", [P, D]) if second_norm else None
        beta = m.sb("beta", [P, D]) if second_norm else None
        ones = m.sb("ones", [P, P])
        ones_row = m.sb("ones_row", [P, E * J])
        xin = m.sb("xin", [P, 2, D])
        xn = m.sb("xn", [P, 2, D])
        rn = m.sb("rn", [P, D]) if second_norm else None
        xnT = m.sb("xnT", [P, KC, P])
        logits = m.sb("logits", [P, NT, E])
        xall = m.sb("xall", [P, NT, D])
        norm = Norm(m, consts)
        if second_norm:
            m2 = Space(nc, ctx, name + "_again", m.sems)
            norm2 = Norm(m2, consts)
        top = m.sb("top", [P, choices, NT])
        ex = m.sb("ex", [P, NT, E])
        total = m.sb("total", [P, NT])
        eq = m.sb("eq", [P, NT, E])
        key = m.sb("key", [P, NT, E])
        least_key = m.sb("least_key", [P, NT])
        chosen = m.sb("chosen", [P, E, J])
        earlier = m.sb("earlier", [P, E, J])
        incl = m.sb("incl", [P, E, J])
        excl = m.sb("excl", [P, E, J])
        totals = m.sb("totals", [P, E, J])
        cnt = m.sb("cnt", [P, E])
        ntiles = m.sb("ntiles", [P, E])
        end = m.sb("end", [P, E])
        adj = m.sb("adj", [P, E])
        slotf = m.sb("slotf", [P, J])
        past = m.sb("past", [P, MAX_TILES, E])
        expf = m.sb("expf", [P, MAX_TILES])
        flag = m.sb("flag", [P, NT])

        ps_x = m.psum("ps_x", [P, 512])
        ps_l = m.psum("ps_l", [P, 512])
        ps_e = m.psum("ps_e", [P, 512])
        ps_t = m.psum("ps_t", [P, 512])

        weights_in = m.sem("weights_in")
        loaded = [m.sem("loaded0"), m.sem("loaded1")]
        norm_stored = [m.sem("norm_stored0"), m.sem("norm_stored1")]
        all_in = m.sem("all_in")
        xn_ready = Tally(m.sem("xn_ready"), 1, 1)
        rn_step = Tally(m.sem("rn_step"), 2)
        rn_ready = Tally(m.sem("rn_ready"), 1)
        xnT_ready = Tally(m.sem("xnT_ready"), 1, 1)
        xnT_copied = Tally(m.sem("xnT_copied"), 1)
        logits_ready = Tally(m.sem("logits_ready"), 1)
        logits_copied = Tally(m.sem("logits_copied"), 1, 1)
        step_done = m.sem("step_done")
        exponent_in = m.sem("exponent_in")
        exponent_out = m.sem("exponent_out")
        chosen_ready = m.sem("chosen_ready")
        counted = m.sem("counted")
        slots_ready = m.sem("slots_ready")
        scattered = w["scattered"].sem
        all_scattered = w["scattered"].target(J)
        ident = consts["ident"]
        gate = w["gate"]
        nweights = 5 + (2 if second_norm else 0)
        block = m.block()

        @block.sync
        def _(sp):
            sp.dma_start(wr[:], w["router"]).then_inc(weights_in, 16)
            sp.dma_start(eidx[:], w["eidx"]).then_inc(weights_in, 16)
            sp.dma_start(before[:], w["before"]).then_inc(weights_in, 16)
            sp.dma_start(tidx[:], w["tidx"]).then_inc(weights_in, 16)
            sp.dma_start(least[:], w["least"]).then_inc(weights_in, 16)
            if second_norm:
                sp.dma_start(gamma[:], w["gamma"].broadcast_to([P, D])).then_inc(weights_in, 16)
                sp.dma_start(beta[:], w["beta"].broadcast_to([P, D])).then_inc(weights_in, 16)

            def turn(n, par, first=False, last=False):
                if first:
                    sp.dma_start(xin[:, 0], tile_rows(x_src, 0)).then_inc(loaded[0], 16)
                if not last:
                    xn_ready.wait(sp, n, 0)
                    sp.dma_start(xin[:, 1 - par], tile_rows(x_src, n + 1)).then_inc(loaded[1 - par], 16)
                xn_ready.wait(sp, n, 1)
                sp.dma_start(xn_dst[n], xn[:, par]).then_inc(norm_stored[par], 16)

            tiles(sp, turn)
            for par in range(2):
                sp.wait_ge(norm_stored[par], 16 * (NT // 2))
            sp.dma_start(xall[:], xn_dst.rearrange("n p d -> p n d")).then_inc(all_in, 16)

        @block.gpsimd
        def _(pool):
            with pool.Fori(0, NT) as n:
                norm.on_pool(pool, n)
                if second_norm:
                    norm2.on_pool(pool, n)
            pool.wait_ge(all_in, 16)
            pool.wait_ge(slots_ready, 1)
            for c in range(choices):
                for n in range(NT):
                    j = c * NT + n
                    pool.indirect_dma_start(
                        out=sorted_dst, out_offset=bass.IndirectOffsetOnAxis(ap=routing.slot[:, j:j + 1], axis=0),
                        in_=xall[:, n, :], in_offset=None).then_inc(scattered, 16)
            pool.wait_ge(scattered, all_scattered)

        @block.tensor
        def _(pe):
            pe.sem_inc(xnT_ready.sem, 1)
            pe.wait_ge(weights_in, 16 * nweights)

            def turn(n, par, first=False, last=False):
                (rn_ready if second_norm else xn_ready).wait(pe, n, 1)
                src = rn if second_norm else xn[:, par]
                for k in range(KC):
                    last_t = pe.transpose(ps_x[:, k * P:(k + 1) * P], src[:, k * P:(k + 1) * P], ident[:])
                last_t.then_inc(xnT_ready.sem, 1)
                xnT_copied.wait(pe, n, 1)
                logits_copied.wait(pe, n, 0)
                for k in range(KC):
                    last_m = pe.matmul(ps_l[:, 0:E], xnT[:, k, :], wr[:, k, :], start=(k == 0), stop=(k == KC - 1))
                last_m.then_inc(logits_ready.sem, 1)

            tiles(pe, turn)
            pe.wait_ge(chosen_ready, 1)
            flat = chosen[:].rearrange("p e j -> p (e j)")
            pe.matmul(ps_e[:, 0:E * J], before[:], flat, start=True, stop=True)
            pe.matmul(ps_t[:, 0:E * J], ones[:], flat, start=True, stop=True).then_inc(counted, 1)

        @block.scalar
        def _(act):
            def turn(n, par, first=False, last=False):
                xnT_ready.wait(act, n, 1)
                act.activation(xnT[:].rearrange("p k n -> p (k n)"), ps_x[:, 0:D],
                               ACT.Copy).then_inc(xnT_copied.sem, 1)

            tiles(act, turn)
            act.wait_ge(exponent_in, 1)
            act.activation(ex[:], logits[:], ACT.Exp).then_inc(exponent_out, 1)

        @block.vector
        def _(dve):
            dve.sem_inc(xn_ready.sem, 1)
            dve.sem_inc(logits_copied.sem, 1)
            done = [0]

            def step(ins):
                done[0] += 1
                ins.then_inc(step_done, 1)
                dve.wait_ge(step_done, done[0])

            step(dve.memset(ones[:], 1.0))
            step(dve.memset(ones_row[:], 1.0))
            dve.wait_ge(weights_in, 16 * nweights)

            def normalise(n, par, first=False):
                dve.wait_ge(loaded[par], tile_times(n, par, 1))
                norm.statistics(dve, xin[:, par], n)
                if not first:
                    dve.wait_ge(norm_stored[par], tile_times(n, par, 1) - 16)
                norm.apply(dve, xn[:, par], xin[:, par], n).then_inc(xn_ready.sem, 1)
                if second_norm:
                    xn_ready.wait(dve, n, 1)
                    norm2.statistics(dve, xn[:, par], n)
                    norm2.apply(dve, rn[:], xn[:, par], n).then_inc(rn_step.sem, 1)
                    rn_step.wait(dve, n, 1)
                    dve.tensor_tensor(rn[:], rn[:], gamma[:], ALU.mult).then_inc(rn_step.sem, 1)
                    rn_step.wait(dve, n, 2)
                    dve.tensor_tensor(rn[:], rn[:], beta[:], ALU.add).then_inc(rn_ready.sem, 1)

            def turn(n, par, first=False, last=False):
                if first:
                    normalise(0, 0, first=True)
                if not last:
                    if second_norm:
                        xnT_ready.wait(dve, n, 1)
                    normalise(n + 1, 1 - par, first=first)
                logits_ready.wait(dve, n, 1)
                dve.tensor_scalar(logits[:, n, :],
                                  ps_l[:, 0:E], 1.0, None, ALU.mult).then_inc(logits_copied.sem, 1)

            tiles(dve, turn)
            logits_copied.wait(dve, NT - 1, 1)

            def over_experts(x):
                return x.unsqueeze(2).broadcast_to([P, NT, E])

            step(dve.tensor_reduce(total[:], logits[:], AX.X, ALU.max))
            dve.tensor_tensor(logits[:], logits[:], over_experts(total[:]), ALU.subtract).then_inc(exponent_in, 1)
            dve.wait_ge(exponent_out, 1)
            step(dve.tensor_reduce(total[:], ex[:], AX.X, ALU.add))
            step(dve.reciprocal(total[:], total[:]))
            step(dve.tensor_tensor(ex[:], ex[:], over_experts(total[:]), ALU.mult))
            eids = eidx[:].unsqueeze(1).broadcast_to([P, NT, E])
            for c in range(choices):
                step(dve.tensor_reduce(top[:, c], ex[:], AX.X, ALU.max))
                step(dve.tensor_tensor(eq[:], ex[:], over_experts(top[:, c]), ALU.is_equal))
                step(dve.scalar_tensor_tensor(key[:], eq[:], -2.0 * E, eids, ALU.mult, ALU.add))
                step(dve.tensor_reduce(least_key[:], key[:], AX.X, ALU.min))
                mine = chosen[:, :, c * NT:(c + 1) * NT].rearrange("p e n -> p n e")
                step(dve.tensor_tensor(mine, key[:], over_experts(least_key[:]), ALU.is_equal))
                if c < choices - 1:
                    step(dve.scalar_tensor_tensor(ex[:], mine, -4.0, ex[:], ALU.mult, ALU.add))
                if none_expert:
                    step(dve.tensor_scalar(flag[:], chosen[:, E - 1, c * NT:(c + 1) * NT], -alpha, alpha,
                                           ALU.mult, ALU.add))
                    step(dve.tensor_tensor(top[:, c], top[:, c], flag[:], ALU.mult))
            step(dve.tensor_scalar(routing.weight[:], top[:], gate, None, ALU.mult))
            dve.sem_inc(chosen_ready, 1)
            dve.wait_ge(counted, 1)
            flat = "p e j -> p (e j)"
            step(dve.tensor_copy(totals[:].rearrange(flat), ps_t[:, 0:E * J]))
            step(dve.tensor_tensor_scan(incl[:].rearrange(flat), ones_row[:], totals[:].rearrange(flat), 0.0,
                                        ALU.mult, ALU.add))
            step(dve.tensor_tensor(excl[:], incl[:], totals[:], ALU.subtract))
            step(dve.tensor_tensor(earlier[:].rearrange(flat), ps_e[:, 0:E * J], excl[:].rearrange(flat), ALU.add))
            step(dve.tensor_tensor(cnt[:], incl[:, :, J - 1], excl[:, :, 0], ALU.subtract))
            step(dve.tensor_scalar(ntiles[:], cnt[:], 1.0 / P, 0.5 - 0.5 / P, ALU.mult, ALU.add))
            step(dve.tensor_scalar(ntiles[:], ntiles[:], MAGIC, None, ALU.add))
            step(dve.tensor_scalar(ntiles[:], ntiles[:], MAGIC, None, ALU.subtract))
            step(dve.tensor_tensor_scan(end[:], ones_row[:, 0:E], ntiles[:], 0.0, ALU.mult, ALU.add))
            step(dve.tensor_tensor(adj[:], end[:], ntiles[:], ALU.subtract))
            step(dve.scalar_tensor_tensor(adj[:], adj[:], float(P), excl[:, :, 0], ALU.mult, ALU.subtract))
            step(dve.tensor_tensor(earlier[:], earlier[:], adj[:].unsqueeze(2).broadcast_to([P, E, J]), ALU.add))
            step(dve.tensor_tensor(earlier[:], earlier[:], chosen[:], ALU.mult))
            step(dve.tensor_reduce(slotf[:], earlier[:].rearrange("p e j -> p j e"), AX.X, ALU.add))
            step(dve.tensor_copy(routing.slot[:], slotf[:]))
            dve.sem_inc(slots_ready, 1)
            ne = experts - 1
            step(dve.tensor_tensor(past[:, :, 0:ne], tidx[:].unsqueeze(2).broadcast_to([P, MAX_TILES, ne]),
                                   end[:, 0:ne].unsqueeze(1).broadcast_to([P, MAX_TILES, ne]), ALU.is_ge))
            step(dve.tensor_reduce(expf[:], past[:, :, 0:ne], AX.X, ALU.add))
            step(dve.tensor_tensor(expf[:], expf[:], least[:], ALU.max))
            step(dve.tensor_copy(routing.expert[:], expf[:]))


def experts_phase(nc, name, x_rows, y_rows, w, routing, n_sorted, n_shared, F, kind):
    FC = F // P
    HC = FC // 2
    HW = HC * P
    mats = 2 if kind == "swiglu" else 1
    up_cols = mats * KC * HW
    down_cols = FC * D + (FC if kind == "relu" else 0)
    ntiles = n_sorted + n_shared
    sets = 3 if n_shared else 2
    with ExitStack() as ctx:
        m = Space(nc, ctx, name)
        wup = m.sb("wup", [P, sets, 2, up_cols])
        wdown = m.sb("wdown", [P, sets, down_cols])
        b2 = m.sb("b2", [P, 2, D])
        x = m.sb("x", [P, 2, D])
        xT = m.sb("xT", [P, 2, KC, P])
        act_out = m.sb("act_out", [P, 2, HW])
        hT = m.sb("hT", [P, 2, FC * P])
        y = m.sb("y", [P, 2, D])
        ps_a = m.psum("ps_a", [P, 2, 512])
        ps_b = m.psum("ps_b", [P, 2, 512])
        ps_x = m.psum("ps_x", [P, 512])
        ps_y = m.psum("ps_y", [P, 2, 512])

        up_in = [[m.sem(f"up_in{half}{par}") for par in range(2)] for half in range(2)]
        down_in = [m.sem("down_in0"), m.sem("down_in1")]
        shared_in = m.sem("shared_in")
        x_in = [m.sem("x_in0"), m.sem("x_in1")]
        stored = [m.sem("stored0"), m.sem("stored1")]
        xT_ready = Tally(m.sem("xT_ready"), 1)
        xT_copied = Tally(m.sem("xT_copied"), 1)
        up_ready = Tally(m.sem("up_ready"), 2)
        act_ready = Tally(m.sem("act_ready"), 2)
        h_ready = Tally(m.sem("h_ready"), 2, 2)
        y_ready = Tally(m.sem("y_ready"), 1, 2)
        y_copied = Tally(m.sem("y_copied"), 1, 2)
        per = 2 if kind == "relu" else 1
        block = m.block()

        def turns(engine, turn):
            turn(0, 0, first=True)
            with engine.Fori(0, (n_sorted - 3) // 2) as pair:
                turn(2 * pair + 1, 1)
                turn(2 * pair + 2, 0)
            turn(n_sorted - 2, 1)
            turn(n_sorted - 1, 0, last=not n_shared, next_shared=True)
            if n_shared:
                turn(n_sorted, 1, shared=True, next_shared=True)
                with engine.Fori(0, n_shared // 2 - 1) as pair:
                    turn(2 * pair + (n_sorted + 1), 0, shared=True, next_shared=True)
                    turn(2 * pair + (n_sorted + 2), 1, shared=True, next_shared=True)
                turn(ntiles - 1, 0, last=True, shared=True)

        @block.sync
        def _(sp):
            def load(i, par, shared):
                reused = not isinstance(i, int) or i >= 2
                if reused:
                    xT_ready.wait(sp, i, -1)
                sp.dma_start(x[:, par], x_rows[i]).then_inc(x_in[par], 16)
                if shared:
                    return
                e = sp.value_load(routing.expert[0:1, i:i + 1] if isinstance(i, int)
                                  else routing.expert[0:1, bass.ds(i, 1)], min_val=0, max_val=E - 1)
                for half in range(2):
                    if reused:
                        up_ready.wait(sp, i, half - 3)
                    sp.dma_start(wup[:, par, half], w["experts"][e][:, half * up_cols:(half + 1) * up_cols]
                                 ).then_inc(up_in[half][par], 16)
                if reused:
                    y_ready.wait(sp, i, -1)
                sp.dma_start(wdown[:, par], w["experts"][e][:, 2 * up_cols:]).then_inc(down_in[par], 16)
                if kind == "relu":
                    if reused:
                        y_copied.wait(sp, i, -1)
                    sp.dma_start(b2[:, par], w["b2"][e].broadcast_to([P, D])).then_inc(down_in[par], 16)

            def turn(i, par, first=False, last=False, shared=False, next_shared=False):
                if first:
                    load(0, 0, False)
                if not last:
                    load(i + 1, 1 - par, next_shared)
                if n_shared and isinstance(i, int) and i == n_sorted - 2:
                    sp.dma_start(wup[:, 2], w["experts"][E - 1][:, 0:2 * up_cols].rearrange("p (h n) -> p h n", h=2)
                                 ).then_inc(shared_in, 16)
                    sp.dma_start(wdown[:, 2], w["experts"][E - 1][:, 2 * up_cols:]).then_inc(shared_in, 16)

            turns(sp, turn)

        @block.tensor
        def _(pe):
            pe.sem_inc(y_ready.sem, 2)

            def turn_x(i, par):
                pe.wait_ge(x_in[par], tile_times(i, par, 1))
                for k in range(KC):
                    last = pe.transpose(ps_x[:, k * P:(k + 1) * P], x[:, par, k * P:(k + 1) * P], w["ident"][:])
                last.then_inc(xT_ready.sem, 1)

            def up(i, par, half, shared):
                if half == 0:
                    xT_copied.wait(pe, i, 1)
                if not shared:
                    pe.wait_ge(up_in[half][par], tile_times(i, par, 1))
                elif half == 0:
                    pe.wait_ge(shared_in, 32)
                wset = 2 if shared else par
                h_ready.wait(pe, i, half - 1)
                for n, bank in enumerate((ps_a, ps_b)[:mats]):
                    for f in range(HC):
                        for k in range(KC):
                            at = (n * KC + k) * HW + f * P
                            last = pe.matmul(bank[:, half, f * P:(f + 1) * P], wup[:, wset, half, at:at + P],
                                             xT[:, par, k, :], start=(k == 0), stop=(k == KC - 1))
                last.then_inc(up_ready.sem, 1)

            def down(i, par, shared):
                if not shared:
                    pe.wait_ge(down_in[par], tile_times(i, par, per))
                h_ready.wait(pe, i, 2)
                y_copied.wait(pe, i, -1)
                wset = 2 if shared else par
                for f in range(FC):
                    last = pe.matmul(ps_y[:, par, 0:D], hT[:, par, f * P:(f + 1) * P],
                                     wdown[:, wset, f * D:(f + 1) * D], start=(f == 0), stop=(f == FC - 1))
                last.then_inc(y_ready.sem, 1)

            def turn(i, par, first=False, last=False, shared=False, next_shared=False):
                if first:
                    turn_x(0, 0)
                up(i, par, 0, shared)
                if not first:
                    down(i - 1, 1 - par, shared and not (isinstance(i, int) and i == n_sorted))
                if not last:
                    turn_x(i + 1, 1 - par)
                up(i, par, 1, shared)

            turns(pe, turn)
            down(ntiles - 1, 0, bool(n_shared))

        @block.scalar
        def _(act):
            act.sem_inc(y_copied.sem, 2)
            act.sem_inc(stored[0], 16)
            act.sem_inc(stored[1], 16)

            def copy_x(i, par):
                xT_ready.wait(act, i, 1)
                act.activation(xT[:, par].rearrange("p k n -> p (k n)"), ps_x[:, 0:D],
                               ACT.Copy).then_inc(xT_copied.sem, 1)

            def activate(i, par, half):
                if kind == "relu":
                    act.wait_ge(down_in[par], tile_times(i, par, per))
                up_ready.wait(act, i, half + 1)
                if kind == "swiglu":
                    act.activation(act_out[:, half], ps_a[:, half, 0:HW], ACT.Silu).then_inc(act_ready.sem, 1)
                if kind == "gelu":
                    act.activation(hT[:, par, half * HW:(half + 1) * HW], ps_a[:, half, 0:HW],
                                   ACT.Gelu).then_inc(h_ready.sem, 1)
                if kind == "relu":
                    for f in range(HC):
                        ff = half * HC + f
                        bias = wdown[:, par, FC * D + ff:FC * D + ff + 1]
                        last = act.activation(hT[:, par, ff * P:(ff + 1) * P], ps_a[:, half, f * P:(f + 1) * P],
                                              ACT.Relu, bias=bias)
                    last.then_inc(h_ready.sem, 1)

            def store(i, par):
                if kind != "relu":
                    y_ready.wait(act, i, 1)
                    act.wait_ge(stored[par], tile_times(i, par, 1))
                    act.activation(y[:, par], ps_y[:, par, 0:D], ACT.Copy).then_inc(y_copied.sem, 1)
                y_copied.wait(act, i, 1)
                act.dma_start(y_rows[i], y[:, par]).then_inc(stored[par], 16)

            def turn(i, par, first=False, last=False, shared=False, next_shared=False):
                if first:
                    if kind != "swiglu":
                        act.sem_inc(h_ready.sem, 2)
                    copy_x(0, 0)
                activate(i, par, 0)
                if not last:
                    copy_x(i + 1, 1 - par)
                if not first:
                    store(i - 1, 1 - par)
                activate(i, par, 1)

            turns(act, turn)
            store(ntiles - 1, 0)
            act.wait_ge(stored[0], 16 * ((ntiles + 1) // 2) + 16)
            act.wait_ge(stored[1], 16 * (ntiles // 2) + 16)

        @block.vector
        def _(dve):
            if kind == "swiglu":
                dve.sem_inc(h_ready.sem, 2)

                def multiply(i, par, half):
                    act_ready.wait(dve, i, half + 1)
                    dve.tensor_tensor(hT[:, par, half * HW:(half + 1) * HW], ps_b[:, half, 0:HW], act_out[:, half],
                                      ALU.mult).then_inc(h_ready.sem, 1)

                def turn(i, par, first=False, last=False, shared=False, next_shared=False):
                    multiply(i, par, 0)
                    multiply(i, par, 1)

                turns(dve, turn)
            if kind == "relu":
                def add_bias(i, par):
                    y_ready.wait(dve, i, 1)
                    dve.wait_ge(stored[par], tile_times(i, par, 1))
                    dve.tensor_tensor(y[:, par], ps_y[:, par, 0:D], b2[:, par], ALU.add).then_inc(y_copied.sem, 1)

                def turn(i, par, first=False, last=False, shared=False, next_shared=False):
                    add_bias(i, par)

                turns(dve, turn)


def combine_phase(nc, name, x_src, x_dst, y_sorted, y_shared, consts, routing, choices, gate_col, gathers):
    QT = NT // 4
    with ExitStack() as ctx:
        m = Space(nc, ctx, name)
        x = m.sb("x", [P, NT, D])
        y = m.sb("y", [P, choices, NT, D])
        ysh = m.sb("ysh", [P, NT, D]) if y_shared is not None else None
        x_in = [m.sem(f"x_in{q}") for q in range(4)]
        gathered = [g.sem for g in gathers]
        all_gathered = [g.target(QT * choices) for g in gathers]
        step_done = m.sem("step_done")
        sum_ready = m.sem("sum_ready")
        stored = m.sem("stored")
        nx = 2 if y_shared is not None else 1
        block = m.block()
        xs = x_src.rearrange("b (t p) d -> p (b t) d", p=P)
        xd = x_dst.rearrange("b (t p) d -> p (b t) d", p=P)
        part = [slice(q * QT, (q + 1) * QT) for q in range(4)]

        @block.sync
        def _(sp):
            for q in range(4):
                sp.dma_start(x[:, part[q]], xs[:, part[q]]).then_inc(x_in[q], 16)
                if y_shared is not None:
                    sp.dma_start(ysh[:, part[q]], y_shared.rearrange("n p d -> p n d")[:, part[q]]).then_inc(x_in[q], 16)
            for q in range(4):
                sp.wait_ge(sum_ready, q + 1)
                sp.dma_start(xd[:, part[q]], x[:, part[q]]).then_inc(stored, 16)
            sp.wait_ge(stored, 64)

        @block.gpsimd
        def _(pool):
            for q in range(4):
                for n in range(q * QT, (q + 1) * QT):
                    for c in range(choices):
                        j = c * NT + n
                        pool.indirect_dma_start(
                            out=y[:, c, n, :], out_offset=None, in_=y_sorted,
                            in_offset=bass.IndirectOffsetOnAxis(ap=routing.slot[:, j:j + 1], axis=0),
                        ).then_inc(gathered[q], 16)

        @block.vector
        def _(dve):
            done = [0]

            def step(ins):
                done[0] += 1
                ins.then_inc(step_done, 1)
                dve.wait_ge(step_done, done[0])

            for q in range(4):
                dve.wait_ge(x_in[q], 16 * nx)
                if y_shared is not None:
                    step(dve.scalar_tensor_tensor(x[:, part[q]], ysh[:, part[q]], consts["gates"][:, gate_col:gate_col + 1],
                                                  x[:, part[q]], ALU.mult, ALU.add))
                dve.wait_ge(gathered[q], all_gathered[q])
                for c in range(choices):
                    for n in range(q * QT, (q + 1) * QT):
                        last = dve.scalar_tensor_tensor(x[:, n, :], y[:, c, n, :], routing.weight[:, c, n:n + 1],
                                                        x[:, n, :], ALU.mult, ALU.add)
                    if c < choices - 1:
                        step(last)
                last.then_inc(sum_ready, 1)


def moe(nc, m, name, x_src, x_dst, consts, w, scratch, choices, F, kind, gate_col, alpha=1.0, shared=False,
        second_norm=False):
    n_sorted = sorted_tiles(choices)
    with ExitStack() as ctx:
        routing = Routing(Space(nc, ctx, name + "_routing"), choices)
        xs, ys = scratch["x_sorted"], scratch["y_sorted"]
        xn = xs[n_sorted:n_sorted + NT] if shared else scratch["x_norm"]
        flat = "n p d -> (n p) d"
        w = dict(w, gate=consts["gates"][:, gate_col:gate_col + 1], ident=consts["ident"], eidx=scratch["eidx"],
                 before=scratch["before"], tidx=scratch["tidx"], scattered=scratch["scattered"])
        route_phase(nc, name + "_route", x_src, xn, xs.rearrange(flat), consts, w, routing, choices, n_sorted,
                    E - 1 if shared else E, alpha, shared, second_norm)
        experts_phase(nc, name + "_experts", xs, ys, w, routing, n_sorted, NT if shared else 0, F, kind)
        combine_phase(nc, name + "_sum", x_src, x_dst, ys.rearrange(flat),
                      ys[n_sorted:n_sorted + NT] if shared else None, consts, routing, choices, gate_col,
                      scratch["gathers"])


def setup_phase(nc, consts, ident_dram, g_dram, x_sorted):
    with ExitStack() as ctx:
        m = Space(nc, ctx, "setup")
        zeros = m.sb("zeros", [P, D])
        const_in = m.sem("const_in")
        zeros_set = m.sem("zeros_set")
        zeros_out = m.sem("zeros_out")
        set_done = m.sem("set_done")
        block = m.block()

        @block.sync
        def _(sp):
            sp.dma_start(consts["ident"][:], ident_dram).then_inc(const_in, 16)
            sp.dma_start(consts["raw_gates"][:], g_dram.broadcast_to([P, 2 * LAYERS])).then_inc(const_in, 16)
            sp.wait_ge(zeros_set, 1)
            sp.dma_start(x_sorted.rearrange("n p d -> p n d"),
                         zeros[:].unsqueeze(1).broadcast_to([P, MAX_TILES, D])).then_inc(zeros_out, 16)
            sp.wait_ge(zeros_out, 16)

        @block.gpsimd
        def _(pool):
            pool.memset(consts["minus_half"][:], -0.5).then_inc(set_done, 1)
            pool.wait_ge(set_done, 1)

        @block.vector
        def _(dve):
            dve.memset(zeros[:], 0.0).then_inc(zeros_set, 1)

        @block.scalar
        def _(act):
            act.wait_ge(const_in, 32)
            act.activation(consts["gates"][:], consts["raw_gates"][:], ACT.Tanh)


def program(nc, t, out, upto):
    with ExitStack() as ctx:
        m = Space(nc, ctx, "all")
        consts = {
            "ident": m.sb("ident", [P, P]),
            "raw_gates": m.sb("raw_gates", [P, 2 * LAYERS]),
            "gates": m.sb("gates", [P, 2 * LAYERS]),
            "minus_half": m.sb("minus_half", [P, TB * H]),
        }
        def dram(name, shape):
            return nc.dram_tensor(name, shape, F32).ap()

        scratch = {
            "x_sorted": dram("x_sorted", [MAX_TILES, P, D]), "y_sorted": dram("y_sorted", [MAX_TILES, P, D]),
            "x_norm": dram("x_norm", [NT, P, D]),
            "scattered": Running(m, "scattered"), "gathers": [Running(m, f"gathered{q}") for q in range(4)],
            "eidx": t["eidx"], "before": t["before"], "tidx": t["tidx"],
        }
        setup_phase(nc, consts, t["ident"], t["gates"], scratch["x_sorted"])
        xs = [t["x"]] + [dram(f"x_after_{i}", [B, S, D]) for i in range(upto - 1)] + [out]
        steps = [
            lambda a, b: attention_phase(nc, "a0", a, b, t["ctx"], consts,
                                         {k: t["a0_" + k] for k in ("wq", "wk", "wv", "wo")}, 0, DH ** -0.5, t["mask"]),
            lambda a, b: quantised_ffn_phase(nc, "f0", a, b, consts,
                                             {"gate": t["f0_gate"], "up": t["f0_up"], "down": t["f0_down"]}, 4),
            lambda a, b: mlstm_phase(nc, "m1", a, b, t["ctx"], consts,
                                     {k: t["m1_" + k] for k in ("gates", "ib", "fb", "ow", "sel", "lower")}, 1, 8,
                                     False),
            lambda a, b: moe(nc, m, "f1", a, b, consts,
                             {"router": t["f1_router"], "experts": t["f1_experts"], "least": t["f1_least"]}, scratch,
                             1, 1024, "swiglu", 5, alpha=2.0, shared=True),
            lambda a, b: attention_phase(nc, "a2", a, b, t["ctx"], consts,
                                         {k: t["a2_" + k] for k in ("wq", "wk", "wv", "wo", "bq", "bk", "bv", "bo")},
                                         2, D ** -0.5),
            lambda a, b: moe(nc, m, "f2", a, b, consts,
                             {"router": t["f2_router"], "experts": t["f2_experts"], "b2": t["f2_b2"],
                              "least": t["least"]}, scratch, 1, 1024, "relu", 6),
            lambda a, b: mlstm_phase(nc, "m3", a, b, t["ctx"], consts,
                                     {k: t["m3_" + k] for k in ("gates", "ib", "fb", "ow", "sel", "lower")}, 3, 4,
                                     True),
            lambda a, b: moe(nc, m, "f3", a, b, consts,
                             {"router": t["f3_router"], "experts": t["f3_experts"], "least": t["least"],
                              "gamma": t["f3_gamma"], "beta": t["f3_beta"]}, scratch, 2, 512, "gelu", 7,
                             second_norm=True),
        ]
        for i, step in enumerate(steps[:upto]):
            step(xs[i], xs[i + 1])


LAYERS = 4
UPTO = 8


def _chunks(w):
    return w.reshape(-1, P, w.shape[-1]).transpose(1, 0, 2)


def _spread(w, heads):
    k = w.shape[0]
    out = np.zeros((k, heads, 32), w.dtype)
    out[:, :, :w.shape[1] // heads] = w.reshape(k, heads, -1)
    return out.reshape(k, heads * 32)


def _experts(up, down, bias=None):
    parts = []
    for half in range(2):
        for m in up:
            f = m.shape[2] // 2
            parts.append(np.stack([_chunks(w[:, half * f:(half + 1) * f]).reshape(P, -1) for w in m]))
    parts.append(np.stack([_chunks(w).reshape(P, -1) for w in down]))
    if bias is not None:
        parts.append(np.stack([_chunks(w[:, None]).reshape(P, -1) for w in bias]))
    return np.concatenate(parts, axis=2)


def _mlstm(prefix, wi, bi, wf, bf, scale):
    nh = len(bi)
    gates = np.zeros((wi.shape[1], 64), np.float32)
    gates[:, 0:nh] = wi.T
    gates[:, FG_ROW:FG_ROW + nh] = wf.T
    t, s = np.arange(P)[:, None], np.arange(P)[None, :]
    return {
        prefix + "gates": _chunks(gates), prefix + "ib": bi[:, None], prefix + "fb": bf[:, None],
        prefix + "ow": scale[None, :],
        prefix + "sel": np.repeat(np.eye(nh, dtype=np.float32), P, axis=1),
        prefix + "lower": np.where(t > s, np.float32(-1e30), np.float32(0)),
    }


def kernel(**inputs):
    import concourse.bacc as bacc
    from concourse.bass_utils import run_bass_kernel_spmd

    v = {k: np.asarray(a) for k, a in inputs.items()}
    laid = {
        "x": v["x"], "ctx": v["ctx_1024"], "mask": v["mask_BxSxS2_ff0"],
        "ident": np.eye(P, dtype=np.float32),
        "gates": np.concatenate([v["g_xattn"], v["g_ffn"]])[None, :],
        "a0_wq": _chunks(_spread(v["L0_xattn_Wq"], H)), "a0_wk": _chunks(_spread(v["L0_xattn_Wk"], H)),
        "a0_wv": _chunks(v["L0_xattn_Wv"]), "a0_wo": _chunks(v["L0_xattn_Wo"]),
        "f0_gate": _chunks(v["L0_ffn_w_gate"].T), "f0_up": _chunks(v["L0_ffn_w_up"].T),
        "f0_down": _chunks(v["L0_ffn_w_down"].T),
        **_mlstm("m1_", v["L1_xattn_igate_w"], v["L1_xattn_igate_b"], v["L1_xattn_fgate_w"],
                 v["L1_xattn_fgate_b"], v["L1_xattn_out_w"]),
    }
    rows_of = np.arange(P)
    laid.update({
        "eidx": np.broadcast_to(np.arange(E, dtype=np.float32), (P, E)),
        "before": (rows_of[:, None] < rows_of[None, :]).astype(np.float32),
        "tidx": np.broadcast_to(np.arange(MAX_TILES, dtype=np.float32), (P, MAX_TILES)),
        "least": np.zeros((P, MAX_TILES), np.float32),
        "f1_least": np.broadcast_to(np.where(np.arange(MAX_TILES) < sorted_tiles(1), 0, E - 1).astype(np.float32),
                                    (P, MAX_TILES)),
        "f1_router": _chunks(v["L1_ffn_Wr"]),
        "f1_experts": _experts([np.concatenate([v["L1_ffn_Wg"], v["L1_ffn_Wg_s"][None]]),
                                np.concatenate([v["L1_ffn_Wu"], v["L1_ffn_Wu_s"][None]])],
                               np.concatenate([v["L1_ffn_Wd"], v["L1_ffn_Wd_s"][None]])),
        "a2_wq": _chunks(_spread(v["L2_xattn_wq"], H)), "a2_wk": _chunks(_spread(v["L2_xattn_wk"], H)),
        "a2_wv": _chunks(v["L2_xattn_wv"]), "a2_wo": _chunks(v["L2_xattn_wo"]),
        "a2_bq": _spread(v["L2_xattn_bq"][None, :], H).reshape(HG, P).T,
        "a2_bk": _spread(v["L2_xattn_bk"][None, :], H).reshape(HG, P).T,
        "a2_bv": v["L2_xattn_bv"][None, :], "a2_bo": v["L2_xattn_bo"][None, :],
        "f2_router": _chunks(v["L2_ffn_gate_w"].T),
        "f2_experts": _experts([v["L2_ffn_w1"]], v["L2_ffn_w2"], v["L2_ffn_b1"]),
        "f2_b2": v["L2_ffn_b2"][:, None, :],
        **_mlstm("m3_", v["L3_xattn_w_igate"], v["L3_xattn_b_igate"], v["L3_xattn_w_fgate"],
                 v["L3_xattn_b_fgate"], v["L3_xattn_ln_weight"]),
        "f3_router": _chunks(v["L3_ffn_gate_w"].T),
        "f3_gamma": v["L3_ffn_ln_gamma"][None, :], "f3_beta": v["L3_ffn_ln_beta"][None, :],
        "f3_experts": _experts([v["L3_ffn_w1"].transpose(0, 2, 1)], v["L3_ffn_w2"].transpose(0, 2, 1)),
    })
    nc = bacc.Bacc("TRN2", target_bir_lowering=False, num_devices=1)
    arrays, tensors = {}, {}
    for name, a in laid.items():
        arrays[f"in_{name}"] = np.ascontiguousarray(a)
        tensors[name] = nc.dram_tensor(f"in_{name}", a.shape, mybir.dt.from_np(a.dtype), kind="ExternalInput").ap()
    out = nc.dram_tensor("out_x", [B, S, D], F32, kind="ExternalOutput").ap()
    program(nc, tensors, out, UPTO)
    result = run_bass_kernel_spmd(nc, [arrays], core_ids=[0])
    return result.results[0]["out_x"]
```

```python
from contextlib import ExitStack

import numpy as np

import concourse.bass as bass
from concourse import mybir

ALU = mybir.AluOpType
ACT = mybir.ActivationFunctionType
AX = mybir.AxisListType
F32 = mybir.dt.float32
BF16 = mybir.dt.bfloat16
I32 = mybir.dt.int32
U32 = mybir.dt.uint32

P = 128
B = 8
S = 256
D = 256
TB = S // P
KC = D // P
LN_EPS = 1e-5
MASK_FACTOR = 1e9


class Space:

    def __init__(self, nc, ctx, name, sems=None):
        self.nc, self.ctx, self.name = nc, ctx, name
        self.sems = [] if sems is None else sems

    def sb(self, name, shape, dt=F32):
        return self.ctx.enter_context(self.nc.sbuf_tensor(f"{self.name}_{name}", shape, dt))

    def psum(self, name, shape, dt=F32):
        return self.ctx.enter_context(self.nc.psum_tensor(f"{self.name}_{name}", shape, dt))

    def sem(self, name):
        sem = self.ctx.enter_context(self.nc.semaphore(f"{self.name}_{name}"))
        self.sems.append(sem)
        return sem

    def block(self):
        self.ctx.callback(self.clear)
        return self.ctx.enter_context(self.nc.Block())

    def clear(self):
        with self.nc.Block() as block:
            @block.sync
            def _(sp):
                for sem in self.sems:
                    sp.sem_clear(sem)


class Tally:

    def __init__(self, sem, per, first=0):
        self.sem, self.per, self.first = sem, per, first

    def wait(self, engine, b, k):
        engine.wait_ge(self.sem, b * self.per + (self.first + k))

    def wait_apart(self, engine, b, k, passed):
        self.wait(engine, b, k)
        engine.sem_inc(passed, 1)


def rows(dram, b):
    return dram[b].rearrange("(t p) d -> p t d", p=P)


def batches(engine, turn):
    turn(0, 0, first=True)
    with engine.Fori(0, B // 2 - 2) as pair:
        turn(2 * pair + 1, 1)
        turn(2 * pair + 2, 0)
    turn(B - 3, 1)
    turn(B - 2, 0, before_last=True)
    turn(B - 1, 1, last=True)


def load_times(b, par, per):
    return (b - par) * (8 * per) + 16 * per


H = 16
DH = D // H
PARTS = 3
Q_PARTS = ((0, 3), (1, 2), (2, 1))
K_PARTS = (3, 2, 1)
STACK = 6 * DH
STACK_M = STACK + PARTS
MAXIMA_AT = {5: 2, 6: 1, 7: 2, 8: 1, 9: 2, 10: 1, 11: 2, 12: 1, 13: 2, 14: 1, 15: 1}


def attention_phase(nc, name, x_src, x_dst, ctx_dram, consts, w, gate_col, score_scale, bounce, mask_drams=None):
    masked = mask_drams is not None
    biased = "bq" in w
    DA = DH + 1
    with ExitStack() as ctx:
        m = Space(nc, ctx, name)
        wq = m.sb("wq", [P, KC, D])
        wk = m.sb("wk", [P, KC, D])
        wv = m.sb("wv", [P, KC, D])
        wo = m.sb("wo", [P, KC, D])
        bq = m.sb("bq", [P, KC])
        bqs = m.sb("bqs", [P, KC])
        bk = m.sb("bk", [P, KC])
        bv = m.sb("bv", [1, D])
        ones_row = m.sb("ones_row", [1, P])
        bo = m.sb("bo", [P, D])
        xin = m.sb("xin", [P, 2, TB, D])
        cin = m.sb("cin", [P, 2, TB, D])
        xres = m.sb("xres", [P, 2, TB, D])
        mask = m.sb("mask", [P, 2, TB, S]) if masked else None
        maskT = m.sb("maskT", [P, 2, TB, S]) if masked else None
        stats = m.sb("stats", [P, TB, 6])
        mv = m.sb("mv", [P, TB, 2])
        veps = m.sb("veps", [P, TB])
        rstd = m.sb("rstd", [P, TB])
        xn = m.sb("xn", [P, TB, D])
        xnT = m.sb("xnT", [P, KC, S])
        cT = m.sb("cT", [P, KC, S])
        full = {k: m.sb(f"{k}_full", [P, KC, S]) for k in "qk"}
        rest = {k: m.sb(f"{k}_rest", [P, KC, S]) for k in "qk"}
        parts = {k: m.sb(f"{k}_parts", [P, PARTS, KC, S], BF16) for k in "qk"}
        stack = {k: m.sb(f"{k}_stack", [STACK_M, 2, H, S], BF16) for k in "qk"}
        va = m.sb("va", [P, 2, TB, H, DA])
        junk = m.sb("junk", [P, 2, TB, S]) if masked else None
        maxima = m.sb("maxima", [P, TB, H])
        m_full = m.sb("m_full", [H, S])
        m_rest = m.sb("m_rest", [H, S])
        m_parts = m.sb("m_parts", [H, PARTS, S], BF16)
        masked_s = m.sb("masked_s", [P, 2, TB, S]) if masked else None
        probs = m.sb("probs", [P, 2, TB, S])
        rinv = m.sb("rinv", [P, TB, H])
        o_sb = m.sb("o_sb", [P, TB, D])
        oT = m.sb("oT", [P, KC, S])
        yb = m.sb("yb", [P, TB, D])

        ps_n = m.psum("ps_n", [P, 2, TB, S])
        ps_t = m.psum("ps_t", [P, 2, TB, S])
        ps_o = m.psum("ps_o", [P, TB, 512])
        ps_w = m.psum("ps_w", [P, 2, TB, S])

        weights_in = m.sem("weights_in")
        bias_scaled = m.sem("bias_scaled")
        ones_set = m.sem("ones_set")
        loaded = [m.sem("loaded0"), m.sem("loaded1")]
        maskT_in = [m.sem("maskT_in0"), m.sem("maskT_in1")]
        xres_in = [m.sem("xres_in0"), m.sem("xres_in1")]
        mask_scaled = Tally(m.sem("mask_scaled"), 1)
        maskT_scaled = Tally(m.sem("maskT_scaled"), 1)
        stored = Tally(m.sem("stored"), 16, 16)
        stats_done = Tally(m.sem("stats_done"), 1)
        mv_ready = Tally(m.sem("mv_ready"), 1)
        eps_added = Tally(m.sem("eps_added"), 1)
        rstd_ready = Tally(m.sem("rstd_ready"), 1)
        xn_ready = Tally(m.sem("xn_ready"), 1)
        filled = [Tally(m.sem("filled0"), 4), Tally(m.sem("filled1"), 4)]
        drained = [Tally(m.sem("drained0"), 4, 1), Tally(m.sem("drained1"), 4, 1)]
        first_part = {k: Tally(m.sem(f"{k}_first_part"), 1) for k in "qk"}
        part_step = {k: Tally(m.sem(f"{k}_part_step"), 2) for k in "qk"}
        parts_ready = {k: Tally(m.sem(f"{k}_parts_ready"), 1) for k in "qk"}
        parts_out = {k: Tally(m.sem(f"{k}_parts_out"), 16) for k in "qk"}
        stacked = Tally(m.sem("stacked"), 2 * 6 * 16)
        m_first = Tally(m.sem("m_first"), 1)
        m_step = Tally(m.sem("m_step"), 2)
        m_parts_ready = Tally(m.sem("m_parts_ready"), 1)
        m_out = Tally(m.sem("m_out"), 16)
        m_stacked = Tally(m.sem("m_stacked"), 16)
        raw_ready = Tally(m.sem("raw_ready"), H)
        maximum_ready = Tally(m.sem("maximum_ready"), H, 2)
        scores_ready = Tally(m.sem("scores_ready"), H)
        mask_added = Tally(m.sem("mask_added"), H, 2)
        probs_ready = Tally(m.sem("probs_ready"), H, 2)
        head_done = Tally(m.sem("head_done"), H, 2)
        rinv_ready = Tally(m.sem("rinv_ready"), 1)
        o_ready = Tally(m.sem("o_ready"), 1, 1)
        bias_added = Tally(m.sem("bias_added"), 1)
        sum_ready = Tally(m.sem("sum_ready"), 1)
        passed = m.sem("passed")
        ident = consts["ident"]
        minus_half = consts["minus_half"]
        gate = consts["gates"][:, gate_col:gate_col + 1]
        nweights = 4 + (4 if biased else 0)
        nload = 3 if masked else 2
        block = m.block()

        @block.sync
        def _(sp):
            for dst, k in ((wq, "wq"), (wk, "wk"), (wv, "wv"), (wo, "wo")) + (
                    ((bq, "bq"), (bk, "bk"), (bv, "bv")) if biased else ()):
                sp.dma_start(dst[:], w[k]).then_inc(weights_in, 16)
            if biased:
                sp.dma_start(bo[:], w["bo"].broadcast_to([P, D])).then_inc(weights_in, 16)

            def load(b, par):
                sp.dma_start(xin[:, par], rows(x_src, b)).then_inc(loaded[par], 16)
                sp.dma_start(cin[:, par], rows(ctx_dram, b)).then_inc(loaded[par], 16)
                if masked:
                    sp.dma_start(mask[:, par], rows(mask_drams[0], b)).then_inc(loaded[par], 16)

            def load_maskT(b, par):
                if masked:
                    sp.dma_start(maskT[:, par], rows(mask_drams[1], b)).then_inc(maskT_in[par], 16)

            def make_stack(b, par):
                for k in "kq":
                    parts_ready[k].wait(sp, b, 1)
                    sp.dma_start(bounce[k].rearrange("i (g p) n -> p i g n", p=P), parts[k][:]
                                 ).then_inc(parts_out[k].sem, 16)
                for k in "kq":
                    parts_out[k].wait(sp, b, 16)
                    heads = bounce[k].rearrange("i (h d) n -> i d h n", d=DH)
                    row = 0
                    if k == "q":
                        for part, times in Q_PARTS:
                            for _ in range(times):
                                sp.dma_start(stack[k][row:row + DH, par], heads[part]).then_inc(stacked.sem, 16)
                                row += DH
                    else:
                        for n in K_PARTS:
                            for part in range(n):
                                sp.dma_start(stack[k][row:row + DH, par], heads[part]).then_inc(stacked.sem, 16)
                                row += DH

            def stack_maxima(b, par):
                m_parts_ready.wait(sp, b, 1)
                sp.dma_start(bounce["m"].rearrange("i h n -> h i n"), m_parts[:]).then_inc(m_out.sem, 16)
                m_out.wait(sp, b, 16)
                sp.dma_start(stack["q"][STACK:STACK_M, par], bounce["m"]).then_inc(m_stacked.sem, 16)

            def store(b, par):
                sum_ready.wait_apart(sp, b, 1, passed)
                sp.dma_start(rows(x_dst, b), xres[:, par]).then_inc(stored.sem, 16)

            def turn(b, par, first=False, last=False, before_last=False):
                if not last:
                    if not first:
                        head_done.wait_apart(sp, b, 0, passed)
                        maximum_ready.wait_apart(sp, b, H, passed)
                    if not before_last:
                        load(b + 2, par)
                    load_maskT(b + 1, 1 - par)
                if not first:
                    stored.wait_apart(sp, b, -16, passed)
                sp.dma_start(xres[:, par], rows(x_src, b)).then_inc(xres_in[par], 16)
                if not first:
                    store(b - 1, 1 - par)
                if not last:
                    make_stack(b + 1, 1 - par)
                    stack_maxima(b + 1, 1 - par)

            load(0, 0)
            load_maskT(0, 0)
            load(1, 1)
            sp.sem_inc(stored.sem, 16)
            make_stack(0, 0)
            stack_maxima(0, 0)
            batches(sp, turn)
            store(B - 1, 1)
            stored.wait(sp, B - 1, 16)

        @block.gpsimd
        def _(pool):
            with pool.Fori(0, B) as b:
                mv_ready.wait_apart(pool, b, 1, passed)
                pool.tensor_scalar(veps[:], mv[:, :, 1], LN_EPS, None, ALU.add).then_inc(eps_added.sem, 1)
                eps_added.wait(pool, b, 1)
                pool.tensor_tensor(rstd[:], veps[:], minus_half[:, 0:TB], ALU.pow).then_inc(rstd_ready.sem, 1)

        @block.tensor
        def _(pe):
            pe.sem_inc(head_done.sem, 2)

            def transposes(dst, src):
                for k in range(KC):
                    for t in range(TB):
                        last = pe.transpose(dst[:, k, t * P:(t + 1) * P], src[:, t, k * P:(k + 1) * P], ident[:])
                return last

            def begin(u, bank, j):
                drained[bank].wait(pe, u, j)
                return ps_w[:, bank]

            def project(u, par, what):
                if what == "xnT":
                    xn_ready.wait(pe, u, 1)
                    transposes(begin(u, 1, 0), xn).then_inc(filled[1].sem, 1)
                if what == "cT":
                    pe.wait_ge(loaded[par], load_times(u, par, nload))
                    transposes(begin(u, 1, 1), cin[:, par]).then_inc(filled[1].sem, 1)
                if what in "qk":
                    weight, act, bank = (wq, xnT, 0) if what == "q" else (wk, cT, 1)
                    out = begin(u, bank, 2)
                    for g in range(KC):
                        for k in range(KC):
                            last = pe.matmul(out[:, g, :], weight[:, k, g * P:(g + 1) * P], act[:, k, :],
                                             start=(k == 0), stop=(k == KC - 1))
                    last.then_inc(filled[bank].sem, 1)
                if what == "v":
                    out = begin(u, 1, 3)
                    for t in range(TB):
                        if biased:
                            pe.matmul(out[:, t, :], ones_row[:], bv[:], start=True, stop=False)
                        for k in range(KC):
                            last = pe.matmul(out[:, t, :], cT[:, k, t * P:(t + 1) * P], wv[:, k, :],
                                             start=(k == 0 and not biased), stop=(k == KC - 1))
                    last.then_inc(filled[1].sem, 1)

            def turn_out(b, u):
                o_ready.wait(pe, b, 1)
                transposes(begin(u, 0, 0), o_sb).then_inc(filled[0].sem, 1)

            def project_out(u):
                out = begin(u, 0, 1)
                for t in range(TB):
                    for k in range(KC):
                        last = pe.matmul(out[:, t, :], oT[:, k, t * P:(t + 1) * P], wo[:, k, :],
                                         start=(k == 0), stop=(k == KC - 1))
                last.then_inc(filled[0].sem, 1)

            def skip(u, j):
                begin(u, 0, j)
                pe.sem_inc(filled[0].sem, 2)

            def raw_scores(u, par, h):
                if h == 0:
                    stacked.wait(pe, u, 2 * 6 * 16)
                maximum_ready.wait(pe, u, h - 1)
                for t in range(TB):
                    last = pe.matmul(ps_n[:, h % 2, t, :], stack["q"][0:STACK, par, h, t * P:(t + 1) * P],
                                     stack["k"][0:STACK, par, h, :], start=True, stop=True)
                last.then_inc(raw_ready.sem, 1)

            def turn_maxima(u):
                maximum_ready.wait(pe, u, H)
                out = begin(u, 0, 3)
                for t in range(TB):
                    last = pe.transpose(out[0:H, 0, t * P:(t + 1) * P], maxima[:, t, :], ident[:])
                last.then_inc(filled[0].sem, 1)

            def scores(b, par, h):
                if h == 0:
                    m_stacked.wait(pe, b, 16)
                (mask_added if masked else probs_ready).wait(pe, b, h - 1)
                for lb in range(TB):
                    last = pe.matmul(ps_t[:, h % 2, lb, :], stack["k"][:, par, h, lb * P:(lb + 1) * P],
                                     stack["q"][:, par, h, :], start=True, stop=True)
                last.then_inc(scores_ready.sem, 1)

            def weigh(b, par, h):
                probs_ready.wait(pe, b, h + 1)
                if h == 0:
                    o_ready.wait(pe, b, 0)
                for t in range(TB):
                    for lb in range(TB):
                        last = pe.matmul(ps_o[:, t, h * DA:(h + 1) * DA], probs[:, h % 2, lb, t * P:(t + 1) * P],
                                         va[:, par, lb, h, :], start=(lb == 0), stop=(lb == TB - 1))
                last.then_inc(head_done.sem, 1)

            def turn(b, par, first=False, last=False, before_last=False):
                if not last:
                    project(b + 1, 1 - par, "xnT")
                if not first:
                    turn_out(b - 1, b + 1)
                else:
                    skip(b + 1, 0)
                if not last:
                    project(b + 1, 1 - par, "cT")
                if not first:
                    project_out(b + 1)
                if not last:
                    project(b + 1, 1 - par, "k")
                    project(b + 1, 1 - par, "q")
                    project(b + 1, 1 - par, "v")
                scores(b, par, 0)
                done = 0
                for h in range(H):
                    if h < H - 1:
                        scores(b, par, h + 1)
                    if not last:
                        for _ in range(MAXIMA_AT.get(h, 0)):
                            raw_scores(b + 1, 1 - par, done)
                            done += 1
                    weigh(b, par, h)
                if not last:
                    turn_maxima(b + 1)

            pe.wait_ge(weights_in, 16 * nweights)
            pe.wait_ge(ones_set, 2)
            project(0, 0, "xnT")
            skip(0, 0)
            for what in ("cT", "k", "q", "v"):
                project(0, 0, what)
            for h in range(H):
                raw_scores(0, 0, h)
            turn_maxima(0)
            batches(pe, turn)
            skip(B, 2)
            turn_out(B - 1, B + 1)
            project_out(B + 1)

        @block.scalar
        def _(act):
            act.sem_inc(drained[0].sem, 1)
            act.sem_inc(drained[1].sem, 1)
            act.sem_inc(probs_ready.sem, 2)

            def end(ins, bank):
                ins.then_inc(drained[bank].sem, 1)

            def drain(u, par, what):
                if what == "xnT":
                    filled[1].wait(act, u, 1)
                    end(act.activation(xnT[:], ps_w[:, 1], ACT.Copy), 1)
                if what == "cT":
                    filled[1].wait(act, u, 2)
                    end(act.activation(cT[:], ps_w[:, 1], ACT.Copy), 1)
                if what in "qk":
                    bank, scale, bias = (0, score_scale, bqs) if what == "q" else (1, 1.0, bk)
                    filled[bank].wait(act, u, 3)
                    if biased:
                        for g in range(KC):
                            last = act.activation(full[what][:, g, :], ps_w[:, bank, g, :], ACT.Identity,
                                                  bias=bias[:, g:g + 1], scale=scale)
                    else:
                        last = act.activation(full[what][:], ps_w[:, bank], ACT.Copy, scale=scale)
                    end(last, bank)
                    drained[bank].wait(act, u, 3)
                    act.activation(parts[what][:, 0], full[what][:], ACT.Copy).then_inc(first_part[what].sem, 1)
                if what == "v":
                    filled[1].wait(act, u, 4)
                    end(act.activation(va[:, par, :, :, 0:DH], ps_w[:, 1].rearrange("p t (h d) -> p t h d", d=DH),
                                       ACT.Copy), 1)
                if what == "maxima":
                    filled[0].wait(act, u, 4)
                    end(act.activation(m_full[:], ps_w[0:H, 0, 0, :], ACT.Copy, scale=-1.0), 0)
                    drained[0].wait(act, u, 4)
                    act.activation(m_parts[:, 0, :], m_full[:], ACT.Copy).then_inc(m_first.sem, 1)

            def copy_oT(u):
                filled[0].wait(act, u, 1)
                end(act.activation(oT[:], ps_w[:, 0], ACT.Copy), 0)

            def exponent(b, par, h):
                if masked:
                    mask_added.wait(act, b, h + 1)
                else:
                    scores_ready.wait(act, b, h + 1)
                head_done.wait(act, b, h - 1)
                src = masked_s[:, h % 2] if masked else ps_t[:, h % 2]
                act.activation(probs[:, h % 2], src, ACT.Exp).then_inc(probs_ready.sem, 1)

            def turn(b, par, first=False, last=False, before_last=False):
                if not last:
                    drain(b + 1, 1 - par, "xnT")
                if not first:
                    copy_oT(b + 1)
                if not last:
                    for what in ("cT", "k", "q", "v"):
                        drain(b + 1, 1 - par, what)
                for h in range(H):
                    exponent(b, par, h)
                if not last:
                    drain(b + 1, 1 - par, "maxima")

            if biased:
                act.wait_ge(weights_in, 16 * nweights)
                act.activation(bqs[:], bq[:], ACT.Copy, scale=score_scale).then_inc(bias_scaled, 1)
                act.wait_ge(bias_scaled, 1)
            act.wait_ge(ones_set, 2)
            for what in ("xnT", "cT", "k", "q", "v", "maxima"):
                drain(0, 0, what)
            batches(act, turn)
            copy_oT(B + 1)

        @block.vector
        def _(dve):
            dve.sem_inc(maximum_ready.sem, 2)
            dve.sem_inc(mask_added.sem, 2)
            dve.sem_inc(o_ready.sem, 1)
            dve.memset(ones_row[:], 1.0)
            dve.memset(stack["k"][STACK:STACK_M], 1.0).then_inc(ones_set, 1)
            dve.memset(va[:], 1.0).then_inc(ones_set, 1)

            def statistics(b, par):
                dve.wait_ge(loaded[par], load_times(b, par, nload))
                for t in range(TB):
                    last = dve.bn_stats(stats[:, t, :], xin[:, par, t, :])
                last.then_inc(stats_done.sem, 1)
                stats_done.wait_apart(dve, b, 1, passed)
                for t in range(TB):
                    last = dve.bn_aggr(mv[:, t, :], stats[:, t, :])
                last.then_inc(mv_ready.sem, 1)
                if masked:
                    dve.tensor_scalar(mask[:, par], mask[:, par], -MASK_FACTOR, None,
                                      ALU.mult).then_inc(mask_scaled.sem, 1)

            def scale_maskT(b, par):
                if masked:
                    dve.wait_ge(maskT_in[par], load_times(b, par, 1))
                    dve.tensor_scalar(maskT[:, par], maskT[:, par], -MASK_FACTOR, None,
                                      ALU.mult).then_inc(maskT_scaled.sem, 1)

            def normalise(b, par):
                rstd_ready.wait(dve, b, 1)
                for t in range(TB):
                    last = dve.tensor_scalar(xn[:, t, :], xin[:, par, t, :], mv[:, t, 0:1], rstd[:, t:t + 1],
                                             ALU.subtract, ALU.mult)
                last.then_inc(xn_ready.sem, 1)

            def split(u, full_, rest_, part_of, first, steps, ready):
                first.wait(dve, u, 1)
                dve.tensor_tensor(rest_, full_, part_of(0), ALU.subtract).then_inc(steps.sem, 1)
                steps.wait(dve, u, 1)
                dve.tensor_copy(part_of(1), rest_).then_inc(steps.sem, 1)
                steps.wait(dve, u, 2)
                dve.tensor_tensor(part_of(2), rest_, part_of(1), ALU.subtract).then_inc(ready.sem, 1)

            def split_qk(u, k):
                split(u, full[k][:], rest[k][:], lambda i: parts[k][:, i], first_part[k], part_step[k],
                      parts_ready[k])

            def split_maxima(u):
                split(u, m_full[:], m_rest[:], lambda i: m_parts[:, i, :], m_first, m_step, m_parts_ready)

            def maximum(u, par, h):
                if masked:
                    if h == 0:
                        mask_scaled.wait(dve, u, 1)
                    raw_ready.wait_apart(dve, u, h + 1, passed)
                    for t in range(TB):
                        last = dve.tensor_tensor_reduce(junk[:, h % 2, t], ps_n[:, h % 2, t, :], mask[:, par, t, :], 1.0,
                                                        -3.0e38, ALU.add, ALU.max, maxima[:, t, h:h + 1])
                else:
                    raw_ready.wait(dve, u, h + 1)
                    last = dve.tensor_reduce(maxima[:, :, h:h + 1], ps_n[:, h % 2], AX.X, ALU.max)
                last.then_inc(maximum_ready.sem, 1)

            def add_mask(b, par, h):
                if not masked:
                    return
                if h == 0:
                    maskT_scaled.wait(dve, b, 1)
                probs_ready.wait(dve, b, h - 1)
                scores_ready.wait(dve, b, h + 1)
                dve.tensor_tensor(masked_s[:, h % 2], ps_t[:, h % 2], maskT[:, par],
                                  ALU.add).then_inc(mask_added.sem, 1)

            def divide(b):
                head_done.wait(dve, b, H)
                outs = ps_o[:, :, 0:H * DA].rearrange("p t (h d) -> p t h d", d=DA)
                dve.reciprocal(rinv[:], outs[:, :, :, DH]).then_inc(rinv_ready.sem, 1)
                rinv_ready.wait(dve, b, 1)
                dve.tensor_tensor(o_sb[:].rearrange("p t (h d) -> p t h d", d=DH), outs[:, :, :, 0:DH],
                                  rinv[:].unsqueeze(3).broadcast_to([P, TB, H, DH]), ALU.mult).then_inc(o_ready.sem, 1)

            def add_residual(b, par, u):
                filled[0].wait(dve, u, 2)
                dve.wait_ge(xres_in[par], load_times(b, par, 1))
                if biased:
                    dve.tensor_tensor(yb[:], ps_w[:, 0], bo[:].unsqueeze(1).broadcast_to([P, TB, D]),
                                      ALU.add).then_inc(bias_added.sem, 1)
                    bias_added.wait(dve, b, 1)
                src = yb[:] if biased else ps_w[:, 0]
                dve.scalar_tensor_tensor(xres[:, par], src, gate, xres[:, par], ALU.mult,
                                         ALU.add).then_inc(sum_ready.sem, 1)
                sum_ready.wait(dve, b, 1)
                dve.sem_inc(drained[0].sem, 1)

            def skip(u, j):
                filled[0].wait(dve, u, j + 2)
                dve.sem_inc(drained[0].sem, 2)

            def turn(b, par, first=False, last=False, before_last=False):
                if not first:
                    divide(b - 1)
                    add_residual(b - 1, 1 - par, b + 1)
                else:
                    skip(b + 1, 0)
                if not last:
                    split_qk(b + 1, "k")
                    split_qk(b + 1, "q")
                done = 0
                for h in range(H):
                    add_mask(b, par, h)
                    if not last:
                        for _ in range(MAXIMA_AT.get(h, 0)):
                            maximum(b + 1, 1 - par, done)
                            done += 1
                    if h == 3 and not last:
                        scale_maskT(b + 1, 1 - par)
                    if not last and not before_last:
                        if h == 3:
                            statistics(b + 2, par)
                        if h == 4:
                            normalise(b + 2, par)
                if not last:
                    split_maxima(b + 1)

            if biased:
                dve.wait_ge(weights_in, 16 * nweights)
            dve.wait_ge(ones_set, 2)
            statistics(0, 0)
            normalise(0, 0)
            scale_maskT(0, 0)
            skip(0, 0)
            split_qk(0, "k")
            split_qk(0, "q")
            filled[1].wait(dve, 0, 1)
            statistics(1, 1)
            normalise(1, 1)
            for h in range(H):
                maximum(0, 0, h)
            split_maxima(0)
            batches(dve, turn)
            skip(B, 2)
            divide(B - 1)
            add_residual(B - 1, 1, B + 1)


NT = B * TB
MAGIC = 1.5 * 2.0 ** 23


def tile_rows(dram, n):
    return dram.rearrange("b (t p) d -> (b t) p d", p=P)[n]


def tiles(engine, turn, count=NT):
    turn(0, 0, first=True)
    with engine.Fori(0, count // 2 - 1) as pair:
        turn(2 * pair + 1, 1)
        turn(2 * pair + 2, 0)
    turn(count - 1, 1, last=True)


def tile_times(n, par, per):
    return (n - par) * (8 * per) + 16 * per


class Norm:

    def __init__(self, m, consts):
        self.stats = m.sb("ln_stats", [P, 6])
        self.mv = m.sb("ln_mv", [P, 2])
        self.veps = m.sb("ln_veps", [P, 1])
        self.rstd = m.sb("ln_rstd", [P, 1])
        self.minus_half = consts["minus_half"]
        self.stats_done = Tally(m.sem("ln_stats_done"), 1)
        self.mv_ready = Tally(m.sem("ln_mv_ready"), 1)
        self.eps_added = Tally(m.sem("ln_eps_added"), 1)
        self.rstd_ready = Tally(m.sem("ln_rstd_ready"), 1)
        self.passed = m.sem("ln_passed")

    def statistics(self, dve, x, n):
        dve.bn_stats(self.stats[:], x).then_inc(self.stats_done.sem, 1)
        self.stats_done.wait_apart(dve, n, 1, self.passed)
        dve.bn_aggr(self.mv[:], self.stats[:]).then_inc(self.mv_ready.sem, 1)

    def on_pool(self, pool, n):
        self.mv_ready.wait_apart(pool, n, 1, self.passed)
        pool.tensor_scalar(self.veps[:], self.mv[:, 1:2], LN_EPS, None, ALU.add).then_inc(self.eps_added.sem, 1)
        self.eps_added.wait(pool, n, 1)
        pool.tensor_tensor(self.rstd[:], self.veps[:], self.minus_half[:, 0:1],
                           ALU.pow).then_inc(self.rstd_ready.sem, 1)

    def apply(self, dve, out, x, n):
        self.rstd_ready.wait(dve, n, 1)
        return dve.tensor_scalar(out, x, self.mv[:, 0:1], self.rstd[:], ALU.subtract, ALU.mult)


F0 = 1024
FC0 = F0 // P
HALF = 512


def quantised_ffn_phase(nc, name, x_src, x_dst, consts, w, gate_col):
    with ExitStack() as ctx:
        m = Space(nc, ctx, name)
        wraw = m.sb("wraw", [P, 3, KC * F0])
        wround = m.sb("wround", [P, KC * F0])
        wt = m.sb("wt", [P, 3, KC * F0], BF16)
        wsum = m.sb("wsum", [P, 3])
        wmean = m.sb("wmean", [P, 3])
        winv = m.sb("winv", [P, 3])
        wfac = m.sb("wfac", [P, 3])
        ones = m.sb("ones", [P, P])
        identb = m.sb("identb", [P, P], BF16)
        xin = m.sb("xin", [P, 2, D])
        xres = m.sb("xres", [P, 2, D])
        xn = m.sb("xn", [P, D])
        amax = m.sb("amax", [P, 2, 1])
        clipped = m.sb("clipped", [P, 2, 1])
        inv = m.sb("inv", [P, 2, 1])
        sc = m.sb("sc", [P, 2, 1])
        fac = m.sb("fac", [P, 2, 2])
        qa = m.sb("qa", [P, D])
        qb = m.sb("qb", [P, D])
        xq = m.sb("xq", [P, D], BF16)
        xqT = m.sb("xqT", [P, KC, P], BF16)
        silu = m.sb("silu", [P, 2, HALF])
        h = m.sb("h", [P, F0])
        ha = m.sb("ha", [P, F0])
        hq = m.sb("hq", [P, F0], BF16)
        hqT = m.sb("hqT", [P, FC0, P], BF16)
        hmax = m.sb("hmax", [P, 1])
        hclip = m.sb("hclip", [P, 1])
        hinv = m.sb("hinv", [P, 1])
        hsc = m.sb("hsc", [P, 1])
        hfac = m.sb("hfac", [P, 2])
        norm = Norm(m, consts)

        ps_g = m.psum("ps_g", [P, 2, HALF])
        ps_u = m.psum("ps_u", [P, 2, HALF])
        ps_x = m.psum("ps_x", [P, 2 * HALF], BF16)
        ps_h = m.psum("ps_h", [P, FC0, P], BF16)
        ps_y = m.psum("ps_y", [P, HALF])
        ps_m = m.psum("ps_m", [P, HALF])

        weights_in = m.sem("weights_in")
        sums_ready = m.sem("sums_ready")
        mean_ready = m.sem("mean_ready")
        wstep = m.sem("wstep")
        weights_ready = m.sem("weights_ready")
        loaded = [m.sem("loaded0"), m.sem("loaded1")]
        xres_in = [m.sem("xres_in0"), m.sem("xres_in1")]
        stored = Tally(m.sem("stored"), 16, 16)
        xstep = Tally(m.sem("xstep"), 7)
        xq_ready = Tally(m.sem("xq_ready"), 1)
        xqT_ready = Tally(m.sem("xqT_ready"), 1)
        xqT_copied = Tally(m.sem("xqT_copied"), 1)
        fac_ready = Tally(m.sem("fac_ready"), 1)
        gate_ready = Tally(m.sem("gate_ready"), 2)
        up_ready = Tally(m.sem("up_ready"), 2)
        silu_ready = Tally(m.sem("silu_ready"), 2, 2)
        h_ready = Tally(m.sem("h_ready"), 2, 2)
        hstep = Tally(m.sem("hstep"), 6)
        hq_ready = Tally(m.sem("hq_ready"), 1, 1)
        hqT_ready = Tally(m.sem("hqT_ready"), 1, 1)
        hqT_copied = Tally(m.sem("hqT_copied"), 1)
        y_ready = Tally(m.sem("y_ready"), 1)
        sum_ready = Tally(m.sem("sum_ready"), 1, 1)
        identb_ready = m.sem("identb_ready")
        gate = consts["gates"][:, gate_col:gate_col + 1]
        block = m.block()

        @block.sync
        def _(sp):
            for i, k in enumerate(("gate", "up", "down")):
                sp.dma_start(wraw[:, i], w[k].rearrange("p k n -> p (k n)")).then_inc(weights_in, 16)

            def turn(n, par, first=False, last=False):
                if first:
                    sp.dma_start(xin[:, 0], tile_rows(x_src, 0)).then_inc(loaded[0], 16)
                if not last:
                    if not first:
                        xq_ready.wait(sp, n - 1, 1)
                    sp.dma_start(xin[:, 1 - par], tile_rows(x_src, n + 1)).then_inc(loaded[1 - par], 16)
                if not first:
                    stored.wait(sp, n, -16)
                sp.dma_start(xres[:, par], tile_rows(x_src, n)).then_inc(xres_in[par], 16)
                if not first:
                    store(n - 1, 1 - par)

            def store(n, par):
                sum_ready.wait(sp, n, 1)
                sp.dma_start(tile_rows(x_dst, n), xres[:, par]).then_inc(stored.sem, 16)

            sp.sem_inc(stored.sem, 16)
            tiles(sp, turn)
            store(NT - 1, 1)
            stored.wait(sp, NT - 1, 16)

        @block.gpsimd
        def _(pool):
            with pool.Fori(0, NT) as n:
                norm.on_pool(pool, n)

        @block.tensor
        def _(pe):
            pe.sem_inc(hqT_ready.sem, 1)
            pe.wait_ge(sums_ready, 1)
            pe.matmul(ps_m[:, 0:3], ones[:], wsum[:], start=True, stop=True).then_inc(mean_ready, 1)
            pe.wait_ge(weights_ready, 1)
            pe.wait_ge(identb_ready, 1)

            def turn_x(n):
                xq_ready.wait(pe, n, 1)
                for k in range(KC):
                    last = pe.transpose(ps_x[:, k * P:(k + 1) * P], xq[:, k * P:(k + 1) * P], identb[:])
                last.then_inc(xqT_ready.sem, 1)

            def gate_up(n):
                xqT_copied.wait(pe, n, 1)
                h_ready.wait(pe, n, 0)
                for c in range(2):
                    for i, bank, ready in ((0, ps_g, gate_ready), (1, ps_u, up_ready)):
                        for k in range(KC):
                            last = pe.matmul(bank[:, c, :], xqT[:, k, :],
                                             wt[:, i, k * F0 + c * HALF:k * F0 + (c + 1) * HALF],
                                             start=(k == 0), stop=(k == KC - 1))
                        last.then_inc(ready.sem, 1)

            def down(n):
                hq_ready.wait(pe, n, 1)
                for f in range(FC0):
                    last = pe.transpose(ps_h[:, f, :], hq[:, f * P:(f + 1) * P], identb[:])
                last.then_inc(hqT_ready.sem, 1)
                hqT_copied.wait(pe, n, 1)
                sum_ready.wait(pe, n, 0)
                for f in range(FC0):
                    last = pe.matmul(ps_y[:, 0:D], hqT[:, f, :], wt[:, 2, f * D:(f + 1) * D],
                                     start=(f == 0), stop=(f == FC0 - 1))
                last.then_inc(y_ready.sem, 1)

            def turn(n, par, first=False, last=False):
                if first:
                    turn_x(0)
                gate_up(n)
                if not last:
                    turn_x(n + 1)
                if not first:
                    down(n - 1)

            tiles(pe, turn)
            down(NT - 1)

        @block.scalar
        def _(act):
            act.sem_inc(silu_ready.sem, 2)
            act.activation(identb[:], consts["ident"][:], ACT.Copy).then_inc(identb_ready, 1)

            def copy_x(n):
                xqT_ready.wait(act, n, 1)
                act.activation(xqT[:].rearrange("p k n -> p (k n)"), ps_x[:, 0:D], ACT.Copy).then_inc(xqT_copied.sem, 1)

            def silus(n, par):
                fac_ready.wait(act, n, 1)
                for c in range(2):
                    gate_ready.wait(act, n, c + 1)
                    h_ready.wait(act, n, c + 1 - 2)
                    act.activation(silu[:, c], ps_g[:, c], ACT.Silu, scale=fac[:, par, 0:1]).then_inc(silu_ready.sem, 1)

            def copy_h(n):
                hqT_ready.wait(act, n, 1)
                act.activation(hqT[:], ps_h[:], ACT.Copy).then_inc(hqT_copied.sem, 1)

            def turn(n, par, first=False, last=False):
                if first:
                    copy_x(0)
                silus(n, par)
                if not last:
                    copy_x(n + 1)
                if not first:
                    copy_h(n - 1)

            tiles(act, turn)
            copy_h(NT - 1)

        @block.vector
        def _(dve):
            dve.sem_inc(h_ready.sem, 2)
            dve.sem_inc(hq_ready.sem, 1)
            dve.sem_inc(sum_ready.sem, 1)
            done = [0]

            def step(ins):
                done[0] += 1
                ins.then_inc(wstep, 1)
                dve.wait_ge(wstep, done[0])

            step(dve.memset(ones[:], 1.0))
            dve.wait_ge(weights_in, 48)
            for i in range(3):
                last = dve.tensor_reduce(wsum[:, i:i + 1], wraw[:, i], AX.X, ALU.add, apply_absolute_value=True)
            last.then_inc(sums_ready, 1)
            dve.wait_ge(mean_ready, 1)
            step(dve.tensor_scalar(wmean[:], ps_m[:, 0:3], 1.0 / (D * F0), 1e-5, ALU.mult, ALU.max))
            step(dve.reciprocal(winv[:], wmean[:]))
            step(dve.tensor_scalar(wfac[:], wmean[:], 1.0 / 127.0, None, ALU.mult))
            step(dve.tensor_scalar(wfac[:, 2:3], wfac[:, 2:3], gate, None, ALU.mult))
            for i in range(3):
                step(dve.tensor_scalar(wround[:], wraw[:, i], winv[:, i:i + 1], 1.0, ALU.mult, ALU.min))
                step(dve.tensor_scalar(wround[:], wround[:], -1.0, MAGIC, ALU.max, ALU.add))
                step(dve.tensor_scalar(wt[:, i], wround[:], MAGIC, None, ALU.subtract))
            dve.sem_inc(weights_ready, 1)

            def prepare(n, par):
                dve.wait_ge(loaded[par], tile_times(n, par, 1))
                norm.statistics(dve, xin[:, par], n)
                norm.apply(dve, xn[:], xin[:, par], n).then_inc(xstep.sem, 1)
                xstep.wait(dve, n, 1)
                dve.tensor_reduce(amax[:, par], xn[:], AX.X, ALU.max, apply_absolute_value=True).then_inc(xstep.sem, 1)
                xstep.wait(dve, n, 2)
                dve.tensor_scalar(clipped[:, par], amax[:, par], 1e-5, None, ALU.max).then_inc(xstep.sem, 1)
                xstep.wait(dve, n, 3)
                dve.reciprocal(inv[:, par], clipped[:, par]).then_inc(xstep.sem, 1)
                dve.tensor_scalar(fac[:, par], wfac[:, 0:2], clipped[:, par], None, ALU.mult).then_inc(fac_ready.sem, 1)
                xstep.wait(dve, n, 4)
                dve.tensor_scalar(sc[:, par], inv[:, par], 127.0, None, ALU.mult).then_inc(xstep.sem, 1)
                xstep.wait(dve, n, 5)
                dve.tensor_scalar(qa[:], xn[:], sc[:, par], 127.0, ALU.mult, ALU.min).then_inc(xstep.sem, 1)
                xstep.wait(dve, n, 6)
                dve.tensor_scalar(qb[:], qa[:], -128.0, MAGIC, ALU.max, ALU.add).then_inc(xstep.sem, 1)
                xstep.wait(dve, n, 7)
                dve.tensor_scalar(xq[:], qb[:], MAGIC, None, ALU.subtract).then_inc(xq_ready.sem, 1)

            def hidden(n, par):
                for c in range(2):
                    up_ready.wait(dve, n, c + 1)
                    silu_ready.wait(dve, n, c + 1)
                    dve.scalar_tensor_tensor(h[:, c * HALF:(c + 1) * HALF], ps_u[:, c], fac[:, par, 1:2], silu[:, c],
                                             ALU.mult, ALU.mult).then_inc(h_ready.sem, 1)
                h_ready.wait(dve, n, 2)
                dve.tensor_reduce(hmax[:], h[:], AX.X, ALU.max, apply_absolute_value=True).then_inc(hstep.sem, 1)
                hstep.wait(dve, n, 1)
                dve.tensor_scalar(hclip[:], hmax[:], 1e-5, None, ALU.max).then_inc(hstep.sem, 1)
                hstep.wait(dve, n, 2)
                dve.reciprocal(hinv[:], hclip[:]).then_inc(hstep.sem, 1)
                dve.tensor_scalar(hfac[:, par:par + 1], wfac[:, 2:3], hclip[:], None, ALU.mult)
                hstep.wait(dve, n, 3)
                dve.tensor_scalar(hsc[:], hinv[:], 127.0, None, ALU.mult).then_inc(hstep.sem, 1)
                hstep.wait(dve, n, 4)
                dve.tensor_scalar(ha[:], h[:], hsc[:], 127.0, ALU.mult, ALU.min).then_inc(hstep.sem, 1)
                hstep.wait(dve, n, 5)
                dve.tensor_scalar(ha[:], ha[:], -128.0, MAGIC, ALU.max, ALU.add).then_inc(hstep.sem, 1)
                hstep.wait(dve, n, 6)
                hqT_ready.wait(dve, n, 0)
                dve.tensor_scalar(hq[:], ha[:], MAGIC, None, ALU.subtract).then_inc(hq_ready.sem, 1)

            def add_residual(n, par):
                y_ready.wait(dve, n, 1)
                dve.wait_ge(xres_in[par], tile_times(n, par, 1))
                dve.scalar_tensor_tensor(xres[:, par], ps_y[:, 0:D], hfac[:, par:par + 1], xres[:, par], ALU.mult,
                                         ALU.add).then_inc(sum_ready.sem, 1)

            def turn(n, par, first=False, last=False):
                if first:
                    prepare(0, 0)
                if not last:
                    xqT_ready.wait(dve, n, 1)
                    prepare(n + 1, 1 - par)
                hidden(n, par)
                if not first:
                    add_residual(n - 1, 1 - par)

            tiles(dve, turn)
            add_residual(NT - 1, 1)


FG_ROW = 32
GN_EPS = 1e-5
NORMALISER_EPS = 1e-6
LOWEST = -3.0e38


def mlstm_phase(nc, name, x_src, x_dst, ctx_dram, consts, w, gate_col, nh, plus_one):
    dh = D // nh
    kh = P // dh
    W = S + P
    G = TB * nh
    slots = 8 // nh
    qk_scale = 1.0 / float(np.sqrt(dh))
    with ExitStack() as ctx:
        m = Space(nc, ctx, name)
        wg = m.sb("wg", [P, 6, 64])
        ib = m.sb("ib", [nh, 1])
        fb = m.sb("fb", [nh, 1])
        ow = m.sb("ow", [P, D])
        owg = m.sb("owg", [P, D])
        sel = m.sb("sel", [nh, nh * P])
        identb = m.sb("identb", [P, P], BF16)
        lower = m.sb("lower", [P, P])
        lowerb = m.sb("lowerb", [P, P], BF16)
        ones = m.sb("ones", [nh, S])
        xin = m.sb("xin", [P, 2, TB, D])
        cin = m.sb("cin", [P, 2, TB, D])
        xres = m.sb("xres", [P, 2, TB, D])
        stats = m.sb("stats", [P, TB, 6])
        mv = m.sb("mv", [P, TB, 2])
        veps = m.sb("veps", [P, TB])
        rstd = m.sb("rstd", [P, TB])
        xn = m.sb("xn", [P, TB, D])
        xnT = m.sb("xnT", [P, 2, KC, S])
        cT = m.sb("cT", [P, 2, KC, S])
        va = m.sb("va", [P, 2, TB, nh, dh + 1])
        igr = m.sb("igr", [nh, S])
        fgr = m.sb("fgr", [nh, S])
        z = m.sb("z", [nh, S])
        zabs = m.sb("zabs", [nh, S])
        zmin = m.sb("zmin", [nh, S])
        ex = m.sb("ex", [nh, S])
        lg = m.sb("lg", [nh, S])
        logf = m.sb("logf", [nh, S])
        cs = m.sb("cs", [nh, S])
        a = m.sb("a", [nh, S])
        mx = m.sb("mx", [nh, S])
        mlog = m.sb("mlog", [nh, S])
        negm = m.sb("negm", [nh, 2, S])
        e = m.sb("e", [nh, S])
        aT = m.sb("aT", [P, 2, 2, TB, nh])
        decay = m.sb("decay", [P, 2, W])
        c = m.sb("c", [P, 2, W])
        den = m.sb("den", [P, TB, nh])
        rden = m.sb("rden", [P, TB, nh])
        hn = m.sb("hn", [P, TB, nh, dh])
        sq = m.sb("sq", [P, TB, nh, dh])
        msum = m.sb("msum", [P, G])
        mean = m.sb("mean", [P, G])
        vsum = m.sb("vsum", [P, G])
        gveps = m.sb("gveps", [P, G])
        grstd = m.sb("grstd", [P, G])

        ps_q = m.psum("ps_q", [P, 2, 512])
        ps_m = m.psum("ps_m", [P, 2, 512])
        ps_o = m.psum("ps_o", [P, TB, 512])
        ps_w = m.psum("ps_w", [P, 2, TB, S])

        weights_in = m.sem("weights_in")
        wstep = m.sem("wstep")
        constants_ready = m.sem("constants_ready")
        loaded = [m.sem("loaded0"), m.sem("loaded1")]
        xres_in = [m.sem("xres_in0"), m.sem("xres_in1")]
        stored = Tally(m.sem("stored"), 16, 16)
        stats_done = Tally(m.sem("stats_done"), 1)
        mv_ready = Tally(m.sem("mv_ready"), 1)
        eps_added = Tally(m.sem("eps_added"), 1)
        rstd_ready = Tally(m.sem("rstd_ready"), 1)
        xn_ready = Tally(m.sem("xn_ready"), 1)
        va_ready = Tally(m.sem("va_ready"), 1)
        work_filled = Tally(m.sem("work_filled"), 4)
        act_drained = Tally(m.sem("act_drained"), 3)
        z_ready = Tally(m.sem("z_ready"), 1)
        ex_ready = Tally(m.sem("ex_ready"), 1)
        lg_ready = Tally(m.sem("lg_ready"), 1)
        gstep = Tally(m.sem("gstep"), 6)
        mlog_ready = Tally(m.sem("mlog_ready"), 1)
        e_ready = Tally(m.sem("e_ready"), 1)
        aT_ready = Tally(m.sem("aT_ready"), 1, 1)
        scores_ready = Tally(m.sem("scores_ready"), nh)
        m_ready = Tally(m.sem("m_ready"), nh)
        decay_ready = Tally(m.sem("decay_ready"), nh, 2)
        c_ready = Tally(m.sem("c_ready"), nh, 2)
        head_done = Tally(m.sem("head_done"), nh, 2)
        estep = Tally(m.sem("estep"), 10)
        out_read = Tally(m.sem("out_read"), 1, 1)
        vsum_ready = Tally(m.sem("vsum_ready"), 1)
        geps_added = Tally(m.sem("geps_added"), 1)
        grstd_ready = Tally(m.sem("grstd_ready"), 1)
        sum_ready = Tally(m.sem("sum_ready"), 1)
        passed = m.sem("passed")
        ident = consts["ident"]
        minus_half = consts["minus_half"]
        gate = consts["gates"][:, gate_col:gate_col + 1]
        block = m.block()

        @block.sync
        def _(sp):
            sp.dma_start(wg[:], w["gates"]).then_inc(weights_in, 16)
            sp.dma_start(ib[:], w["ib"]).then_inc(weights_in, 16)
            sp.dma_start(fb[:], w["fb"]).then_inc(weights_in, 16)
            sp.dma_start(ow[:], w["ow"].broadcast_to([P, D])).then_inc(weights_in, 16)
            sp.dma_start(sel[:], w["sel"]).then_inc(weights_in, 16)
            sp.dma_start(lower[:], w["lower"]).then_inc(weights_in, 16)

            def load(b, par):
                sp.dma_start(xin[:, par], rows(x_src, b)).then_inc(loaded[par], 16)
                sp.dma_start(cin[:, par], rows(ctx_dram, b)).then_inc(loaded[par], 16)

            def store(b, par):
                sum_ready.wait(sp, b, 1)
                sp.dma_start(rows(x_dst, b), xres[:, par]).then_inc(stored.sem, 16)

            def turn(b, par, first=False, last=False, before_last=False):
                if first:
                    load(0, 0)
                if not last:
                    head_done.wait(sp, b, 0)
                    load(b + 1, 1 - par)
                if not first:
                    stored.wait(sp, b, -16)
                sp.dma_start(xres[:, par], rows(x_src, b)).then_inc(xres_in[par], 16)
                if not first:
                    store(b - 1, 1 - par)

            sp.sem_inc(stored.sem, 16)
            batches(sp, turn)
            store(B - 1, 1)
            stored.wait(sp, B - 1, 16)

        @block.gpsimd
        def _(pool):
            def layer(b):
                mv_ready.wait_apart(pool, b, 1, passed)
                pool.tensor_scalar(veps[:], mv[:, :, 1], LN_EPS, None, ALU.add).then_inc(eps_added.sem, 1)
                eps_added.wait(pool, b, 1)
                pool.tensor_tensor(rstd[:], veps[:], minus_half[:, 0:TB], ALU.pow).then_inc(rstd_ready.sem, 1)

            def group(b):
                vsum_ready.wait_apart(pool, b, 1, passed)
                pool.tensor_scalar(gveps[:], vsum[:], 1.0 / dh, GN_EPS, ALU.mult,
                                   ALU.add).then_inc(geps_added.sem, 1)
                geps_added.wait(pool, b, 1)
                pool.tensor_tensor(grstd[:], gveps[:], minus_half[:, 0:G], ALU.pow).then_inc(grstd_ready.sem, 1)

            layer(0)
            layer(1)
            with pool.Fori(0, B - 2) as b:
                layer(b + 2)
                group(b)
            group(B - 2)
            group(B - 1)

        @block.tensor
        def _(pe):
            pe.sem_inc(head_done.sem, 2)
            pe.wait_ge(weights_in, 96)
            pe.wait_ge(constants_ready, 1)

            def transposes(dst, src):
                for k in range(KC):
                    for t in range(TB):
                        last = pe.transpose(dst[:, k, t * P:(t + 1) * P], src[:, t, k * P:(k + 1) * P], ident[:])
                return last

            def prepare(b, par, j):
                if j == 1:
                    xn_ready.wait(pe, b, 1)
                    act_drained.wait(pe, b, 0)
                    transposes(ps_w[:, 0], xn).then_inc(work_filled.sem, 1)
                if j == 2:
                    pe.wait_ge(loaded[par], load_times(b, par, 2))
                    aT_ready.wait(pe, b, 0)
                    transposes(ps_w[:, 1], cin[:, par]).then_inc(work_filled.sem, 1)
                if j == 3:
                    act_drained.wait(pe, b, 2)
                    for k in range(6):
                        src = xnT[:, par, k, :] if k < KC else cT[:, par, k % KC, :]
                        last = pe.matmul(ps_w[0:64, 0, 0, :], wg[:, k, :], src, start=(k == 0), stop=(k == 5))
                    last.then_inc(work_filled.sem, 1)
                if j == 6:
                    e_ready.wait_apart(pe, b, 1, passed)
                    for i, src in enumerate((a, e)):
                        for t in range(TB):
                            at = (i * TB + t) * nh
                            last = pe.transpose(ps_w[:, 1, 0, at:at + nh], src[:, t * P:(t + 1) * P],
                                                ident[0:nh, 0:nh])
                    last.then_inc(work_filled.sem, 1)

            def scores(b, par, h):
                if h == 0:
                    mlog_ready.wait(pe, b, 1)
                k, r = h // kh, dh * (h % kh)
                c_ready.wait(pe, b, h - 1)
                pe.matmul(ps_q[:, h % 2, 0:S], cT[r:r + dh, par, k, 0:P], xnT[r:r + dh, par, k, :],
                          start=True, stop=True)
                pe.matmul(ps_q[:, h % 2, S:W], cT[r:r + dh, par, k, P:S], xnT[r:r + dh, par, k, P:S],
                          start=True, stop=True).then_inc(scores_ready.sem, 1)
                decay_ready.wait(pe, b, h - 1)
                row = sel[:, h * P:(h + 1) * P]
                pe.matmul(ps_m[:, h % 2, 0:S], row, negm[:, par, :], start=True, stop=False, skip_group_check=True)
                pe.matmul(ps_m[:, h % 2, S:W], row, negm[:, par, P:S], start=False, stop=False,
                          skip_group_check=True)
                for at in (0, S):
                    last = pe.matmul(ps_m[:, h % 2, at:at + P], identb[:], lowerb[:], start=False, stop=True,
                                     skip_group_check=True)
                last.then_inc(m_ready.sem, 1)

            def weigh(b, par, h):
                c_ready.wait(pe, b, h + 1)
                if h == 0:
                    out_read.wait(pe, b, 0)
                    va_ready.wait(pe, b, 1)
                cols = slice(h * (dh + 1), (h + 1) * (dh + 1))
                pe.matmul(ps_o[:, 0, cols], c[:, h % 2, 0:P], va[:, par, 0, h, :], start=True, stop=True)
                pe.matmul(ps_o[:, 1, cols], c[:, h % 2, P:S], va[:, par, 0, h, :], start=True, stop=False)
                pe.matmul(ps_o[:, 1, cols], c[:, h % 2, S:W], va[:, par, 1, h, :], start=False,
                          stop=True).then_inc(head_done.sem, 1)

            def turn(b, par, first=False, last=False, before_last=False):
                for h in range(nh):
                    if h < nh - 1:
                        scores(b, par, h + 1)
                    if h:
                        weigh(b, par, h - 1)
                    if not last:
                        for j in range(h * slots, (h + 1) * slots):
                            prepare(b + 1, 1 - par, j)
                if not last:
                    scores(b + 1, 1 - par, 0)
                weigh(b, par, nh - 1)

            for j in range(8):
                prepare(0, 0, j)
            scores(0, 0, 0)
            batches(pe, turn)

        @block.scalar
        def _(act):
            act.sem_inc(decay_ready.sem, 2)
            act.wait_ge(weights_in, 96)
            act.activation(identb[:], ident[:], ACT.Copy)
            act.activation(lowerb[:], lower[:], ACT.Copy).then_inc(constants_ready, 1)

            def prepare(b, par, j):
                if j == 1 or j == 2:
                    work_filled.wait(act, b, j)
                    dst = xnT if j == 1 else cT
                    act.activation(dst[:, par], ps_w[:, j - 1], ACT.Copy).then_inc(act_drained.sem, 1)
                if j == 3:
                    work_filled.wait(act, b, 3)
                    act.activation(igr[:], ps_w[0:nh, 0, 0, :], ACT.Copy)
                    act.activation(fgr[:], ps_w[FG_ROW:FG_ROW + nh, 0, 0, :], ACT.Copy).then_inc(act_drained.sem, 1)
                if j == 4:
                    z_ready.wait(act, b, 1)
                    act.activation(ex[:], zabs[:], ACT.Exp).then_inc(ex_ready.sem, 1)
                    ex_ready.wait(act, b, 1)
                    act.activation(lg[:], ex[:], ACT.Ln, bias=1.0).then_inc(lg_ready.sem, 1)
                if j == 5:
                    mlog_ready.wait(act, b, 1)
                    act.activation(e[:], mlog[:], ACT.Exp, scale=-1.0).then_inc(e_ready.sem, 1)

            def decays(b, par, h):
                m_ready.wait(act, b, h + 1)
                if h == 0:
                    aT_ready.wait(act, b, 1)
                c_ready.wait(act, b, h - 1)
                act.activation(decay[:, h % 2, 0:S], ps_m[:, h % 2, 0:S], ACT.Exp, bias=aT[:, par, 0, 0, h:h + 1])
                act.activation(decay[:, h % 2, S:W], ps_m[:, h % 2, S:W], ACT.Exp,
                               bias=aT[:, par, 0, 1, h:h + 1]).then_inc(decay_ready.sem, 1)

            def turn(b, par, first=False, last=False, before_last=False):
                for h in range(nh):
                    decays(b, par, h)
                    if not last:
                        for j in range(h * slots, (h + 1) * slots):
                            prepare(b + 1, 1 - par, j)

            for j in range(8):
                prepare(0, 0, j)
            batches(act, turn)

        @block.vector
        def _(dve):
            dve.sem_inc(c_ready.sem, 2)
            dve.sem_inc(out_read.sem, 1)
            dve.sem_inc(aT_ready.sem, 1)
            dve.memset(ones[:], 1.0)
            dve.memset(va[:], 1.0).then_inc(wstep, 1)
            dve.wait_ge(weights_in, 96)
            dve.wait_ge(wstep, 1)
            dve.tensor_scalar(owg[:], ow[:], 1.0 if plus_one else 0.0, gate, ALU.add,
                              ALU.mult).then_inc(wstep, 1)
            dve.wait_ge(wstep, 2)

            def prepare(b, par, j):
                if j == 0:
                    dve.wait_ge(loaded[par], load_times(b, par, 2))
                    for t in range(TB):
                        last = dve.bn_stats(stats[:, t, :], xin[:, par, t, :])
                    last.then_inc(stats_done.sem, 1)
                    stats_done.wait_apart(dve, b, 1, passed)
                    for t in range(TB):
                        last = dve.bn_aggr(mv[:, t, :], stats[:, t, :])
                    last.then_inc(mv_ready.sem, 1)
                    dve.tensor_copy(va[:, par, :, :, 0:dh],
                                    cin[:, par].rearrange("p t (h d) -> p t h d", d=dh)).then_inc(va_ready.sem, 1)
                if j == 1:
                    rstd_ready.wait(dve, b, 1)
                    for t in range(TB):
                        last = dve.tensor_scalar(xn[:, t, :], xin[:, par, t, :], mv[:, t, 0:1], rstd[:, t:t + 1],
                                                 ALU.subtract, ALU.mult)
                    last.then_inc(xn_ready.sem, 1)
                if j == 3:
                    act_drained.wait(dve, b, 3)
                    dve.tensor_scalar(z[:], fgr[:], fb[:], None, ALU.add).then_inc(gstep.sem, 1)
                    dve.tensor_scalar(zmin[:], fgr[:], fb[:], 0.0, ALU.add, ALU.min).then_inc(gstep.sem, 1)
                    gstep.wait(dve, b, 2)
                    dve.scalar_tensor_tensor(zabs[:], zmin[:], 2.0, z[:], ALU.mult,
                                             ALU.subtract).then_inc(z_ready.sem, 1)
                if j == 4:
                    lg_ready.wait(dve, b, 1)
                    dve.tensor_tensor(logf[:], zmin[:], lg[:], ALU.subtract).then_inc(gstep.sem, 1)
                    gstep.wait(dve, b, 3)
                    dve.tensor_tensor_scan(cs[:], ones[:], logf[:], 0.0, ALU.mult, ALU.add).then_inc(gstep.sem, 1)
                    gstep.wait(dve, b, 4)
                    aT_ready.wait(dve, b, 0)
                    dve.scalar_tensor_tensor(a[:], igr[:], ib[:], cs[:], ALU.add, ALU.subtract).then_inc(gstep.sem, 1)
                    gstep.wait(dve, b, 5)
                    dve.tensor_tensor_scan(mx[:], a[:], a[:], LOWEST, ALU.max, ALU.max).then_inc(gstep.sem, 1)
                    gstep.wait(dve, b, 6)
                    dve.tensor_scalar(negm[:, par], mx[:], -1.0, None, ALU.mult)
                    dve.tensor_tensor(mlog[:], mx[:], cs[:], ALU.add).then_inc(mlog_ready.sem, 1)
                if j == 7:
                    work_filled.wait(dve, b, 4)
                    dve.tensor_copy(aT[:, par].rearrange("p i t h -> p (i t h)"),
                                    ps_w[:, 1, 0, 0:2 * G]).then_inc(aT_ready.sem, 1)

            def combine(b, par, h):
                scores_ready.wait(dve, b, h + 1)
                decay_ready.wait(dve, b, h + 1)
                head_done.wait(dve, b, h - 1)
                dve.scalar_tensor_tensor(c[:, h % 2, :], ps_q[:, h % 2, 0:W], qk_scale, decay[:, h % 2, :],
                                         ALU.mult, ALU.mult).then_inc(c_ready.sem, 1)

            def spread(x):
                return x.unsqueeze(2).broadcast_to([P, G, dh])

            def divide(b, par):
                head_done.wait(dve, b, nh)
                outs = ps_o[:, :, 0:nh * (dh + 1)].rearrange("p t (h d) -> p t h d", d=dh + 1)
                total = outs[:, :, :, dh]
                dve.scalar_tensor_tensor(den[:], total, -1.0, aT[:, par, 1], ALU.mult, ALU.max).then_inc(estep.sem, 1)
                estep.wait(dve, b, 1)
                dve.tensor_tensor(den[:], total, den[:], ALU.max).then_inc(estep.sem, 1)
                estep.wait(dve, b, 2)
                dve.tensor_scalar(den[:], den[:], NORMALISER_EPS, None, ALU.add).then_inc(estep.sem, 1)
                estep.wait(dve, b, 3)
                dve.reciprocal(rden[:], den[:]).then_inc(estep.sem, 1)
                estep.wait(dve, b, 4)
                dve.tensor_tensor(hn[:], outs[:, :, :, 0:dh], rden[:].unsqueeze(3).broadcast_to([P, TB, nh, dh]),
                                  ALU.mult).then_inc(out_read.sem, 1)

            def group_statistics(b):
                flat = hn[:].rearrange("p t h d -> p (t h) d")
                out_read.wait(dve, b, 1)
                dve.tensor_reduce(msum[:], flat, AX.X, ALU.add).then_inc(estep.sem, 1)
                estep.wait(dve, b, 5)
                dve.tensor_scalar(mean[:], msum[:], 1.0 / dh, None, ALU.mult).then_inc(estep.sem, 1)
                estep.wait(dve, b, 6)
                dve.tensor_tensor(flat, flat, spread(mean[:]), ALU.subtract).then_inc(estep.sem, 1)
                estep.wait(dve, b, 7)
                dve.tensor_tensor(sq[:], hn[:], hn[:], ALU.mult).then_inc(estep.sem, 1)
                estep.wait(dve, b, 8)
                dve.tensor_reduce(vsum[:], sq[:].rearrange("p t h d -> p (t h) d"), AX.X,
                                  ALU.add).then_inc(vsum_ready.sem, 1)

            def add_residual(b, par):
                flat = hn[:].rearrange("p t h d -> p (t h) d")
                rowsv = hn[:].rearrange("p t h d -> p t (h d)")
                grstd_ready.wait(dve, b, 1)
                dve.tensor_tensor(flat, flat, spread(grstd[:]), ALU.mult).then_inc(estep.sem, 1)
                estep.wait(dve, b, 9)
                dve.tensor_tensor(rowsv, rowsv, owg[:].unsqueeze(1).broadcast_to([P, TB, D]),
                                  ALU.mult).then_inc(estep.sem, 1)
                dve.wait_ge(xres_in[par], load_times(b, par, 1))
                estep.wait(dve, b, 10)
                dve.tensor_tensor(xres[:, par], rowsv, xres[:, par], ALU.add).then_inc(sum_ready.sem, 1)

            def finish(b, par, j):
                if j == 1:
                    divide(b, par)
                if j == 2:
                    group_statistics(b)
                if j == 5:
                    add_residual(b, par)

            def turn(b, par, first=False, last=False, before_last=False):
                for h in range(nh):
                    combine(b, par, h)
                    for j in range(h * slots, (h + 1) * slots):
                        if not first:
                            finish(b - 1, 1 - par, j)
                        if not last:
                            prepare(b + 1, 1 - par, j)

            for j in range(8):
                prepare(0, 0, j)
            batches(dve, turn)
            for j in range(8):
                finish(B - 1, 1, j)


E = 8


def sorted_tiles(choices):
    return (choices * B * S + E * (P - 1)) // P


MAX_TILES = sorted_tiles(2)


class Running:

    def __init__(self, m, name):
        self.sem, self.before = m.sem(name), 0

    def target(self, dmas):
        self.before += 16 * dmas
        return self.before


class Routing:

    def __init__(self, m, choices):
        self.slot = m.sb("slot", [P, choices * NT], U32)
        self.weight = m.sb("weight", [P, choices, NT])
        self.expert = m.sb("expert", [P, MAX_TILES], I32)


def route_phase(nc, name, x_src, xn_dst, sorted_dst, consts, w, routing, choices, tiles_used, experts,
                alpha, none_expert, second_norm):
    J = choices * NT
    with ExitStack() as ctx:
        m = Space(nc, ctx, name)
        wr = m.sb("wr", [P, KC, E])
        eidx = m.sb("eidx", [P, E])
        before = m.sb("before", [P, P])
        tidx = m.sb("tidx", [P, MAX_TILES])
        least = m.sb("least", [P, MAX_TILES])
        gamma = m.sb("gamma", [P, D]) if second_norm else None
        beta = m.sb("beta", [P, D]) if second_norm else None
        ones = m.sb("ones", [P, P])
        ones_row = m.sb("ones_row", [P, E * J])
        xin = m.sb("xin", [P, 2, D])
        xn = m.sb("xn", [P, 2, D])
        rn = m.sb("rn", [P, D]) if second_norm else None
        xnT = m.sb("xnT", [P, KC, P])
        logits = m.sb("logits", [P, NT, E])
        xall = m.sb("xall", [P, NT, D])
        norm = Norm(m, consts)
        if second_norm:
            m2 = Space(nc, ctx, name + "_again", m.sems)
            norm2 = Norm(m2, consts)
        top = m.sb("top", [P, choices, NT])
        ex = m.sb("ex", [P, NT, E])
        total = m.sb("total", [P, NT])
        eq = m.sb("eq", [P, NT, E])
        key = m.sb("key", [P, NT, E])
        least_key = m.sb("least_key", [P, NT])
        chosen = m.sb("chosen", [P, E, J])
        earlier = m.sb("earlier", [P, E, J])
        incl = m.sb("incl", [P, E, J])
        excl = m.sb("excl", [P, E, J])
        totals = m.sb("totals", [P, E, J])
        cnt = m.sb("cnt", [P, E])
        ntiles = m.sb("ntiles", [P, E])
        end = m.sb("end", [P, E])
        adj = m.sb("adj", [P, E])
        slotf = m.sb("slotf", [P, J])
        past = m.sb("past", [P, MAX_TILES, E])
        expf = m.sb("expf", [P, MAX_TILES])
        flag = m.sb("flag", [P, NT])

        ps_x = m.psum("ps_x", [P, 512])
        ps_l = m.psum("ps_l", [P, 512])
        ps_e = m.psum("ps_e", [P, 512])
        ps_t = m.psum("ps_t", [P, 512])

        weights_in = m.sem("weights_in")
        loaded = [m.sem("loaded0"), m.sem("loaded1")]
        norm_stored = [m.sem("norm_stored0"), m.sem("norm_stored1")]
        all_in = m.sem("all_in")
        xn_ready = Tally(m.sem("xn_ready"), 1, 1)
        rn_step = Tally(m.sem("rn_step"), 2)
        rn_ready = Tally(m.sem("rn_ready"), 1)
        xnT_ready = Tally(m.sem("xnT_ready"), 1, 1)
        xnT_copied = Tally(m.sem("xnT_copied"), 1)
        logits_ready = Tally(m.sem("logits_ready"), 1)
        logits_copied = Tally(m.sem("logits_copied"), 1, 1)
        step_done = m.sem("step_done")
        exponent_in = m.sem("exponent_in")
        exponent_out = m.sem("exponent_out")
        chosen_ready = m.sem("chosen_ready")
        counted = m.sem("counted")
        slots_ready = m.sem("slots_ready")
        scattered = w["scattered"].sem
        all_scattered = w["scattered"].target(J)
        ident = consts["ident"]
        gate = w["gate"]
        nweights = 5 + (2 if second_norm else 0)
        block = m.block()

        @block.sync
        def _(sp):
            sp.dma_start(wr[:], w["router"]).then_inc(weights_in, 16)
            sp.dma_start(eidx[:], w["eidx"]).then_inc(weights_in, 16)
            sp.dma_start(before[:], w["before"]).then_inc(weights_in, 16)
            sp.dma_start(tidx[:], w["tidx"]).then_inc(weights_in, 16)
            sp.dma_start(least[:], w["least"]).then_inc(weights_in, 16)
            if second_norm:
                sp.dma_start(gamma[:], w["gamma"].broadcast_to([P, D])).then_inc(weights_in, 16)
                sp.dma_start(beta[:], w["beta"].broadcast_to([P, D])).then_inc(weights_in, 16)

            def turn(n, par, first=False, last=False):
                if first:
                    sp.dma_start(xin[:, 0], tile_rows(x_src, 0)).then_inc(loaded[0], 16)
                if not last:
                    xn_ready.wait(sp, n, 0)
                    sp.dma_start(xin[:, 1 - par], tile_rows(x_src, n + 1)).then_inc(loaded[1 - par], 16)
                xn_ready.wait(sp, n, 1)
                sp.dma_start(xn_dst[n], xn[:, par]).then_inc(norm_stored[par], 16)

            tiles(sp, turn)
            for par in range(2):
                sp.wait_ge(norm_stored[par], 16 * (NT // 2))
            sp.dma_start(xall[:], xn_dst.rearrange("n p d -> p n d")).then_inc(all_in, 16)

        @block.gpsimd
        def _(pool):
            with pool.Fori(0, NT) as n:
                norm.on_pool(pool, n)
                if second_norm:
                    norm2.on_pool(pool, n)
            pool.wait_ge(all_in, 16)
            pool.wait_ge(slots_ready, 1)
            for c in range(choices):
                for n in range(NT):
                    j = c * NT + n
                    pool.indirect_dma_start(
                        out=sorted_dst, out_offset=bass.IndirectOffsetOnAxis(ap=routing.slot[:, j:j + 1], axis=0),
                        in_=xall[:, n, :], in_offset=None).then_inc(scattered, 16)
            pool.wait_ge(scattered, all_scattered)

        @block.tensor
        def _(pe):
            pe.sem_inc(xnT_ready.sem, 1)
            pe.wait_ge(weights_in, 16 * nweights)

            def turn(n, par, first=False, last=False):
                (rn_ready if second_norm else xn_ready).wait(pe, n, 1)
                src = rn if second_norm else xn[:, par]
                for k in range(KC):
                    last_t = pe.transpose(ps_x[:, k * P:(k + 1) * P], src[:, k * P:(k + 1) * P], ident[:])
                last_t.then_inc(xnT_ready.sem, 1)
                xnT_copied.wait(pe, n, 1)
                logits_copied.wait(pe, n, 0)
                for k in range(KC):
                    last_m = pe.matmul(ps_l[:, 0:E], xnT[:, k, :], wr[:, k, :], start=(k == 0), stop=(k == KC - 1))
                last_m.then_inc(logits_ready.sem, 1)

            tiles(pe, turn)
            pe.wait_ge(chosen_ready, 1)
            flat = chosen[:].rearrange("p e j -> p (e j)")
            pe.matmul(ps_e[:, 0:E * J], before[:], flat, start=True, stop=True)
            pe.matmul(ps_t[:, 0:E * J], ones[:], flat, start=True, stop=True).then_inc(counted, 1)

        @block.scalar
        def _(act):
            def turn(n, par, first=False, last=False):
                xnT_ready.wait(act, n, 1)
                act.activation(xnT[:].rearrange("p k n -> p (k n)"), ps_x[:, 0:D],
                               ACT.Copy).then_inc(xnT_copied.sem, 1)

            tiles(act, turn)
            act.wait_ge(exponent_in, 1)
            act.activation(ex[:], logits[:], ACT.Exp).then_inc(exponent_out, 1)

        @block.vector
        def _(dve):
            dve.sem_inc(xn_ready.sem, 1)
            dve.sem_inc(logits_copied.sem, 1)
            done = [0]

            def step(ins):
                done[0] += 1
                ins.then_inc(step_done, 1)
                dve.wait_ge(step_done, done[0])

            step(dve.memset(ones[:], 1.0))
            step(dve.memset(ones_row[:], 1.0))
            dve.wait_ge(weights_in, 16 * nweights)

            def normalise(n, par, first=False):
                dve.wait_ge(loaded[par], tile_times(n, par, 1))
                norm.statistics(dve, xin[:, par], n)
                if not first:
                    dve.wait_ge(norm_stored[par], tile_times(n, par, 1) - 16)
                norm.apply(dve, xn[:, par], xin[:, par], n).then_inc(xn_ready.sem, 1)
                if second_norm:
                    xn_ready.wait(dve, n, 1)
                    norm2.statistics(dve, xn[:, par], n)
                    norm2.apply(dve, rn[:], xn[:, par], n).then_inc(rn_step.sem, 1)
                    rn_step.wait(dve, n, 1)
                    dve.tensor_tensor(rn[:], rn[:], gamma[:], ALU.mult).then_inc(rn_step.sem, 1)
                    rn_step.wait(dve, n, 2)
                    dve.tensor_tensor(rn[:], rn[:], beta[:], ALU.add).then_inc(rn_ready.sem, 1)

            def turn(n, par, first=False, last=False):
                if first:
                    normalise(0, 0, first=True)
                if not last:
                    if second_norm:
                        xnT_ready.wait(dve, n, 1)
                    normalise(n + 1, 1 - par, first=first)
                logits_ready.wait(dve, n, 1)
                dve.tensor_scalar(logits[:, n, :],
                                  ps_l[:, 0:E], 1.0, None, ALU.mult).then_inc(logits_copied.sem, 1)

            tiles(dve, turn)
            logits_copied.wait(dve, NT - 1, 1)

            def over_experts(x):
                return x.unsqueeze(2).broadcast_to([P, NT, E])

            step(dve.tensor_reduce(total[:], logits[:], AX.X, ALU.max))
            dve.tensor_tensor(logits[:], logits[:], over_experts(total[:]), ALU.subtract).then_inc(exponent_in, 1)
            dve.wait_ge(exponent_out, 1)
            step(dve.tensor_reduce(total[:], ex[:], AX.X, ALU.add))
            step(dve.reciprocal(total[:], total[:]))
            step(dve.tensor_tensor(ex[:], ex[:], over_experts(total[:]), ALU.mult))
            eids = eidx[:].unsqueeze(1).broadcast_to([P, NT, E])
            for c in range(choices):
                step(dve.tensor_reduce(top[:, c], ex[:], AX.X, ALU.max))
                step(dve.tensor_tensor(eq[:], ex[:], over_experts(top[:, c]), ALU.is_equal))
                step(dve.scalar_tensor_tensor(key[:], eq[:], -2.0 * E, eids, ALU.mult, ALU.add))
                step(dve.tensor_reduce(least_key[:], key[:], AX.X, ALU.min))
                mine = chosen[:, :, c * NT:(c + 1) * NT].rearrange("p e n -> p n e")
                step(dve.tensor_tensor(mine, key[:], over_experts(least_key[:]), ALU.is_equal))
                if c < choices - 1:
                    step(dve.scalar_tensor_tensor(ex[:], mine, -4.0, ex[:], ALU.mult, ALU.add))
                if none_expert:
                    step(dve.tensor_scalar(flag[:], chosen[:, E - 1, c * NT:(c + 1) * NT], -alpha, alpha,
                                           ALU.mult, ALU.add))
                    step(dve.tensor_tensor(top[:, c], top[:, c], flag[:], ALU.mult))
            step(dve.tensor_scalar(routing.weight[:], top[:], gate, None, ALU.mult))
            dve.sem_inc(chosen_ready, 1)
            dve.wait_ge(counted, 1)
            flat = "p e j -> p (e j)"
            step(dve.tensor_copy(totals[:].rearrange(flat), ps_t[:, 0:E * J]))
            step(dve.tensor_tensor_scan(incl[:].rearrange(flat), ones_row[:], totals[:].rearrange(flat), 0.0,
                                        ALU.mult, ALU.add))
            step(dve.tensor_tensor(excl[:], incl[:], totals[:], ALU.subtract))
            step(dve.tensor_tensor(earlier[:].rearrange(flat), ps_e[:, 0:E * J], excl[:].rearrange(flat), ALU.add))
            step(dve.tensor_tensor(cnt[:], incl[:, :, J - 1], excl[:, :, 0], ALU.subtract))
            step(dve.tensor_scalar(ntiles[:], cnt[:], 1.0 / P, 0.5 - 0.5 / P, ALU.mult, ALU.add))
            step(dve.tensor_scalar(ntiles[:], ntiles[:], MAGIC, None, ALU.add))
            step(dve.tensor_scalar(ntiles[:], ntiles[:], MAGIC, None, ALU.subtract))
            step(dve.tensor_tensor_scan(end[:], ones_row[:, 0:E], ntiles[:], 0.0, ALU.mult, ALU.add))
            step(dve.tensor_tensor(adj[:], end[:], ntiles[:], ALU.subtract))
            step(dve.scalar_tensor_tensor(adj[:], adj[:], float(P), excl[:, :, 0], ALU.mult, ALU.subtract))
            step(dve.tensor_tensor(earlier[:], earlier[:], adj[:].unsqueeze(2).broadcast_to([P, E, J]), ALU.add))
            step(dve.tensor_tensor(earlier[:], earlier[:], chosen[:], ALU.mult))
            step(dve.tensor_reduce(slotf[:], earlier[:].rearrange("p e j -> p j e"), AX.X, ALU.add))
            step(dve.tensor_copy(routing.slot[:], slotf[:]))
            dve.sem_inc(slots_ready, 1)
            ne = experts - 1
            step(dve.tensor_tensor(past[:, :, 0:ne], tidx[:].unsqueeze(2).broadcast_to([P, MAX_TILES, ne]),
                                   end[:, 0:ne].unsqueeze(1).broadcast_to([P, MAX_TILES, ne]), ALU.is_ge))
            step(dve.tensor_reduce(expf[:], past[:, :, 0:ne], AX.X, ALU.add))
            step(dve.tensor_tensor(expf[:], expf[:], least[:], ALU.max))
            step(dve.tensor_copy(routing.expert[:], expf[:]))


def experts_phase(nc, name, x_rows, y_rows, w, routing, n_sorted, n_shared, F, kind):
    FC = F // P
    HC = FC // 2
    HW = HC * P
    mats = 2 if kind == "swiglu" else 1
    up_cols = mats * KC * HW
    down_cols = FC * D + (FC if kind == "relu" else 0)
    ntiles = n_sorted + n_shared
    sets = 3 if n_shared else 2
    with ExitStack() as ctx:
        m = Space(nc, ctx, name)
        wup = m.sb("wup", [P, sets, 2, up_cols])
        wdown = m.sb("wdown", [P, sets, down_cols])
        b2 = m.sb("b2", [P, 2, D])
        x = m.sb("x", [P, 2, D])
        xT = m.sb("xT", [P, 2, KC, P])
        act_out = m.sb("act_out", [P, 2, HW])
        hT = m.sb("hT", [P, 2, FC * P])
        y = m.sb("y", [P, 2, D])
        ps_a = m.psum("ps_a", [P, 2, 512])
        ps_b = m.psum("ps_b", [P, 2, 512])
        ps_x = m.psum("ps_x", [P, 512])
        ps_y = m.psum("ps_y", [P, 2, 512])

        up_in = [[m.sem(f"up_in{half}{par}") for par in range(2)] for half in range(2)]
        down_in = [m.sem("down_in0"), m.sem("down_in1")]
        shared_in = m.sem("shared_in")
        x_in = [m.sem("x_in0"), m.sem("x_in1")]
        stored = [m.sem("stored0"), m.sem("stored1")]
        xT_ready = Tally(m.sem("xT_ready"), 1)
        xT_copied = Tally(m.sem("xT_copied"), 1)
        up_ready = Tally(m.sem("up_ready"), 2)
        act_ready = Tally(m.sem("act_ready"), 2)
        h_ready = Tally(m.sem("h_ready"), 2, 2)
        y_ready = Tally(m.sem("y_ready"), 1, 2)
        y_copied = Tally(m.sem("y_copied"), 1, 2)
        per = 2 if kind == "relu" else 1
        block = m.block()

        def turns(engine, turn):
            turn(0, 0, first=True)
            with engine.Fori(0, (n_sorted - 3) // 2) as pair:
                turn(2 * pair + 1, 1)
                turn(2 * pair + 2, 0)
            turn(n_sorted - 2, 1)
            turn(n_sorted - 1, 0, last=not n_shared, next_shared=True)
            if n_shared:
                turn(n_sorted, 1, shared=True, next_shared=True)
                with engine.Fori(0, n_shared // 2 - 1) as pair:
                    turn(2 * pair + (n_sorted + 1), 0, shared=True, next_shared=True)
                    turn(2 * pair + (n_sorted + 2), 1, shared=True, next_shared=True)
                turn(ntiles - 1, 0, last=True, shared=True)

        @block.sync
        def _(sp):
            def load(i, par, shared):
                reused = not isinstance(i, int) or i >= 2
                if reused:
                    xT_ready.wait(sp, i, -1)
                sp.dma_start(x[:, par], x_rows[i]).then_inc(x_in[par], 16)
                if shared:
                    return
                e = sp.value_load(routing.expert[0:1, i:i + 1] if isinstance(i, int)
                                  else routing.expert[0:1, bass.ds(i, 1)], min_val=0, max_val=E - 1)
                for half in range(2):
                    if reused:
                        up_ready.wait(sp, i, half - 3)
                    sp.dma_start(wup[:, par, half], w["experts"][e][:, half * up_cols:(half + 1) * up_cols]
                                 ).then_inc(up_in[half][par], 16)
                if reused:
                    y_ready.wait(sp, i, -1)
                sp.dma_start(wdown[:, par], w["experts"][e][:, 2 * up_cols:]).then_inc(down_in[par], 16)
                if kind == "relu":
                    if reused:
                        y_copied.wait(sp, i, -1)
                    sp.dma_start(b2[:, par], w["b2"][e].broadcast_to([P, D])).then_inc(down_in[par], 16)

            def turn(i, par, first=False, last=False, shared=False, next_shared=False):
                if first:
                    load(0, 0, False)
                if not last:
                    load(i + 1, 1 - par, next_shared)
                if n_shared and isinstance(i, int) and i == n_sorted - 2:
                    sp.dma_start(wup[:, 2], w["experts"][E - 1][:, 0:2 * up_cols].rearrange("p (h n) -> p h n", h=2)
                                 ).then_inc(shared_in, 16)
                    sp.dma_start(wdown[:, 2], w["experts"][E - 1][:, 2 * up_cols:]).then_inc(shared_in, 16)

            turns(sp, turn)

        @block.tensor
        def _(pe):
            pe.sem_inc(y_ready.sem, 2)

            def turn_x(i, par):
                pe.wait_ge(x_in[par], tile_times(i, par, 1))
                for k in range(KC):
                    last = pe.transpose(ps_x[:, k * P:(k + 1) * P], x[:, par, k * P:(k + 1) * P], w["ident"][:])
                last.then_inc(xT_ready.sem, 1)

            def up(i, par, half, shared):
                if half == 0:
                    xT_copied.wait(pe, i, 1)
                if not shared:
                    pe.wait_ge(up_in[half][par], tile_times(i, par, 1))
                elif half == 0:
                    pe.wait_ge(shared_in, 32)
                wset = 2 if shared else par
                h_ready.wait(pe, i, half - 1)
                for n, bank in enumerate((ps_a, ps_b)[:mats]):
                    for f in range(HC):
                        for k in range(KC):
                            at = (n * KC + k) * HW + f * P
                            last = pe.matmul(bank[:, half, f * P:(f + 1) * P], wup[:, wset, half, at:at + P],
                                             xT[:, par, k, :], start=(k == 0), stop=(k == KC - 1))
                last.then_inc(up_ready.sem, 1)

            def down(i, par, shared):
                if not shared:
                    pe.wait_ge(down_in[par], tile_times(i, par, per))
                h_ready.wait(pe, i, 2)
                y_copied.wait(pe, i, -1)
                wset = 2 if shared else par
                for f in range(FC):
                    last = pe.matmul(ps_y[:, par, 0:D], hT[:, par, f * P:(f + 1) * P],
                                     wdown[:, wset, f * D:(f + 1) * D], start=(f == 0), stop=(f == FC - 1))
                last.then_inc(y_ready.sem, 1)

            def turn(i, par, first=False, last=False, shared=False, next_shared=False):
                if first:
                    turn_x(0, 0)
                up(i, par, 0, shared)
                if not first:
                    down(i - 1, 1 - par, shared and not (isinstance(i, int) and i == n_sorted))
                if not last:
                    turn_x(i + 1, 1 - par)
                up(i, par, 1, shared)

            turns(pe, turn)
            down(ntiles - 1, 0, bool(n_shared))

        @block.scalar
        def _(act):
            act.sem_inc(y_copied.sem, 2)
            act.sem_inc(stored[0], 16)
            act.sem_inc(stored[1], 16)

            def copy_x(i, par):
                xT_ready.wait(act, i, 1)
                act.activation(xT[:, par].rearrange("p k n -> p (k n)"), ps_x[:, 0:D],
                               ACT.Copy).then_inc(xT_copied.sem, 1)

            def activate(i, par, half):
                if kind == "relu":
                    act.wait_ge(down_in[par], tile_times(i, par, per))
                up_ready.wait(act, i, half + 1)
                if kind == "swiglu":
                    act.activation(act_out[:, half], ps_a[:, half, 0:HW], ACT.Silu).then_inc(act_ready.sem, 1)
                if kind == "gelu":
                    act.activation(hT[:, par, half * HW:(half + 1) * HW], ps_a[:, half, 0:HW],
                                   ACT.Gelu).then_inc(h_ready.sem, 1)
                if kind == "relu":
                    for f in range(HC):
                        ff = half * HC + f
                        bias = wdown[:, par, FC * D + ff:FC * D + ff + 1]
                        last = act.activation(hT[:, par, ff * P:(ff + 1) * P], ps_a[:, half, f * P:(f + 1) * P],
                                              ACT.Relu, bias=bias)
                    last.then_inc(h_ready.sem, 1)

            def store(i, par):
                if kind != "relu":
                    y_ready.wait(act, i, 1)
                    act.wait_ge(stored[par], tile_times(i, par, 1))
                    act.activation(y[:, par], ps_y[:, par, 0:D], ACT.Copy).then_inc(y_copied.sem, 1)
                y_copied.wait(act, i, 1)
                act.dma_start(y_rows[i], y[:, par]).then_inc(stored[par], 16)

            def turn(i, par, first=False, last=False, shared=False, next_shared=False):
                if first:
                    if kind != "swiglu":
                        act.sem_inc(h_ready.sem, 2)
                    copy_x(0, 0)
                activate(i, par, 0)
                if not last:
                    copy_x(i + 1, 1 - par)
                if not first:
                    store(i - 1, 1 - par)
                activate(i, par, 1)

            turns(act, turn)
            store(ntiles - 1, 0)
            act.wait_ge(stored[0], 16 * ((ntiles + 1) // 2) + 16)
            act.wait_ge(stored[1], 16 * (ntiles // 2) + 16)

        @block.vector
        def _(dve):
            if kind == "swiglu":
                dve.sem_inc(h_ready.sem, 2)

                def multiply(i, par, half):
                    act_ready.wait(dve, i, half + 1)
                    dve.tensor_tensor(hT[:, par, half * HW:(half + 1) * HW], ps_b[:, half, 0:HW], act_out[:, half],
                                      ALU.mult).then_inc(h_ready.sem, 1)

                def turn(i, par, first=False, last=False, shared=False, next_shared=False):
                    multiply(i, par, 0)
                    multiply(i, par, 1)

                turns(dve, turn)
            if kind == "relu":
                def add_bias(i, par):
                    y_ready.wait(dve, i, 1)
                    dve.wait_ge(stored[par], tile_times(i, par, 1))
                    dve.tensor_tensor(y[:, par], ps_y[:, par, 0:D], b2[:, par], ALU.add).then_inc(y_copied.sem, 1)

                def turn(i, par, first=False, last=False, shared=False, next_shared=False):
                    add_bias(i, par)

                turns(dve, turn)


def combine_phase(nc, name, x_src, x_dst, y_sorted, y_shared, consts, routing, choices, gate_col, gathers):
    QT = NT // 4
    with ExitStack() as ctx:
        m = Space(nc, ctx, name)
        x = m.sb("x", [P, NT, D])
        y = m.sb("y", [P, choices, NT, D])
        ysh = m.sb("ysh", [P, NT, D]) if y_shared is not None else None
        x_in = [m.sem(f"x_in{q}") for q in range(4)]
        gathered = [g.sem for g in gathers]
        all_gathered = [g.target(QT * choices) for g in gathers]
        step_done = m.sem("step_done")
        sum_ready = m.sem("sum_ready")
        stored = m.sem("stored")
        nx = 2 if y_shared is not None else 1
        block = m.block()
        xs = x_src.rearrange("b (t p) d -> p (b t) d", p=P)
        xd = x_dst.rearrange("b (t p) d -> p (b t) d", p=P)
        part = [slice(q * QT, (q + 1) * QT) for q in range(4)]

        @block.sync
        def _(sp):
            for q in range(4):
                sp.dma_start(x[:, part[q]], xs[:, part[q]]).then_inc(x_in[q], 16)
                if y_shared is not None:
                    sp.dma_start(ysh[:, part[q]], y_shared.rearrange("n p d -> p n d")[:, part[q]]).then_inc(x_in[q], 16)
            for q in range(4):
                sp.wait_ge(sum_ready, q + 1)
                sp.dma_start(xd[:, part[q]], x[:, part[q]]).then_inc(stored, 16)
            sp.wait_ge(stored, 64)

        @block.gpsimd
        def _(pool):
            for q in range(4):
                for n in range(q * QT, (q + 1) * QT):
                    for c in range(choices):
                        j = c * NT + n
                        pool.indirect_dma_start(
                            out=y[:, c, n, :], out_offset=None, in_=y_sorted,
                            in_offset=bass.IndirectOffsetOnAxis(ap=routing.slot[:, j:j + 1], axis=0),
                        ).then_inc(gathered[q], 16)

        @block.vector
        def _(dve):
            done = [0]

            def step(ins):
                done[0] += 1
                ins.then_inc(step_done, 1)
                dve.wait_ge(step_done, done[0])

            for q in range(4):
                dve.wait_ge(x_in[q], 16 * nx)
                if y_shared is not None:
                    step(dve.scalar_tensor_tensor(x[:, part[q]], ysh[:, part[q]], consts["gates"][:, gate_col:gate_col + 1],
                                                  x[:, part[q]], ALU.mult, ALU.add))
                dve.wait_ge(gathered[q], all_gathered[q])
                for c in range(choices):
                    for n in range(q * QT, (q + 1) * QT):
                        last = dve.scalar_tensor_tensor(x[:, n, :], y[:, c, n, :], routing.weight[:, c, n:n + 1],
                                                        x[:, n, :], ALU.mult, ALU.add)
                    if c < choices - 1:
                        step(last)
                last.then_inc(sum_ready, 1)


def moe(nc, m, name, x_src, x_dst, consts, w, scratch, choices, F, kind, gate_col, alpha=1.0, shared=False,
        second_norm=False):
    n_sorted = sorted_tiles(choices)
    with ExitStack() as ctx:
        routing = Routing(Space(nc, ctx, name + "_routing"), choices)
        xs, ys = scratch["x_sorted"], scratch["y_sorted"]
        xn = xs[n_sorted:n_sorted + NT] if shared else scratch["x_norm"]
        flat = "n p d -> (n p) d"
        w = dict(w, gate=consts["gates"][:, gate_col:gate_col + 1], ident=consts["ident"], eidx=scratch["eidx"],
                 before=scratch["before"], tidx=scratch["tidx"], scattered=scratch["scattered"])
        route_phase(nc, name + "_route", x_src, xn, xs.rearrange(flat), consts, w, routing, choices, n_sorted,
                    E - 1 if shared else E, alpha, shared, second_norm)
        experts_phase(nc, name + "_experts", xs, ys, w, routing, n_sorted, NT if shared else 0, F, kind)
        combine_phase(nc, name + "_sum", x_src, x_dst, ys.rearrange(flat),
                      ys[n_sorted:n_sorted + NT] if shared else None, consts, routing, choices, gate_col,
                      scratch["gathers"])


def setup_phase(nc, consts, ident_dram, g_dram, x_sorted):
    with ExitStack() as ctx:
        m = Space(nc, ctx, "setup")
        zeros = m.sb("zeros", [P, D])
        const_in = m.sem("const_in")
        zeros_set = m.sem("zeros_set")
        zeros_out = m.sem("zeros_out")
        set_done = m.sem("set_done")
        block = m.block()

        @block.sync
        def _(sp):
            sp.dma_start(consts["ident"][:], ident_dram).then_inc(const_in, 16)
            sp.dma_start(consts["raw_gates"][:], g_dram.broadcast_to([P, 2 * LAYERS])).then_inc(const_in, 16)
            sp.wait_ge(zeros_set, 1)
            sp.dma_start(x_sorted.rearrange("n p d -> p n d"),
                         zeros[:].unsqueeze(1).broadcast_to([P, MAX_TILES, D])).then_inc(zeros_out, 16)
            sp.wait_ge(zeros_out, 16)

        @block.gpsimd
        def _(pool):
            pool.memset(consts["minus_half"][:], -0.5).then_inc(set_done, 1)
            pool.wait_ge(set_done, 1)

        @block.vector
        def _(dve):
            dve.memset(zeros[:], 0.0).then_inc(zeros_set, 1)

        @block.scalar
        def _(act):
            act.wait_ge(const_in, 32)
            act.activation(consts["gates"][:], consts["raw_gates"][:], ACT.Tanh)


def program(nc, t, out, upto):
    with ExitStack() as ctx:
        m = Space(nc, ctx, "all")
        consts = {
            "ident": m.sb("ident", [P, P]),
            "raw_gates": m.sb("raw_gates", [P, 2 * LAYERS]),
            "gates": m.sb("gates", [P, 2 * LAYERS]),
            "minus_half": m.sb("minus_half", [P, TB * H]),
        }
        def dram(name, shape):
            return nc.dram_tensor(name, shape, F32).ap()

        scratch = {
            "x_sorted": dram("x_sorted", [MAX_TILES, P, D]), "y_sorted": dram("y_sorted", [MAX_TILES, P, D]),
            "x_norm": dram("x_norm", [NT, P, D]),
            "scattered": Running(m, "scattered"), "gathers": [Running(m, f"gathered{q}") for q in range(4)],
            "eidx": t["eidx"], "before": t["before"], "tidx": t["tidx"],
        }
        bounce = {
            "q": nc.dram_tensor("q_parts", [PARTS, D, S], BF16).ap(),
            "k": nc.dram_tensor("k_parts", [PARTS, D, S], BF16).ap(),
            "m": nc.dram_tensor("m_parts", [PARTS, H, S], BF16).ap(),
        }
        setup_phase(nc, consts, t["ident"], t["gates"], scratch["x_sorted"])
        xs = [t["x"]] + [dram(f"x_after_{i}", [B, S, D]) for i in range(upto - 1)] + [out]
        steps = [
            lambda a, b: attention_phase(nc, "a0", a, b, t["ctx"], consts,
                                         {k: t["a0_" + k] for k in ("wq", "wk", "wv", "wo")}, 0, DH ** -0.5, bounce,
                                         (t["mask"], t["maskT"])),
            lambda a, b: quantised_ffn_phase(nc, "f0", a, b, consts,
                                             {"gate": t["f0_gate"], "up": t["f0_up"], "down": t["f0_down"]}, 4),
            lambda a, b: mlstm_phase(nc, "m1", a, b, t["ctx"], consts,
                                     {k: t["m1_" + k] for k in ("gates", "ib", "fb", "ow", "sel", "lower")}, 1, 8,
                                     False),
            lambda a, b: moe(nc, m, "f1", a, b, consts,
                             {"router": t["f1_router"], "experts": t["f1_experts"], "least": t["f1_least"]}, scratch,
                             1, 1024, "swiglu", 5, alpha=2.0, shared=True),
            lambda a, b: attention_phase(nc, "a2", a, b, t["ctx"], consts,
                                         {k: t["a2_" + k] for k in ("wq", "wk", "wv", "wo", "bq", "bk", "bv", "bo")},
                                         2, D ** -0.5, bounce),
            lambda a, b: moe(nc, m, "f2", a, b, consts,
                             {"router": t["f2_router"], "experts": t["f2_experts"], "b2": t["f2_b2"],
                              "least": t["least"]}, scratch, 1, 1024, "relu", 6),
            lambda a, b: mlstm_phase(nc, "m3", a, b, t["ctx"], consts,
                                     {k: t["m3_" + k] for k in ("gates", "ib", "fb", "ow", "sel", "lower")}, 3, 4,
                                     True),
            lambda a, b: moe(nc, m, "f3", a, b, consts,
                             {"router": t["f3_router"], "experts": t["f3_experts"], "least": t["least"],
                              "gamma": t["f3_gamma"], "beta": t["f3_beta"]}, scratch, 2, 512, "gelu", 7,
                             second_norm=True),
        ]
        for i, step in enumerate(steps[:upto]):
            step(xs[i], xs[i + 1])


LAYERS = 4
UPTO = 8


def _chunks(w):
    return w.reshape(-1, P, w.shape[-1]).transpose(1, 0, 2)


def _experts(up, down, bias=None):
    parts = []
    for half in range(2):
        for m in up:
            f = m.shape[2] // 2
            parts.append(np.stack([_chunks(w[:, half * f:(half + 1) * f]).reshape(P, -1) for w in m]))
    parts.append(np.stack([_chunks(w).reshape(P, -1) for w in down]))
    if bias is not None:
        parts.append(np.stack([_chunks(w[:, None]).reshape(P, -1) for w in bias]))
    return np.concatenate(parts, axis=2)


def _mlstm(prefix, wi, bi, wf, bf, scale):
    nh = len(bi)
    gates = np.zeros((wi.shape[1], 64), np.float32)
    gates[:, 0:nh] = wi.T
    gates[:, FG_ROW:FG_ROW + nh] = wf.T
    t, s = np.arange(P)[:, None], np.arange(P)[None, :]
    return {
        prefix + "gates": _chunks(gates), prefix + "ib": bi[:, None], prefix + "fb": bf[:, None],
        prefix + "ow": scale[None, :],
        prefix + "sel": np.repeat(np.eye(nh, dtype=np.float32), P, axis=1),
        prefix + "lower": np.where(t > s, np.float32(-1e30), np.float32(0)),
    }


def kernel(**inputs):
    import concourse.bacc as bacc
    from concourse.bass_utils import run_bass_kernel_spmd

    v = {k: np.asarray(a) for k, a in inputs.items()}
    laid = {
        "x": v["x"], "ctx": v["ctx_1024"], "mask": v["mask_BxSxS2_ff0"],
        "maskT": v["mask_BxSxS2_ff0"].transpose(0, 2, 1),
        "ident": np.eye(P, dtype=np.float32),
        "gates": np.concatenate([v["g_xattn"], v["g_ffn"]])[None, :],
        "a0_wq": _chunks(v["L0_xattn_Wq"]), "a0_wk": _chunks(v["L0_xattn_Wk"]),
        "a0_wv": _chunks(v["L0_xattn_Wv"]), "a0_wo": _chunks(v["L0_xattn_Wo"]),
        "f0_gate": _chunks(v["L0_ffn_w_gate"].T), "f0_up": _chunks(v["L0_ffn_w_up"].T),
        "f0_down": _chunks(v["L0_ffn_w_down"].T),
        **_mlstm("m1_", v["L1_xattn_igate_w"], v["L1_xattn_igate_b"], v["L1_xattn_fgate_w"],
                 v["L1_xattn_fgate_b"], v["L1_xattn_out_w"]),
    }
    rows_of = np.arange(P)
    laid.update({
        "eidx": np.broadcast_to(np.arange(E, dtype=np.float32), (P, E)),
        "before": (rows_of[:, None] < rows_of[None, :]).astype(np.float32),
        "tidx": np.broadcast_to(np.arange(MAX_TILES, dtype=np.float32), (P, MAX_TILES)),
        "least": np.zeros((P, MAX_TILES), np.float32),
        "f1_least": np.broadcast_to(np.where(np.arange(MAX_TILES) < sorted_tiles(1), 0, E - 1).astype(np.float32),
                                    (P, MAX_TILES)),
        "f1_router": _chunks(v["L1_ffn_Wr"]),
        "f1_experts": _experts([np.concatenate([v["L1_ffn_Wg"], v["L1_ffn_Wg_s"][None]]),
                                np.concatenate([v["L1_ffn_Wu"], v["L1_ffn_Wu_s"][None]])],
                               np.concatenate([v["L1_ffn_Wd"], v["L1_ffn_Wd_s"][None]])),
        "a2_wq": _chunks(v["L2_xattn_wq"]), "a2_wk": _chunks(v["L2_xattn_wk"]),
        "a2_wv": _chunks(v["L2_xattn_wv"]), "a2_wo": _chunks(v["L2_xattn_wo"]),
        "a2_bq": v["L2_xattn_bq"].reshape(KC, P).T, "a2_bk": v["L2_xattn_bk"].reshape(KC, P).T,
        "a2_bv": v["L2_xattn_bv"][None, :], "a2_bo": v["L2_xattn_bo"][None, :],
        "f2_router": _chunks(v["L2_ffn_gate_w"].T),
        "f2_experts": _experts([v["L2_ffn_w1"]], v["L2_ffn_w2"], v["L2_ffn_b1"]),
        "f2_b2": v["L2_ffn_b2"][:, None, :],
        **_mlstm("m3_", v["L3_xattn_w_igate"], v["L3_xattn_b_igate"], v["L3_xattn_w_fgate"],
                 v["L3_xattn_b_fgate"], v["L3_xattn_ln_weight"]),
        "f3_router": _chunks(v["L3_ffn_gate_w"].T),
        "f3_gamma": v["L3_ffn_ln_gamma"][None, :], "f3_beta": v["L3_ffn_ln_beta"][None, :],
        "f3_experts": _experts([v["L3_ffn_w1"].transpose(0, 2, 1)], v["L3_ffn_w2"].transpose(0, 2, 1)),
    })
    nc = bacc.Bacc("TRN2", target_bir_lowering=False, num_devices=1)
    arrays, tensors = {}, {}
    for name, a in laid.items():
        arrays[f"in_{name}"] = np.ascontiguousarray(a)
        tensors[name] = nc.dram_tensor(f"in_{name}", a.shape, mybir.dt.from_np(a.dtype), kind="ExternalInput").ap()
    out = nc.dram_tensor("out_x", [B, S, D], F32, kind="ExternalOutput").ap()
    program(nc, tensors, out, UPTO)
    result = run_bass_kernel_spmd(nc, [arrays], core_ids=[0])
    return result.results[0]["out_x"]
```

```python
from contextlib import ExitStack

import numpy as np

import concourse.bass as bass
from concourse import mybir

ALU = mybir.AluOpType
ACT = mybir.ActivationFunctionType
AX = mybir.AxisListType
F32 = mybir.dt.float32
BF16 = mybir.dt.bfloat16
I32 = mybir.dt.int32
U32 = mybir.dt.uint32

P = 128
B = 8
S = 256
D = 256
TB = S // P
KC = D // P
LN_EPS = 1e-5
MASK_FACTOR = 1e9


class Space:

    def __init__(self, nc, ctx, name, sems=None):
        self.nc, self.ctx, self.name = nc, ctx, name
        self.sems = [] if sems is None else sems

    def sb(self, name, shape, dt=F32):
        return self.ctx.enter_context(self.nc.sbuf_tensor(f"{self.name}_{name}", shape, dt))

    def psum(self, name, shape, dt=F32):
        return self.ctx.enter_context(self.nc.psum_tensor(f"{self.name}_{name}", shape, dt))

    def sem(self, name):
        sem = self.ctx.enter_context(self.nc.semaphore(f"{self.name}_{name}"))
        self.sems.append(sem)
        return sem

    def block(self):
        self.ctx.callback(self.clear)
        return self.ctx.enter_context(self.nc.Block())

    def clear(self):
        with self.nc.Block() as block:
            @block.sync
            def _(sp):
                for sem in self.sems:
                    sp.sem_clear(sem)


class Tally:

    def __init__(self, sem, per, first=0):
        self.sem, self.per, self.first = sem, per, first

    def wait(self, engine, b, k):
        value = b * self.per + (self.first + k)
        if not isinstance(value, int) or value > 0:
            engine.wait_ge(self.sem, value)

    def wait_apart(self, engine, b, k, passed):
        self.wait(engine, b, k)
        engine.sem_inc(passed, 1)


def rows(dram, b):
    return dram[b].rearrange("(t p) d -> p t d", p=P)


def batches(engine, turn):
    turn(0, 0, first=True)
    with engine.Fori(0, B // 2 - 2) as pair:
        turn(2 * pair + 1, 1)
        turn(2 * pair + 2, 0)
    turn(B - 3, 1)
    turn(B - 2, 0, before_last=True)
    turn(B - 1, 1, last=True)


def load_times(b, par, per):
    return (b - par) * (8 * per) + 16 * per


H = 16
DH = D // H
PARTS = 3
Q_PARTS = ((0, 3), (1, 2), (2, 1))
STACK = 6 * DH
STACK_DMAS = PARTS + 6
STACK_M = STACK + PARTS
FILLS = (("outs0", "oT", "y", "q", "maxima"), ("outs1", "xnT", "v", "cT", "k"))
AHEAD = {"outs0": -1, "outs1": -1, "oT": -1, "y": -1, "v": 1, "maxima": 1, "xnT": 2, "cT": 2, "k": 2, "q": 2}
FILLS_AT = {0: ("outs0", "outs1"), 1: ("xnT",), 2: ("oT",), 3: ("y",), 4: ("v",), 5: ("cT",), 6: ("k",), 7: ("q",), 12: ("maxima",)}
MAXIMA_AT = {2: 1, 3: 1, 4: 1, 5: 2, 6: 1, 7: 2, 8: 2, 9: 2, 10: 2, 11: 2}


def has(b, ahead):
    return not isinstance(b, int) or 0 <= b + ahead < B


def fill_number(b, what):
    if not isinstance(b, int):
        return b * len(FILLS[0]) + (fill_number(1, what) - len(FILLS[0]))
    bank = what in FILLS[1]
    before = sum(has(turn, AHEAD[each]) for turn in range(FIRST_TURN, b) for each in FILLS[bank])
    here = [each for each in FILLS[bank] if has(b, AHEAD[each])]
    return before + here.index(what) + 1


FIRST_TURN = -3


def attention_turns(engine, turn):
    for b in range(FIRST_TURN, 1):
        turn(b, b % 2)
    with engine.Fori(0, B // 2 - 2) as pair:
        turn(2 * pair + 1, 1)
        turn(2 * pair + 2, 0)
    for b in range(B - 3, B + 1):
        turn(b, b % 2)


def attention_phase(nc, name, x_src, x_dst, ctx_dram, consts, w, gate_col, score_scale, bounce, mask_drams=None):
    masked = mask_drams is not None
    biased = "bq" in w
    DA = 32
    HG = P // DA
    with ExitStack() as ctx:
        m = Space(nc, ctx, name)
        wq = m.sb("wq", [P, KC, D])
        wk = m.sb("wk", [P, KC, D])
        wv = m.sb("wv", [P, KC, D])
        wo = m.sb("wo", [P, KC, D])
        bq = m.sb("bq", [P, KC])
        bqs = m.sb("bqs", [P, KC])
        bk = m.sb("bk", [P, KC])
        bv = m.sb("bv", [1, D])
        ones_row = m.sb("ones_row", [1, P])
        bo = m.sb("bo", [P, D])
        xin = m.sb("xin", [P, 2, TB, D])
        cin = m.sb("cin", [P, 2, TB, D])
        xres = m.sb("xres", [P, 2, TB, D])
        mask = m.sb("mask", [P, 2, TB, S]) if masked else None
        maskT = m.sb("maskT", [P, 2, TB, S]) if masked else None
        stats = m.sb("stats", [P, TB, 6])
        mv = m.sb("mv", [P, TB, 2])
        veps = m.sb("veps", [P, TB])
        rstd = m.sb("rstd", [P, TB])
        xn = m.sb("xn", [P, TB, D])
        xnT = m.sb("xnT", [P, KC, S])
        cT = m.sb("cT", [P, KC, S])
        full = {k: m.sb(f"{k}_full", [P, KC, S]) for k in "qk"}
        rest = {k: m.sb(f"{k}_rest", [P, KC, S]) for k in "qk"}
        parts = {k: m.sb(f"{k}_parts", [P, PARTS, KC, S], BF16) for k in "qk"}
        stack = {k: m.sb(f"{k}_stack", [STACK_M, 2, H, S], BF16) for k in "qk"}
        va = m.sb("va", [P, 2, TB, H, DA])
        junk = m.sb("junk", [P, 2, TB, S]) if masked else None
        maxima = m.sb("maxima", [P, TB, H])
        m_full = m.sb("m_full", [H, S])
        m_rest = m.sb("m_rest", [H, S])
        m_parts = m.sb("m_parts", [H, PARTS, S], BF16)
        masked_s = m.sb("masked_s", [P, 2, TB, S]) if masked else None
        probs = m.sb("probs", [P, 2, TB, S])
        rinv = m.sb("rinv", [P, TB, H])
        o_raw = m.sb("o_raw", [P, H // HG, S])
        o_sb = m.sb("o_sb", [P, TB, D])
        oT = m.sb("oT", [P, KC, S])
        yb = m.sb("yb", [P, TB, D])

        ps_n = m.psum("ps_n", [P, 2, TB, S])
        ps_t = m.psum("ps_t", [P, 2, TB, S])
        ps_o = m.psum("ps_o", [P, H // HG, S])
        ps_w = m.psum("ps_w", [P, 2, TB * S])

        weights_in = m.sem("weights_in")
        bias_scaled = m.sem("bias_scaled")
        ones_set = m.sem("ones_set")
        loaded = [m.sem("loaded0"), m.sem("loaded1")]
        mask_in = [m.sem("mask_in0"), m.sem("mask_in1")]
        maskT_in = [m.sem("maskT_in0"), m.sem("maskT_in1")]
        xres_in = [m.sem("xres_in0"), m.sem("xres_in1")]
        mask_scaled = Tally(m.sem("mask_scaled"), 1)
        maskT_scaled = Tally(m.sem("maskT_scaled"), 1)
        stored = Tally(m.sem("stored"), 16)
        stats_done = Tally(m.sem("stats_done"), 1)
        mv_ready = Tally(m.sem("mv_ready"), 1)
        eps_added = Tally(m.sem("eps_added"), 1)
        rstd_ready = Tally(m.sem("rstd_ready"), 1)
        xn_ready = Tally(m.sem("xn_ready"), 1)
        filled = [m.sem("filled0"), m.sem("filled1")]
        drained = [m.sem("drained0"), m.sem("drained1")]
        first_part = {k: Tally(m.sem(f"{k}_first_part"), 1) for k in "qk"}
        part_step = {k: Tally(m.sem(f"{k}_part_step"), 2) for k in "qk"}
        parts_ready = {k: Tally(m.sem(f"{k}_parts_ready"), 1) for k in "qk"}
        parts_out = {k: Tally(m.sem(f"{k}_parts_out"), 16) for k in "qk"}
        stacked = Tally(m.sem("stacked"), STACK_DMAS * 16)
        m_first = Tally(m.sem("m_first"), 1)
        m_step = Tally(m.sem("m_step"), 2)
        m_parts_ready = Tally(m.sem("m_parts_ready"), 1)
        m_out = Tally(m.sem("m_out"), 16)
        m_stacked = Tally(m.sem("m_stacked"), 16)
        raw_ready = Tally(m.sem("raw_ready"), H)
        maximum_ready = Tally(m.sem("maximum_ready"), H)
        scores_ready = Tally(m.sem("scores_ready"), H)
        mask_added = Tally(m.sem("mask_added"), H)
        probs_ready = Tally(m.sem("probs_ready"), H)
        head_done = Tally(m.sem("head_done"), H)
        o_unloaded = Tally(m.sem("o_unloaded"), 1)
        rinv_ready = Tally(m.sem("rinv_ready"), TB)
        o_ready = Tally(m.sem("o_ready"), 1)
        bias_added = Tally(m.sem("bias_added"), 1)
        sum_ready = Tally(m.sem("sum_ready"), 1)
        passed = m.sem("passed")
        ident = consts["ident"]
        minus_half = consts["minus_half"]
        gate = consts["gates"][:, gate_col:gate_col + 1]
        nweights = 4 + (4 if biased else 0)
        block = m.block()

        def wait_fill(engine, b, what, apart=False):
            sem = filled[what in FILLS[1]]
            engine.wait_ge(sem, fill_number(b, what))
            if apart:
                engine.sem_inc(passed, 1)

        @block.sync
        def _(sp):
            for dst, k in ((wq, "wq"), (wk, "wk"), (wv, "wv"), (wo, "wo")) + (
                    ((bq, "bq"), (bk, "bk"), (bv, "bv")) if biased else ()):
                sp.dma_start(dst[:], w[k]).then_inc(weights_in, 16)
            if biased:
                sp.dma_start(bo[:], w["bo"].broadcast_to([P, D])).then_inc(weights_in, 16)

            def load(b, par):
                sp.dma_start(xin[:, par], rows(x_src, b)).then_inc(loaded[par], 16)
                sp.dma_start(cin[:, par], rows(ctx_dram, b)).then_inc(loaded[par], 16)

            def load_mask(b, par):
                sp.dma_start(mask[:, par], rows(mask_drams[0], b)).then_inc(mask_in[par], 16)

            def load_maskT(b, par):
                sp.dma_start(maskT[:, par], rows(mask_drams[1], b)).then_inc(maskT_in[par], 16)

            def send_parts(b):
                for k in "kq":
                    parts_ready[k].wait_apart(sp, b, 1, passed)
                    sp.dma_start(bounce[k].rearrange("i d (e g) n -> (d e) i g n", g=KC), parts[k][:]
                                 ).then_inc(parts_out[k].sem, 16)

            def make_stack(b, par):
                for k in "kq":
                    parts_out[k].wait_apart(sp, b, 16, passed)
                row = 0
                for part, n in Q_PARTS:
                    sp.dma_start(stack["k"][row:row + n * DH, par],
                                 bounce["k"][0:n].rearrange("i d h n -> (i d) h n")).then_inc(stacked.sem, 16)
                    for _ in range(n):
                        sp.dma_start(stack["q"][row:row + DH, par], bounce["q"][part]).then_inc(stacked.sem, 16)
                        row += DH

            def stack_maxima(b, par):
                m_parts_ready.wait_apart(sp, b, 1, passed)
                sp.dma_start(bounce["m"].rearrange("i h n -> h i n"), m_parts[:]).then_inc(m_out.sem, 16)
                m_out.wait_apart(sp, b, 16, passed)
                sp.dma_start(stack["q"][STACK:STACK_M, par], bounce["m"]).then_inc(m_stacked.sem, 16)

            def turn(b, par):
                if has(b, -1):
                    head_done.wait_apart(sp, b - 1, H, passed)
                if has(b, 1):
                    make_stack(b + 1, 1 - par)
                if has(b, 0):
                    maximum_ready.wait_apart(sp, b, H, passed)
                    if has(b, -2):
                        stored.wait_apart(sp, b - 2, 16, passed)
                    sp.dma_start(xres[:, par], rows(x_src, b)).then_inc(xres_in[par], 16)
                if has(b, 1):
                    xn_ready.wait_apart(sp, b + 1, 1, passed)
                    wait_fill(sp, b - 1, "cT", apart=True)
                if has(b, 3):
                    load(b + 3, 1 - par)
                if masked and has(b, 2):
                    load_mask(b + 2, par)
                if masked and has(b, 1):
                    load_maskT(b + 1, 1 - par)
                if has(b, -1):
                    sum_ready.wait_apart(sp, b - 1, 1, passed)
                    sp.dma_start(rows(x_dst, b - 1), xres[:, 1 - par]).then_inc(stored.sem, 16)
                if has(b, 2):
                    if has(b, 1):
                        stacked.wait_apart(sp, b + 1, STACK_DMAS * 16, passed)
                    send_parts(b + 2)
                if has(b, 1):
                    stack_maxima(b + 1, 1 - par)

            attention_turns(sp, turn)
            stored.wait(sp, B - 1, 16)

        @block.gpsimd
        def _(pool):
            def deviation(b):
                mv_ready.wait_apart(pool, b, 1, passed)
                pool.tensor_scalar(veps[:], mv[:, :, 1], LN_EPS, None, ALU.add).then_inc(eps_added.sem, 1)
                eps_added.wait(pool, b, 1)
                pool.tensor_tensor(rstd[:], veps[:], minus_half[:, 0:TB], ALU.pow).then_inc(rstd_ready.sem, 1)

            def scale_mask(b, par):
                pool.wait_ge(mask_in[par], load_times(b, par, 1))
                pool.sem_inc(passed, 1)
                pool.tensor_scalar(mask[:, par], mask[:, par], -MASK_FACTOR, None,
                                   ALU.mult).then_inc(mask_scaled.sem, 1)

            def scale_maskT(b, par):
                pool.wait_ge(maskT_in[par], load_times(b, par, 1))
                pool.sem_inc(passed, 1)
                pool.tensor_scalar(maskT[:, par], maskT[:, par], -MASK_FACTOR, None,
                                   ALU.mult).then_inc(maskT_scaled.sem, 1)

            def split(u, k):
                part, left, steps = parts[k], rest[k], part_step[k]
                first_part[k].wait_apart(pool, u, 1, passed)
                pool.tensor_tensor(left[:], full[k][:], part[:, 0], ALU.subtract).then_inc(steps.sem, 1)
                steps.wait_apart(pool, u, 1, passed)
                pool.tensor_copy(part[:, 1], left[:]).then_inc(steps.sem, 1)
                steps.wait_apart(pool, u, 2, passed)
                pool.tensor_tensor(part[:, 2], left[:], part[:, 1], ALU.subtract).then_inc(parts_ready[k].sem, 1)

            def turn(b, par):
                if masked and has(b, 1):
                    scale_maskT(b + 1, 1 - par)
                if masked and has(b, 2):
                    scale_mask(b + 2, par)
                if has(b, 2):
                    split(b + 2, "k")
                    split(b + 2, "q")
                if has(b, 3):
                    deviation(b + 3)

            attention_turns(pool, turn)

        @block.tensor
        def _(pe):
            def transposes(dst, src):
                for k in range(KC):
                    for t in range(TB):
                        last = pe.transpose(dst[:, k, t * P:(t + 1) * P], src[:, t, k * P:(k + 1) * P], ident[:])
                return last

            def fill(b, par, what):
                bank = int(what in FILLS[1])
                before = fill_number(b, what) - 1
                if not (isinstance(before, int) and before == 0):
                    pe.wait_ge(drained[bank], before)
                out = ps_w[:, bank].rearrange("p (t s) -> p t s", t=TB)
                if what == "xnT":
                    xn_ready.wait(pe, b + 2, 1)
                    last = transposes(out, xn)
                if what == "cT":
                    pe.wait_ge(loaded[par], load_times(b + 2, par, 2))
                    last = transposes(out, cin[:, par])
                if what in ("q", "k"):
                    weight, act = (wq, xnT) if what == "q" else (wk, cT)
                    if what == "q":
                        pe.wait_ge(drained[1], fill_number(b, "xnT"))
                    for g in range(KC):
                        for k in range(KC):
                            last = pe.matmul(out[:, g, :], weight[:, k, g * P:(g + 1) * P], act[:, k, :],
                                             start=(k == 0), stop=(k == KC - 1))
                if what == "v":
                    for t in range(TB):
                        if biased:
                            pe.matmul(out[:, t, :], ones_row[:], bv[:], start=True, stop=False)
                        for k in range(KC):
                            last = pe.matmul(out[:, t, :], cT[:, k, t * P:(t + 1) * P], wv[:, k, :],
                                             start=(k == 0 and not biased), stop=(k == KC - 1))
                if what in ("outs0", "outs1"):
                    o_unloaded.wait(pe, b - 1, 1)
                    for g in range(H // HG):
                        last = pe.transpose(ps_w[:, bank, g * P:(g + 1) * P], o_raw[:, g, bank * P:(bank + 1) * P],
                                            ident[:])
                if what == "oT":
                    o_ready.wait(pe, b - 1, 1)
                    last = transposes(out, o_sb)
                if what == "y":
                    for t in range(TB):
                        for k in range(KC):
                            last = pe.matmul(out[:, t, :], oT[:, k, t * P:(t + 1) * P], wo[:, k, :],
                                             start=(k == 0), stop=(k == KC - 1))
                if what == "maxima":
                    maximum_ready.wait(pe, b + 1, H)
                    for t in range(TB):
                        last = pe.transpose(out[0:H, 0, t * P:(t + 1) * P], maxima[:, t, :], ident[:])
                last.then_inc(filled[bank], 1)

            def raw_scores(u, par, h):
                if h == 0:
                    stacked.wait(pe, u, STACK_DMAS * 16)
                maximum_ready.wait(pe, u, h - 1)
                for t in range(TB):
                    last = pe.matmul(ps_n[:, h % 2, t, :], stack["q"][0:STACK, par, h, t * P:(t + 1) * P],
                                     stack["k"][0:STACK, par, h, :], start=True, stop=True)
                last.then_inc(raw_ready.sem, 1)

            def scores(b, par, h):
                if h == 0:
                    m_stacked.wait(pe, b, 16)
                (mask_added if masked else probs_ready).wait(pe, b, h - 1)
                for lb in range(TB):
                    last = pe.matmul(ps_t[:, h % 2, lb, :], stack["k"][:, par, h, lb * P:(lb + 1) * P],
                                     stack["q"][:, par, h, :], start=True, stop=True)
                last.then_inc(scores_ready.sem, 1)

            def weigh(b, par, h):
                probs_ready.wait(pe, b, h + 1)
                if h == 0:
                    if has(b, -1):
                        o_unloaded.wait(pe, b - 1, 1)
                    pe.wait_ge(drained[1], fill_number(b - 1, "v"))
                j = h % HG * DA
                for lb in range(TB):
                    last = pe.matmul(ps_o[j:j + DA, h // HG, :], va[:, par, lb, h, :], probs[:, h % 2, lb, :],
                                     start=(lb == 0), stop=(lb == TB - 1))
                last.then_inc(head_done.sem, 1)

            def turn(b, par):
                if isinstance(b, int) and b == 0:
                    pe.wait_ge(ones_set, 3)
                if has(b, 0):
                    scores(b, par, 0)
                done = 0
                for h in range(H):
                    if has(b, 0) and h < H - 1:
                        scores(b, par, h + 1)
                    for what in FILLS_AT.get(h, ()):
                        if has(b, AHEAD[what]):
                            fill(b, par, what)
                    for _ in range(MAXIMA_AT.get(h, 0)):
                        if has(b, 1):
                            raw_scores(b + 1, 1 - par, done)
                        done += 1
                    if has(b, 0):
                        weigh(b, par, h)

            pe.wait_ge(weights_in, 16 * nweights)
            pe.wait_ge(ones_set, 1)
            attention_turns(pe, turn)

        @block.scalar
        def _(act):
            def unload(b):
                head_done.wait(act, b, H)
                act.activation(o_raw[:], ps_o[:], ACT.Copy).then_inc(o_unloaded.sem, 1)

            def drain(b, par, what):
                if what in ("outs0", "outs1", "y"):
                    return
                bank = int(what in FILLS[1])
                src = ps_w[:, bank].rearrange("p (t s) -> p t s", t=TB)
                wait_fill(act, b, what)
                if what == "xnT":
                    last = act.activation(xnT[:], src, ACT.Copy)
                if what == "cT":
                    last = act.activation(cT[:], src, ACT.Copy)
                if what == "oT":
                    last = act.activation(oT[:], src, ACT.Copy)
                if what in ("q", "k"):
                    scale, bias = (score_scale, bqs) if what == "q" else (1.0, bk)
                    if biased:
                        for g in range(KC):
                            last = act.activation(full[what][:, g, :], src[:, g, :], ACT.Identity,
                                                  bias=bias[:, g:g + 1], scale=scale)
                    else:
                        last = act.activation(full[what][:], src, ACT.Copy, scale=scale)
                if what == "v":
                    if not has(b, 0):
                        act.wait_ge(ones_set, 2)
                    last = act.activation(va[:, 1 - par, :, :, 0:DH], src.rearrange("p t (h d) -> p t h d", d=DH),
                                          ACT.Copy)
                if what == "maxima":
                    last = act.activation(m_full[:], src[0:H, 0, :], ACT.Copy, scale=-1.0)
                last.then_inc(drained[bank], 1)
                if what in ("q", "k"):
                    act.wait_ge(drained[bank], fill_number(b, what))
                    if has(b, 1):
                        parts_out[what].wait(act, b + 1, 16)
                    act.activation(parts[what][:, 0], full[what][:], ACT.Copy).then_inc(first_part[what].sem, 1)
                if what == "maxima":
                    act.wait_ge(drained[bank], fill_number(b, what))
                    act.activation(m_parts[:, 0, :], m_full[:], ACT.Copy).then_inc(m_first.sem, 1)

            def exponent(b, par, h):
                if masked:
                    mask_added.wait(act, b, h + 1)
                else:
                    scores_ready.wait(act, b, h + 1)
                head_done.wait(act, b, h - 1)
                src = masked_s[:, h % 2] if masked else ps_t[:, h % 2]
                act.activation(probs[:, h % 2], src, ACT.Exp).then_inc(probs_ready.sem, 1)

            def turn(b, par):
                if has(b, -1):
                    unload(b - 1)
                for h in range(H):
                    if has(b, 0):
                        exponent(b, par, h)
                    for what in FILLS_AT.get(h, ()):
                        if has(b, AHEAD[what]):
                            drain(b, par, what)

            if biased:
                act.wait_ge(weights_in, 16 * nweights)
                act.activation(bqs[:], bq[:], ACT.Copy, scale=score_scale).then_inc(bias_scaled, 1)
                act.wait_ge(bias_scaled, 1)
            attention_turns(act, turn)

        @block.vector
        def _(dve):
            dve.memset(ones_row[:], 1.0).then_inc(ones_set, 1)

            def statistics(b, par):
                dve.wait_ge(loaded[par], load_times(b, par, 2))
                for t in range(TB):
                    last = dve.bn_stats(stats[:, t, :], xin[:, par, t, :])
                last.then_inc(stats_done.sem, 1)
                stats_done.wait_apart(dve, b, 1, passed)
                for t in range(TB):
                    last = dve.bn_aggr(mv[:, t, :], stats[:, t, :])
                last.then_inc(mv_ready.sem, 1)

            def normalise(b, par, turn):
                rstd_ready.wait(dve, b, 1)
                if has(turn, 2):
                    wait_fill(dve, turn, "xnT")
                for t in range(TB):
                    last = dve.tensor_scalar(xn[:, t, :], xin[:, par, t, :], mv[:, t, 0:1], rstd[:, t:t + 1],
                                             ALU.subtract, ALU.mult)
                last.then_inc(xn_ready.sem, 1)

            def split_maxima(u):
                m_first.wait(dve, u, 1)
                dve.tensor_tensor(m_rest[:], m_full[:], m_parts[:, 0, :], ALU.subtract).then_inc(m_step.sem, 1)
                m_step.wait(dve, u, 1)
                dve.tensor_copy(m_parts[:, 1, :], m_rest[:]).then_inc(m_step.sem, 1)
                m_step.wait(dve, u, 2)
                dve.tensor_tensor(m_parts[:, 2, :], m_rest[:], m_parts[:, 1, :],
                                  ALU.subtract).then_inc(m_parts_ready.sem, 1)

            def maximum(u, par, h):
                if masked:
                    if h == 0:
                        mask_scaled.wait(dve, u, 1)
                    raw_ready.wait_apart(dve, u, h + 1, passed)
                    for t in range(TB):
                        last = dve.tensor_tensor_reduce(junk[:, h % 2, t], ps_n[:, h % 2, t, :], mask[:, par, t, :],
                                                        1.0, -3.0e38, ALU.add, ALU.max, maxima[:, t, h:h + 1])
                else:
                    raw_ready.wait(dve, u, h + 1)
                    last = dve.tensor_reduce(maxima[:, :, h:h + 1], ps_n[:, h % 2], AX.X, ALU.max)
                last.then_inc(maximum_ready.sem, 1)

            def add_mask(b, par, h):
                if not masked:
                    return
                if h == 0:
                    maskT_scaled.wait(dve, b, 1)
                probs_ready.wait(dve, b, h - 1)
                scores_ready.wait(dve, b, h + 1)
                dve.tensor_tensor(masked_s[:, h % 2], ps_t[:, h % 2], maskT[:, par],
                                  ALU.add).then_inc(mask_added.sem, 1)

            def divide(b, turn):
                for t in range(TB):
                    wait_fill(dve, turn, f"outs{t}")
                    heads = ps_w[:, t].rearrange("p (h d) -> p h d", d=DA)
                    dve.reciprocal(rinv[:, t], heads[:, :, DH]).then_inc(rinv_ready.sem, 1)
                    rinv_ready.wait(dve, b, t + 1)
                    last = dve.tensor_tensor(o_sb[:, t].rearrange("p (h d) -> p h d", d=DH), heads[:, :, 0:DH],
                                             rinv[:, t].unsqueeze(2).broadcast_to([P, H, DH]), ALU.mult)
                    last.then_inc(drained[t], 1)
                dve.wait_ge(drained[TB - 1], fill_number(turn, f"outs{TB - 1}"))
                dve.sem_inc(o_ready.sem, 1)

            def add_residual(b, par, turn):
                wait_fill(dve, turn, "y")
                dve.wait_ge(xres_in[par], load_times(b, par, 1))
                y = ps_w[:, 0].rearrange("p (t s) -> p t s", t=TB)
                if biased:
                    dve.tensor_tensor(yb[:], y, bo[:].unsqueeze(1).broadcast_to([P, TB, D]),
                                      ALU.add).then_inc(bias_added.sem, 1)
                    bias_added.wait(dve, b, 1)
                dve.scalar_tensor_tensor(xres[:, par], yb[:] if biased else y, gate, xres[:, par], ALU.mult,
                                         ALU.add).then_inc(sum_ready.sem, 1)
                sum_ready.wait(dve, b, 1)
                dve.sem_inc(drained[0], 1)

            def turn(b, par):
                if isinstance(b, int) and b == FIRST_TURN + 1:
                    dve.memset(va[:], 1.0).then_inc(ones_set, 1)
                    dve.memset(stack["k"][STACK:STACK_M], 1.0).then_inc(ones_set, 1)
                done = 0
                for h in range(H):
                    if has(b, 0):
                        add_mask(b, par, h)
                    for _ in range(MAXIMA_AT.get(h, 0)):
                        if has(b, 1):
                            maximum(b + 1, 1 - par, done)
                        done += 1
                    if h == 0 and has(b, -1):
                        divide(b - 1, b)
                    if h == 3 and has(b, -1):
                        add_residual(b - 1, 1 - par, b)
                    if h == 12 and has(b, 1):
                        split_maxima(b + 1)
                    if has(b, 3):
                        if h == 13:
                            statistics(b + 3, 1 - par)
                        if h == 15:
                            normalise(b + 3, 1 - par, b)

            if biased:
                dve.wait_ge(weights_in, 16 * nweights)
            attention_turns(dve, turn)


NT = B * TB
MAGIC = 1.5 * 2.0 ** 23


def tile_rows(dram, n):
    return dram.rearrange("b (t p) d -> (b t) p d", p=P)[n]


def tiles(engine, turn, count=NT):
    turn(0, 0, first=True)
    with engine.Fori(0, count // 2 - 1) as pair:
        turn(2 * pair + 1, 1)
        turn(2 * pair + 2, 0)
    turn(count - 1, 1, last=True)


def tile_times(n, par, per):
    return (n - par) * (8 * per) + 16 * per


class Norm:

    def __init__(self, m, consts):
        self.stats = m.sb("ln_stats", [P, 6])
        self.mv = m.sb("ln_mv", [P, 2])
        self.veps = m.sb("ln_veps", [P, 1])
        self.rstd = m.sb("ln_rstd", [P, 1])
        self.minus_half = consts["minus_half"]
        self.stats_done = Tally(m.sem("ln_stats_done"), 1)
        self.mv_ready = Tally(m.sem("ln_mv_ready"), 1)
        self.eps_added = Tally(m.sem("ln_eps_added"), 1)
        self.rstd_ready = Tally(m.sem("ln_rstd_ready"), 1)
        self.passed = m.sem("ln_passed")

    def statistics(self, dve, x, n):
        dve.bn_stats(self.stats[:], x).then_inc(self.stats_done.sem, 1)
        self.stats_done.wait_apart(dve, n, 1, self.passed)
        dve.bn_aggr(self.mv[:], self.stats[:]).then_inc(self.mv_ready.sem, 1)

    def on_pool(self, pool, n):
        self.mv_ready.wait_apart(pool, n, 1, self.passed)
        pool.tensor_scalar(self.veps[:], self.mv[:, 1:2], LN_EPS, None, ALU.add).then_inc(self.eps_added.sem, 1)
        self.eps_added.wait(pool, n, 1)
        pool.tensor_tensor(self.rstd[:], self.veps[:], self.minus_half[:, 0:1],
                           ALU.pow).then_inc(self.rstd_ready.sem, 1)

    def apply(self, dve, out, x, n):
        self.rstd_ready.wait(dve, n, 1)
        return dve.tensor_scalar(out, x, self.mv[:, 0:1], self.rstd[:], ALU.subtract, ALU.mult)


F0 = 1024
FC0 = F0 // P
HALF = 512


def quantised_ffn_phase(nc, name, x_src, x_dst, consts, w, gate_col):
    with ExitStack() as ctx:
        m = Space(nc, ctx, name)
        wraw = m.sb("wraw", [P, 3, KC * F0])
        wround = m.sb("wround", [P, KC * F0])
        wt = m.sb("wt", [P, 3, KC * F0], BF16)
        wsum = m.sb("wsum", [P, 3])
        wmean = m.sb("wmean", [P, 3])
        winv = m.sb("winv", [P, 3])
        wfac = m.sb("wfac", [P, 3])
        ones = m.sb("ones", [P, P])
        identb = m.sb("identb", [P, P], BF16)
        xin = m.sb("xin", [P, 2, D])
        xres = m.sb("xres", [P, 2, D])
        xn = m.sb("xn", [P, D])
        amax = m.sb("amax", [P, 2, 1])
        clipped = m.sb("clipped", [P, 2, 1])
        inv = m.sb("inv", [P, 2, 1])
        sc = m.sb("sc", [P, 2, 1])
        fac = m.sb("fac", [P, 2, 2])
        qa = m.sb("qa", [P, D])
        qb = m.sb("qb", [P, D])
        xq = m.sb("xq", [P, D], BF16)
        xqT = m.sb("xqT", [P, KC, P], BF16)
        silu = m.sb("silu", [P, 2, HALF])
        h = m.sb("h", [P, F0])
        ha = m.sb("ha", [P, F0])
        hq = m.sb("hq", [P, F0], BF16)
        hqT = m.sb("hqT", [P, FC0, P], BF16)
        hmax = m.sb("hmax", [P, 1])
        hclip = m.sb("hclip", [P, 1])
        hinv = m.sb("hinv", [P, 1])
        hsc = m.sb("hsc", [P, 1])
        hfac = m.sb("hfac", [P, 2])
        norm = Norm(m, consts)

        ps_g = m.psum("ps_g", [P, 2, HALF])
        ps_u = m.psum("ps_u", [P, 2, HALF])
        ps_x = m.psum("ps_x", [P, 2 * HALF], BF16)
        ps_h = m.psum("ps_h", [P, FC0, P], BF16)
        ps_y = m.psum("ps_y", [P, HALF])
        ps_m = m.psum("ps_m", [P, HALF])

        weights_in = [m.sem(f"weights_in{i}") for i in range(3)]
        sums_ready = m.sem("sums_ready")
        mean_ready = m.sem("mean_ready")
        wstep = m.sem("wstep")
        weights_ready = m.sem("weights_ready")
        loaded = [m.sem("loaded0"), m.sem("loaded1")]
        xres_in = [m.sem("xres_in0"), m.sem("xres_in1")]
        stored = Tally(m.sem("stored"), 16, 16)
        xstep = Tally(m.sem("xstep"), 7)
        xq_ready = Tally(m.sem("xq_ready"), 1)
        xqT_ready = Tally(m.sem("xqT_ready"), 1)
        xqT_copied = Tally(m.sem("xqT_copied"), 1)
        fac_ready = Tally(m.sem("fac_ready"), 1)
        gate_ready = Tally(m.sem("gate_ready"), 2)
        up_ready = Tally(m.sem("up_ready"), 2)
        silu_ready = Tally(m.sem("silu_ready"), 2, 2)
        h_ready = Tally(m.sem("h_ready"), 2, 2)
        hstep = Tally(m.sem("hstep"), 6)
        hq_ready = Tally(m.sem("hq_ready"), 1, 1)
        hqT_ready = Tally(m.sem("hqT_ready"), 1, 1)
        hqT_copied = Tally(m.sem("hqT_copied"), 1)
        y_ready = Tally(m.sem("y_ready"), 1)
        sum_ready = Tally(m.sem("sum_ready"), 1, 1)
        identb_ready = m.sem("identb_ready")
        gate = consts["gates"][:, gate_col:gate_col + 1]
        block = m.block()

        @block.sync
        def _(sp):
            for i, k in enumerate(("gate", "up", "down")):
                sp.dma_start(wraw[:, i], w[k].rearrange("p k n -> p (k n)")).then_inc(weights_in[i], 16)

            def turn(n, par, first=False, last=False, before_last=False):
                if first:
                    sp.dma_start(xin[:, 0], tile_rows(x_src, 0)).then_inc(loaded[0], 16)
                    sp.dma_start(xin[:, 1], tile_rows(x_src, 1)).then_inc(loaded[1], 16)
                if not last and not before_last:
                    xq_ready.wait(sp, n, 1)
                    sp.dma_start(xin[:, par], tile_rows(x_src, n + 2)).then_inc(loaded[par], 16)
                if not first:
                    stored.wait(sp, n, -16)
                sp.dma_start(xres[:, par], tile_rows(x_src, n)).then_inc(xres_in[par], 16)
                if not first:
                    store(n - 1, 1 - par)

            def store(n, par):
                sum_ready.wait(sp, n, 1)
                sp.dma_start(tile_rows(x_dst, n), xres[:, par]).then_inc(stored.sem, 16)

            sp.sem_inc(stored.sem, 16)
            turn(0, 0, first=True)
            with sp.Fori(0, NT // 2 - 2) as pair:
                turn(2 * pair + 1, 1)
                turn(2 * pair + 2, 0)
            turn(NT - 3, 1)
            turn(NT - 2, 0, before_last=True)
            turn(NT - 1, 1, last=True)
            store(NT - 1, 1)
            stored.wait(sp, NT - 1, 16)

        @block.gpsimd
        def _(pool):
            with pool.Fori(0, NT) as n:
                norm.on_pool(pool, n)

        @block.tensor
        def _(pe):
            pe.sem_inc(hqT_ready.sem, 1)
            pe.wait_ge(sums_ready, 1)
            pe.matmul(ps_m[:, 0:3], ones[:], wsum[:], start=True, stop=True).then_inc(mean_ready, 1)
            pe.wait_ge(weights_ready, 1)
            pe.wait_ge(identb_ready, 1)

            def turn_x(n):
                xq_ready.wait(pe, n, 1)
                for k in range(KC):
                    last = pe.transpose(ps_x[:, k * P:(k + 1) * P], xq[:, k * P:(k + 1) * P], identb[:])
                last.then_inc(xqT_ready.sem, 1)

            def gate_up(n):
                xqT_copied.wait(pe, n, 1)
                h_ready.wait(pe, n, 0)
                for c in range(2):
                    for i, bank, ready in ((0, ps_g, gate_ready), (1, ps_u, up_ready)):
                        for k in range(KC):
                            last = pe.matmul(bank[:, c, :], xqT[:, k, :],
                                             wt[:, i, k * F0 + c * HALF:k * F0 + (c + 1) * HALF],
                                             start=(k == 0), stop=(k == KC - 1))
                        last.then_inc(ready.sem, 1)

            def down(n):
                hq_ready.wait(pe, n, 1)
                for f in range(FC0):
                    last = pe.transpose(ps_h[:, f, :], hq[:, f * P:(f + 1) * P], identb[:])
                last.then_inc(hqT_ready.sem, 1)
                hqT_copied.wait(pe, n, 1)
                sum_ready.wait(pe, n, 0)
                for f in range(FC0):
                    last = pe.matmul(ps_y[:, 0:D], hqT[:, f, :], wt[:, 2, f * D:(f + 1) * D],
                                     start=(f == 0), stop=(f == FC0 - 1))
                last.then_inc(y_ready.sem, 1)

            def turn(n, par, first=False, last=False):
                if first:
                    turn_x(0)
                gate_up(n)
                if not last:
                    turn_x(n + 1)
                if not first:
                    down(n - 1)

            tiles(pe, turn)
            down(NT - 1)

        @block.scalar
        def _(act):
            act.sem_inc(silu_ready.sem, 2)
            act.activation(identb[:], consts["ident"][:], ACT.Copy).then_inc(identb_ready, 1)

            def copy_x(n):
                xqT_ready.wait(act, n, 1)
                act.activation(xqT[:].rearrange("p k n -> p (k n)"), ps_x[:, 0:D], ACT.Copy).then_inc(xqT_copied.sem, 1)

            def silus(n, par):
                fac_ready.wait(act, n, 1)
                for c in range(2):
                    gate_ready.wait(act, n, c + 1)
                    h_ready.wait(act, n, c + 1 - 2)
                    act.activation(silu[:, c], ps_g[:, c], ACT.Silu, scale=fac[:, par, 0:1]).then_inc(silu_ready.sem, 1)

            def copy_h(n):
                hqT_ready.wait(act, n, 1)
                act.activation(hqT[:], ps_h[:], ACT.Copy).then_inc(hqT_copied.sem, 1)

            def turn(n, par, first=False, last=False):
                if first:
                    copy_x(0)
                silus(n, par)
                if not last:
                    copy_x(n + 1)
                if not first:
                    copy_h(n - 1)

            tiles(act, turn)
            copy_h(NT - 1)

        @block.vector
        def _(dve):
            dve.sem_inc(h_ready.sem, 2)
            dve.sem_inc(hq_ready.sem, 1)
            dve.sem_inc(sum_ready.sem, 1)
            done = [0]

            def step(ins):
                done[0] += 1
                ins.then_inc(wstep, 1)
                dve.wait_ge(wstep, done[0])

            step(dve.memset(ones[:], 1.0))
            for i in range(3):
                dve.wait_ge(weights_in[i], 16)
                last = dve.tensor_reduce(wsum[:, i:i + 1], wraw[:, i], AX.X, ALU.add, apply_absolute_value=True)
            last.then_inc(sums_ready, 1)
            dve.wait_ge(mean_ready, 1)
            step(dve.tensor_scalar(wmean[:], ps_m[:, 0:3], 1.0 / (D * F0), 1e-5, ALU.mult, ALU.max))
            step(dve.reciprocal(winv[:], wmean[:]))
            step(dve.tensor_scalar(wfac[:], wmean[:], 1.0 / 127.0, None, ALU.mult))
            step(dve.tensor_scalar(wfac[:, 2:3], wfac[:, 2:3], gate, None, ALU.mult))
            for i in range(3):
                step(dve.tensor_scalar(wround[:], wraw[:, i], winv[:, i:i + 1], 1.0, ALU.mult, ALU.min))
                step(dve.tensor_scalar(wround[:], wround[:], -1.0, MAGIC, ALU.max, ALU.add))
                step(dve.tensor_scalar(wt[:, i], wround[:], MAGIC, None, ALU.subtract))
            dve.sem_inc(weights_ready, 1)

            def prepare(n, par):
                dve.wait_ge(loaded[par], tile_times(n, par, 1))
                norm.statistics(dve, xin[:, par], n)
                norm.apply(dve, xn[:], xin[:, par], n).then_inc(xstep.sem, 1)
                xstep.wait(dve, n, 1)
                dve.tensor_reduce(amax[:, par], xn[:], AX.X, ALU.max, apply_absolute_value=True).then_inc(xstep.sem, 1)
                xstep.wait(dve, n, 2)
                dve.tensor_scalar(clipped[:, par], amax[:, par], 1e-5, None, ALU.max).then_inc(xstep.sem, 1)
                xstep.wait(dve, n, 3)
                dve.reciprocal(inv[:, par], clipped[:, par]).then_inc(xstep.sem, 1)
                dve.tensor_scalar(fac[:, par], wfac[:, 0:2], clipped[:, par], None, ALU.mult).then_inc(fac_ready.sem, 1)
                xstep.wait(dve, n, 4)
                dve.tensor_scalar(sc[:, par], inv[:, par], 127.0, None, ALU.mult).then_inc(xstep.sem, 1)
                xstep.wait(dve, n, 5)
                dve.tensor_scalar(qa[:], xn[:], sc[:, par], 127.0, ALU.mult, ALU.min).then_inc(xstep.sem, 1)
                xstep.wait(dve, n, 6)
                dve.tensor_scalar(qb[:], qa[:], -128.0, MAGIC, ALU.max, ALU.add).then_inc(xstep.sem, 1)
                xstep.wait(dve, n, 7)
                dve.tensor_scalar(xq[:], qb[:], MAGIC, None, ALU.subtract).then_inc(xq_ready.sem, 1)

            def hidden(n, par):
                for c in range(2):
                    up_ready.wait(dve, n, c + 1)
                    silu_ready.wait(dve, n, c + 1)
                    dve.scalar_tensor_tensor(h[:, c * HALF:(c + 1) * HALF], ps_u[:, c], fac[:, par, 1:2], silu[:, c],
                                             ALU.mult, ALU.mult).then_inc(h_ready.sem, 1)
                h_ready.wait(dve, n, 2)
                dve.tensor_reduce(hmax[:], h[:], AX.X, ALU.max, apply_absolute_value=True).then_inc(hstep.sem, 1)
                hstep.wait(dve, n, 1)
                dve.tensor_scalar(hclip[:], hmax[:], 1e-5, None, ALU.max).then_inc(hstep.sem, 1)
                hstep.wait(dve, n, 2)
                dve.reciprocal(hinv[:], hclip[:]).then_inc(hstep.sem, 1)
                dve.tensor_scalar(hfac[:, par:par + 1], wfac[:, 2:3], hclip[:], None, ALU.mult)
                hstep.wait(dve, n, 3)
                dve.tensor_scalar(hsc[:], hinv[:], 127.0, None, ALU.mult).then_inc(hstep.sem, 1)
                hstep.wait(dve, n, 4)
                dve.tensor_scalar(ha[:], h[:], hsc[:], 127.0, ALU.mult, ALU.min).then_inc(hstep.sem, 1)
                hstep.wait(dve, n, 5)
                dve.tensor_scalar(ha[:], ha[:], -128.0, MAGIC, ALU.max, ALU.add).then_inc(hstep.sem, 1)
                hstep.wait(dve, n, 6)
                hqT_ready.wait(dve, n, 0)
                dve.tensor_scalar(hq[:], ha[:], MAGIC, None, ALU.subtract).then_inc(hq_ready.sem, 1)

            def add_residual(n, par):
                y_ready.wait(dve, n, 1)
                dve.wait_ge(xres_in[par], tile_times(n, par, 1))
                dve.scalar_tensor_tensor(xres[:, par], ps_y[:, 0:D], hfac[:, par:par + 1], xres[:, par], ALU.mult,
                                         ALU.add).then_inc(sum_ready.sem, 1)

            def turn(n, par, first=False, last=False):
                if first:
                    prepare(0, 0)
                if not last:
                    xqT_ready.wait(dve, n, 1)
                    prepare(n + 1, 1 - par)
                hidden(n, par)
                if not first:
                    add_residual(n - 1, 1 - par)

            tiles(dve, turn)
            add_residual(NT - 1, 1)


FG_ROW = 32
GN_EPS = 1e-5
NORMALISER_EPS = 1e-6
LOWEST = -3.0e38


PART_ROWS = 32


PREPARE = (((1, 4),), ((1, 5),), ((1, 6),), ((1, 7),), ((2, 0),), (), ((2, 1),), ((2, 2), (2, 3)))


def mlstm_phase(nc, name, x_src, x_dst, ctx_dram, consts, w, gate_col, nh, plus_one):
    dh = D // nh
    kh = P // dh
    W = S + P
    G = TB * nh
    GROUPS = 4
    DA = GROUPS * P // nh
    slots = 8 // nh
    qk_scale = 1.0 / float(np.sqrt(dh))
    with ExitStack() as ctx:
        m = Space(nc, ctx, name)
        wg = m.sb("wg", [P, 6, 64])
        ib = m.sb("ib", [nh, 1])
        fb = m.sb("fb", [nh, 1])
        ow = m.sb("ow", [P, D])
        owg = m.sb("owg", [P, D])
        sel = m.sb("sel", [3 * PART_ROWS, nh * P])
        selb = m.sb("selb", [3 * PART_ROWS, nh * P], BF16)
        identb = m.sb("identb", [P, P], BF16)
        lower = m.sb("lower", [P, P])
        lowerb = m.sb("lowerb", [P, P], BF16)
        ones = m.sb("ones", [nh, S])
        xin = m.sb("xin", [P, 2, TB, D])
        cin = m.sb("cin", [P, 2, TB, D])
        xres = m.sb("xres", [P, 2, TB, D])
        stats = m.sb("stats", [P, TB, 6])
        mv = m.sb("mv", [P, TB, 2])
        veps = m.sb("veps", [P, TB])
        rstd = m.sb("rstd", [P, TB])
        xn = m.sb("xn", [P, TB, D])
        xnT = m.sb("xnT", [P, 2, KC, S])
        cT = m.sb("cT", [P, 2, KC, S])
        va = m.sb("va", [P, 2, TB, nh, DA])
        igr = m.sb("igr", [nh, S])
        fgr = m.sb("fgr", [nh, S])
        z = m.sb("z", [nh, S])
        zabs = m.sb("zabs", [nh, S])
        zmin = m.sb("zmin", [nh, S])
        ex = m.sb("ex", [nh, S])
        lg = m.sb("lg", [nh, S])
        logf = m.sb("logf", [nh, S])
        cs = m.sb("cs", [nh, S])
        a = m.sb("a", [nh, S])
        mx = m.sb("mx", [nh, S])
        mlog = m.sb("mlog", [nh, S])
        negm = m.sb("negm", [nh, S])
        negm_rest = m.sb("negm_rest", [nh, S])
        negm_second = m.sb("negm_second", [nh, S], BF16)
        negm_parts = m.sb("negm_parts", [3 * PART_ROWS, 2, S], BF16)
        e = m.sb("e", [nh, S])
        aT = m.sb("aT", [P, 2, 2, TB, nh])
        decay = m.sb("decay", [P, 2, W])
        c = m.sb("c", [P, 2, W])
        o_raw = m.sb("o_raw", [P, GROUPS, S])
        den = m.sb("den", [P, TB, nh])
        rden = m.sb("rden", [P, TB, nh])
        hn = m.sb("hn", [P, TB, nh, dh])
        sq = m.sb("sq", [P, TB, nh, dh])
        msum = m.sb("msum", [P, G])
        mean = m.sb("mean", [P, G])
        vsum = m.sb("vsum", [P, G])
        gveps = m.sb("gveps", [P, G])
        grstd = m.sb("grstd", [P, G])

        ps_q = m.psum("ps_q", [P, 2, 512])
        ps_m = m.psum("ps_m", [P, 2, 512])
        ps_o = m.psum("ps_o", [P, GROUPS, S])
        ps_w = m.psum("ps_w", [P, 2, TB, S])

        weights_in = m.sem("weights_in")
        wstep = m.sem("wstep")
        constants_ready = m.sem("constants_ready")
        loaded = [m.sem("loaded0"), m.sem("loaded1")]
        xres_in = [m.sem("xres_in0"), m.sem("xres_in1")]
        stored = Tally(m.sem("stored"), 16, 16)
        stats_done = Tally(m.sem("stats_done"), 1)
        mv_ready = Tally(m.sem("mv_ready"), 1)
        eps_added = Tally(m.sem("eps_added"), 1)
        rstd_ready = Tally(m.sem("rstd_ready"), 1)
        xn_ready = Tally(m.sem("xn_ready"), 1)
        va_ready = Tally(m.sem("va_ready"), 1)
        work_filled = Tally(m.sem("work_filled"), 4)
        act_drained = Tally(m.sem("act_drained"), 3)
        z_ready = Tally(m.sem("z_ready"), 1)
        ex_ready = Tally(m.sem("ex_ready"), 1)
        lg_ready = Tally(m.sem("lg_ready"), 1)
        gstep = Tally(m.sem("gstep"), 6)
        negm_ready = Tally(m.sem("negm_ready"), 1)
        part_step = Tally(m.sem("part_step"), 3)
        parts_ready = Tally(m.sem("parts_ready"), 2)
        mlog_ready = Tally(m.sem("mlog_ready"), 1)
        e_ready = Tally(m.sem("e_ready"), 1)
        aT_ready = Tally(m.sem("aT_ready"), 1, 1)
        scores_ready = Tally(m.sem("scores_ready"), nh)
        m_ready = Tally(m.sem("m_ready"), nh)
        decay_ready = Tally(m.sem("decay_ready"), nh, 2)
        c_ready = Tally(m.sem("c_ready"), nh, 2)
        head_done = Tally(m.sem("head_done"), nh, 2)
        estep = Tally(m.sem("estep"), 10)
        o_unloaded = Tally(m.sem("o_unloaded"), 1)
        o_turned = Tally(m.sem("o_turned"), 1)
        out_read = Tally(m.sem("out_read"), 1, 1)
        vsum_ready = Tally(m.sem("vsum_ready"), 1)
        geps_added = Tally(m.sem("geps_added"), 1)
        grstd_ready = Tally(m.sem("grstd_ready"), 1)
        sum_ready = Tally(m.sem("sum_ready"), 1)
        passed = m.sem("passed")
        ident = consts["ident"]
        minus_half = consts["minus_half"]
        gate = consts["gates"][:, gate_col:gate_col + 1]
        outs = ps_o[:].rearrange("p (t a) s -> p t (a s)", t=TB)
        block = m.block()

        def prepare_ahead(prepare, b, par, h, last, before_last):
            for steps in PREPARE[h * slots:(h + 1) * slots]:
                for ahead, step in steps:
                    if not last and not (before_last and ahead == 2):
                        prepare(b + ahead, (par + ahead) % 2, step)

        def prepare_first(prepare):
            for step in range(8):
                prepare(0, 0, step)
            for step in range(4):
                prepare(1, 1, step)

        @block.sync
        def _(sp):
            sp.dma_start(wg[:], w["gates"]).then_inc(weights_in, 16)
            sp.dma_start(ib[:], w["ib"]).then_inc(weights_in, 16)
            sp.dma_start(fb[:], w["fb"]).then_inc(weights_in, 16)
            sp.dma_start(ow[:], w["ow"].broadcast_to([P, D])).then_inc(weights_in, 16)
            sp.dma_start(sel[:], w["sel"]).then_inc(weights_in, 16)
            sp.dma_start(lower[:], w["lower"]).then_inc(weights_in, 16)

            def load(b, par):
                sp.dma_start(xin[:, par], rows(x_src, b)).then_inc(loaded[par], 16)
                sp.dma_start(cin[:, par], rows(ctx_dram, b)).then_inc(loaded[par], 16)

            def store(b, par):
                sum_ready.wait(sp, b, 1)
                sp.dma_start(rows(x_dst, b), xres[:, par]).then_inc(stored.sem, 16)

            def turn(b, par, first=False, last=False, before_last=False):
                if not last and not before_last:
                    act_drained.wait_apart(sp, b, 2, passed)
                    va_ready.wait_apart(sp, b, 1, passed)
                    load(b + 2, par)
                if not first:
                    stored.wait(sp, b, -16)
                sp.dma_start(xres[:, par], rows(x_src, b)).then_inc(xres_in[par], 16)
                if not first:
                    store(b - 1, 1 - par)

            sp.sem_inc(stored.sem, 16)
            load(0, 0)
            load(1, 1)
            batches(sp, turn)
            store(B - 1, 1)
            stored.wait(sp, B - 1, 16)

        @block.gpsimd
        def _(pool):
            def layer(b):
                mv_ready.wait_apart(pool, b, 1, passed)
                pool.tensor_scalar(veps[:], mv[:, :, 1], LN_EPS, None, ALU.add).then_inc(eps_added.sem, 1)
                eps_added.wait(pool, b, 1)
                pool.tensor_tensor(rstd[:], veps[:], minus_half[:, 0:TB], ALU.pow).then_inc(rstd_ready.sem, 1)

            def group(b):
                vsum_ready.wait_apart(pool, b, 1, passed)
                pool.tensor_scalar(gveps[:], vsum[:], 1.0 / dh, GN_EPS, ALU.mult,
                                   ALU.add).then_inc(geps_added.sem, 1)
                geps_added.wait(pool, b, 1)
                pool.tensor_tensor(grstd[:], gveps[:], minus_half[:, 0:G], ALU.pow).then_inc(grstd_ready.sem, 1)

            def values(b, par):
                pool.wait_ge(loaded[par], load_times(b, par, 2))
                pool.sem_inc(passed, 1)
                pool.tensor_copy(va[:, par, :, :, 0:dh],
                                 cin[:, par].rearrange("p t (h d) -> p t h d", d=dh)).then_inc(va_ready.sem, 1)

            def turn(b, par, first=False, last=False, before_last=False):
                if not last:
                    if not first:
                        head_done.wait_apart(pool, b - 1, nh, passed)
                    values(b + 1, 1 - par)
                if not first:
                    group(b - 1)
                if not last and not before_last:
                    layer(b + 2)

            pool.wait_ge(wstep, 1)
            layer(0)
            values(0, 0)
            layer(1)
            batches(pool, turn)
            group(B - 1)

        @block.tensor
        def _(pe):
            pe.sem_inc(head_done.sem, 2)
            pe.wait_ge(weights_in, 96)
            pe.wait_ge(constants_ready, 1)

            def transposes(dst, src):
                for k in range(KC):
                    for t in range(TB):
                        last = pe.transpose(dst[:, k, t * P:(t + 1) * P], src[:, t, k * P:(k + 1) * P], ident[:])
                return last

            def prepare(b, par, j):
                if j == 1:
                    xn_ready.wait(pe, b, 1)
                    act_drained.wait(pe, b, 0)
                    transposes(ps_w[:, 0], xn).then_inc(work_filled.sem, 1)
                if j == 2:
                    pe.wait_ge(loaded[par], load_times(b, par, 2))
                    aT_ready.wait(pe, b, 0)
                    transposes(ps_w[:, 1], cin[:, par]).then_inc(work_filled.sem, 1)
                if j == 3:
                    act_drained.wait(pe, b, 2)
                    for k in range(6):
                        src = xnT[:, par, k, :] if k < KC else cT[:, par, k % KC, :]
                        last = pe.matmul(ps_w[0:64, 0, 0, :], wg[:, k, :], src, start=(k == 0), stop=(k == 5))
                    last.then_inc(work_filled.sem, 1)
                if j == 7:
                    e_ready.wait_apart(pe, b, 1, passed)
                    for i, src in enumerate((a, e)):
                        for t in range(TB):
                            at = (i * TB + t) * nh
                            last = pe.transpose(ps_w[:, 1, 0, at:at + nh], src[:, t * P:(t + 1) * P],
                                                ident[0:nh, 0:nh])
                    last.then_inc(work_filled.sem, 1)

            def scores(b, par, h):
                if h == 0:
                    parts_ready.wait(pe, b, 2)
                k, r = h // kh, dh * (h % kh)
                c_ready.wait(pe, b, h - 1)
                pe.matmul(ps_q[:, h % 2, 0:S], cT[r:r + dh, par, k, 0:P], xnT[r:r + dh, par, k, :],
                          start=True, stop=True)
                pe.matmul(ps_q[:, h % 2, S:W], cT[r:r + dh, par, k, P:S], xnT[r:r + dh, par, k, P:S],
                          start=True, stop=True).then_inc(scores_ready.sem, 1)
                decay_ready.wait(pe, b, h - 1)
                row = selb[:, h * P:(h + 1) * P]
                pe.matmul(ps_m[:, h % 2, 0:S], row, negm_parts[:, par, :], start=True, stop=False, skip_group_check=True)
                pe.matmul(ps_m[:, h % 2, S:W], row, negm_parts[:, par, P:S], start=False, stop=False,
                          skip_group_check=True)
                for at in (0, S):
                    last = pe.matmul(ps_m[:, h % 2, at:at + P], identb[:], lowerb[:], start=False, stop=True,
                                     skip_group_check=True)
                last.then_inc(m_ready.sem, 1)

            def weigh(b, par, h):
                c_ready.wait(pe, b, h + 1)
                if h == 0:
                    out_read.wait(pe, b, 0)
                    va_ready.wait(pe, b, 1)
                at, g = h * DA % P, h * DA // P
                pe.matmul(ps_o[at:at + DA, g, :], va[:, par, 0, h, :], c[:, h % 2, 0:S], start=True, stop=False,
                          skip_group_check=True)
                pe.matmul(ps_o[at:at + DA, g, P:S], va[:, par, 1, h, :], c[:, h % 2, S:W], start=False, stop=True,
                          skip_group_check=True).then_inc(head_done.sem, 1)

            def turn_outputs(b):
                o_unloaded.wait(pe, b, 1)
                for t in range(TB):
                    for g in range(GROUPS):
                        last = pe.transpose(outs[:, t, g * P:(g + 1) * P], o_raw[:, g, t * P:(t + 1) * P], ident[:])
                last.then_inc(o_turned.sem, 1)

            def turn(b, par, first=False, last=False, before_last=False):
                for h in range(nh):
                    if h < nh - 1:
                        scores(b, par, h + 1)
                    if h == 0 and not first:
                        turn_outputs(b - 1)
                    if h:
                        weigh(b, par, h - 1)
                    prepare_ahead(prepare, b, par, h, last, before_last)
                if not last:
                    scores(b + 1, 1 - par, 0)
                weigh(b, par, nh - 1)

            prepare_first(prepare)
            scores(0, 0, 0)
            batches(pe, turn)
            turn_outputs(B - 1)

        @block.scalar
        def _(act):
            act.sem_inc(decay_ready.sem, 2)
            act.wait_ge(weights_in, 96)
            act.activation(identb[:], ident[:], ACT.Copy)
            act.activation(selb[:], sel[:], ACT.Copy)
            act.activation(lowerb[:], lower[:], ACT.Copy).then_inc(constants_ready, 1)

            def prepare(b, par, j):
                if j == 1 or j == 2:
                    work_filled.wait(act, b, j)
                    dst = xnT if j == 1 else cT
                    act.activation(dst[:, par], ps_w[:, j - 1], ACT.Copy).then_inc(act_drained.sem, 1)
                if j == 3:
                    work_filled.wait(act, b, 3)
                    act.activation(igr[:], ps_w[0:nh, 0, 0, :], ACT.Copy)
                    act.activation(fgr[:], ps_w[FG_ROW:FG_ROW + nh, 0, 0, :], ACT.Copy).then_inc(act_drained.sem, 1)
                if j == 4:
                    z_ready.wait(act, b, 1)
                    act.activation(ex[:], zabs[:], ACT.Exp).then_inc(ex_ready.sem, 1)
                    ex_ready.wait(act, b, 1)
                    act.activation(lg[:], ex[:], ACT.Ln, bias=1.0).then_inc(lg_ready.sem, 1)
                if j == 6:
                    mlog_ready.wait(act, b, 1)
                    act.activation(e[:], mlog[:], ACT.Exp, scale=-1.0).then_inc(e_ready.sem, 1)

            def decays(b, par, h):
                m_ready.wait(act, b, h + 1)
                if h == 0:
                    aT_ready.wait(act, b, 1)
                c_ready.wait(act, b, h - 1)
                act.activation(decay[:, h % 2, 0:S], ps_m[:, h % 2, 0:S], ACT.Exp, bias=aT[:, par, 0, 0, h:h + 1])
                act.activation(decay[:, h % 2, S:W], ps_m[:, h % 2, S:W], ACT.Exp,
                               bias=aT[:, par, 0, 1, h:h + 1]).then_inc(decay_ready.sem, 1)

            def unload(b):
                head_done.wait(act, b, nh)
                act.activation(o_raw[:], ps_o[:], ACT.Copy).then_inc(o_unloaded.sem, 1)

            def turn(b, par, first=False, last=False, before_last=False):
                if not first:
                    unload(b - 1)
                for h in range(nh):
                    decays(b, par, h)
                    prepare_ahead(prepare, b, par, h, last, before_last)

            prepare_first(prepare)
            batches(act, turn)
            unload(B - 1)

        @block.vector
        def _(dve):
            dve.sem_inc(c_ready.sem, 2)
            dve.sem_inc(out_read.sem, 1)
            dve.sem_inc(aT_ready.sem, 1)
            dve.memset(ones[:], 1.0)
            dve.memset(negm_parts[:], 0.0)
            dve.memset(va[:], 1.0).then_inc(wstep, 1)
            dve.wait_ge(weights_in, 96)
            dve.wait_ge(wstep, 1)
            dve.tensor_scalar(owg[:], ow[:], 1.0 if plus_one else 0.0, gate, ALU.add,
                              ALU.mult).then_inc(wstep, 1)
            dve.wait_ge(wstep, 2)

            def prepare(b, par, j):
                if j == 0:
                    dve.wait_ge(loaded[par], load_times(b, par, 2))
                    for t in range(TB):
                        last = dve.bn_stats(stats[:, t, :], xin[:, par, t, :])
                    last.then_inc(stats_done.sem, 1)
                    stats_done.wait_apart(dve, b, 1, passed)
                    for t in range(TB):
                        last = dve.bn_aggr(mv[:, t, :], stats[:, t, :])
                    last.then_inc(mv_ready.sem, 1)
                if j == 1:
                    rstd_ready.wait(dve, b, 1)
                    for t in range(TB):
                        last = dve.tensor_scalar(xn[:, t, :], xin[:, par, t, :], mv[:, t, 0:1], rstd[:, t:t + 1],
                                                 ALU.subtract, ALU.mult)
                    last.then_inc(xn_ready.sem, 1)
                if j == 3:
                    act_drained.wait(dve, b, 3)
                    dve.tensor_scalar(z[:], fgr[:], fb[:], None, ALU.add).then_inc(gstep.sem, 1)
                    dve.tensor_scalar(zmin[:], fgr[:], fb[:], 0.0, ALU.add, ALU.min).then_inc(gstep.sem, 1)
                    gstep.wait(dve, b, 2)
                    dve.scalar_tensor_tensor(zabs[:], zmin[:], 2.0, z[:], ALU.mult,
                                             ALU.subtract).then_inc(z_ready.sem, 1)
                if j == 4:
                    lg_ready.wait(dve, b, 1)
                    dve.tensor_tensor(logf[:], zmin[:], lg[:], ALU.subtract).then_inc(gstep.sem, 1)
                    gstep.wait(dve, b, 3)
                    dve.tensor_tensor_scan(cs[:], ones[:], logf[:], 0.0, ALU.mult, ALU.add).then_inc(gstep.sem, 1)
                    gstep.wait(dve, b, 4)
                    aT_ready.wait(dve, b, 0)
                    dve.scalar_tensor_tensor(a[:], igr[:], ib[:], cs[:], ALU.add, ALU.subtract).then_inc(gstep.sem, 1)
                if j == 5:
                    gstep.wait(dve, b, 5)
                    dve.tensor_tensor_scan(mx[:], a[:], a[:], LOWEST, ALU.max, ALU.max).then_inc(gstep.sem, 1)
                    gstep.wait(dve, b, 6)
                    dve.tensor_scalar(negm[:], mx[:], -1.0, None, ALU.mult).then_inc(negm_ready.sem, 1)
                    dve.tensor_tensor(mlog[:], mx[:], cs[:], ALU.add).then_inc(mlog_ready.sem, 1)
                    negm_ready.wait(dve, b, 1)
                    dve.tensor_copy(negm_parts[0:nh, par], negm[:]).then_inc(part_step.sem, 1)
                    part_step.wait(dve, b, 1)
                    dve.tensor_tensor(negm_rest[:], negm[:], negm_parts[0:nh, par], ALU.subtract
                                      ).then_inc(part_step.sem, 1)
                if j == 6:
                    part_step.wait(dve, b, 2)
                    dve.tensor_copy(negm_second[:], negm_rest[:]).then_inc(part_step.sem, 1)
                    part_step.wait(dve, b, 3)
                    dve.tensor_copy(negm_parts[PART_ROWS:PART_ROWS + nh, par], negm_second[:]
                                    ).then_inc(parts_ready.sem, 1)
                    dve.tensor_tensor(negm_parts[2 * PART_ROWS:2 * PART_ROWS + nh, par], negm_rest[:], negm_second[:],
                                      ALU.subtract).then_inc(parts_ready.sem, 1)
                if j == 7:
                    work_filled.wait(dve, b, 4)
                    dve.tensor_copy(aT[:, par].rearrange("p i t h -> p (i t h)"),
                                    ps_w[:, 1, 0, 0:2 * G]).then_inc(aT_ready.sem, 1)

            def combine(b, par, h):
                scores_ready.wait(dve, b, h + 1)
                decay_ready.wait(dve, b, h + 1)
                head_done.wait(dve, b, h - 1)
                dve.scalar_tensor_tensor(c[:, h % 2, :], ps_q[:, h % 2, 0:W], qk_scale, decay[:, h % 2, :],
                                         ALU.mult, ALU.mult).then_inc(c_ready.sem, 1)

            def spread(x):
                return x.unsqueeze(2).broadcast_to([P, G, dh])

            def divide(b, par):
                o_turned.wait(dve, b, 1)
                heads = outs.rearrange("p t (h d) -> p t h d", d=DA)
                total = heads[:, :, :, dh]
                dve.scalar_tensor_tensor(den[:], total, -1.0, aT[:, par, 1], ALU.mult, ALU.max).then_inc(estep.sem, 1)
                estep.wait(dve, b, 1)
                dve.tensor_tensor(den[:], total, den[:], ALU.max).then_inc(estep.sem, 1)
                estep.wait(dve, b, 2)
                dve.tensor_scalar(den[:], den[:], NORMALISER_EPS, None, ALU.add).then_inc(estep.sem, 1)
                estep.wait(dve, b, 3)
                dve.reciprocal(rden[:], den[:]).then_inc(estep.sem, 1)
                estep.wait(dve, b, 4)
                dve.tensor_tensor(hn[:], heads[:, :, :, 0:dh], rden[:].unsqueeze(3).broadcast_to([P, TB, nh, dh]),
                                  ALU.mult).then_inc(out_read.sem, 1)

            def group_statistics(b):
                flat = hn[:].rearrange("p t h d -> p (t h) d")
                out_read.wait(dve, b, 1)
                dve.tensor_reduce(msum[:], flat, AX.X, ALU.add).then_inc(estep.sem, 1)
                estep.wait(dve, b, 5)
                dve.tensor_scalar(mean[:], msum[:], 1.0 / dh, None, ALU.mult).then_inc(estep.sem, 1)
                estep.wait(dve, b, 6)
                dve.tensor_tensor(flat, flat, spread(mean[:]), ALU.subtract).then_inc(estep.sem, 1)

            def group_squares(b):
                estep.wait(dve, b, 7)
                dve.tensor_tensor(sq[:], hn[:], hn[:], ALU.mult).then_inc(estep.sem, 1)
                estep.wait(dve, b, 8)
                dve.tensor_reduce(vsum[:], sq[:].rearrange("p t h d -> p (t h) d"), AX.X,
                                  ALU.add).then_inc(vsum_ready.sem, 1)

            def add_residual(b, par):
                flat = hn[:].rearrange("p t h d -> p (t h) d")
                rowsv = hn[:].rearrange("p t h d -> p t (h d)")
                grstd_ready.wait(dve, b, 1)
                dve.tensor_tensor(flat, flat, spread(grstd[:]), ALU.mult).then_inc(estep.sem, 1)
                estep.wait(dve, b, 9)
                dve.tensor_tensor(rowsv, rowsv, owg[:].unsqueeze(1).broadcast_to([P, TB, D]),
                                  ALU.mult).then_inc(estep.sem, 1)
                dve.wait_ge(xres_in[par], load_times(b, par, 1))
                estep.wait(dve, b, 10)
                dve.tensor_tensor(xres[:, par], rowsv, xres[:, par], ALU.add).then_inc(sum_ready.sem, 1)

            def finish(b, par, j):
                if j == 0:
                    divide(b, par)
                if j == 1:
                    group_statistics(b)
                if j == 2:
                    group_squares(b)
                if j == 6:
                    add_residual(b, par)

            def turn(b, par, first=False, last=False, before_last=False):
                for h in range(nh):
                    combine(b, par, h)
                    steps = range(h * slots, (h + 1) * slots)
                    for j in steps:
                        if not first and j < 6:
                            finish(b - 1, 1 - par, j)
                    prepare_ahead(prepare, b, par, h, last, before_last)
                    for j in steps:
                        if not first and j >= 6:
                            finish(b - 1, 1 - par, j)

            prepare_first(prepare)
            batches(dve, turn)
            for j in range(8):
                finish(B - 1, 1, j)


E = 8


def sorted_tiles(choices):
    return (choices * B * S + E * (P - 1)) // P


MAX_TILES = sorted_tiles(2)


class Running:

    def __init__(self, m, name):
        self.sem, self.before = m.sem(name), 0

    def target(self, dmas):
        self.before += 16 * dmas
        return self.before


class Routing:

    def __init__(self, m, choices):
        self.slot = m.sb("slot", [P, choices * NT], U32)
        self.weight = m.sb("weight", [P, choices, NT])
        self.expert = m.sb("expert", [P, MAX_TILES], I32)


class BatchNorm:

    def __init__(self, m, consts, name):
        self.stats = m.sb(name + "_stats", [P, 2, TB, 6])
        self.mv = m.sb(name + "_mv", [P, 2, TB, 2])
        self.veps = m.sb(name + "_veps", [P, 2, TB])
        self.rstd = m.sb(name + "_rstd", [P, 2, TB])
        self.minus_half = consts["minus_half"]
        self.stats_done = Tally(m.sem(name + "_stats_done"), 1)
        self.mv_ready = Tally(m.sem(name + "_mv_ready"), 1)
        self.eps_added = Tally(m.sem(name + "_eps_added"), 1)
        self.rstd_ready = Tally(m.sem(name + "_rstd_ready"), 1)
        self.passed = m.sem(name + "_passed")

    def statistics(self, dve, x, b, par):
        for t in range(TB):
            last = dve.bn_stats(self.stats[:, par, t, :], x(t))
        last.then_inc(self.stats_done.sem, 1)
        self.stats_done.wait_apart(dve, b, 1, self.passed)
        for t in range(TB):
            last = dve.bn_aggr(self.mv[:, par, t, :], self.stats[:, par, t, :])
        last.then_inc(self.mv_ready.sem, 1)

    def on_pool(self, pool, b, par):
        self.mv_ready.wait_apart(pool, b, 1, self.passed)
        pool.tensor_scalar(self.veps[:, par], self.mv[:, par, :, 1], LN_EPS, None, ALU.add).then_inc(self.eps_added.sem, 1)
        self.eps_added.wait(pool, b, 1)
        pool.tensor_tensor(self.rstd[:, par], self.veps[:, par], self.minus_half[:, 0:TB],
                           ALU.pow).then_inc(self.rstd_ready.sem, 1)

    def apply(self, dve, out, x, b, par):
        self.rstd_ready.wait_apart(dve, b, 1, self.passed)
        for t in range(TB):
            last = dve.tensor_scalar(out(t), x(t), self.mv[:, par, t, 0:1], self.rstd[:, par, t:t + 1],
                                     ALU.subtract, ALU.mult)
        return last


def route_phase(nc, name, x_src, xn_dst, sorted_dst, consts, w, routing, choices, tiles_used, experts,
                alpha, none_expert, second_norm):
    J = choices * NT
    with ExitStack() as ctx:
        m = Space(nc, ctx, name)
        wr = m.sb("wr", [P, KC, E])
        eidx = m.sb("eidx", [P, E])
        before = m.sb("before", [P, P])
        tidx = m.sb("tidx", [P, MAX_TILES])
        least = m.sb("least", [P, MAX_TILES])
        gamma = m.sb("gamma", [P, D]) if second_norm else None
        beta = m.sb("beta", [P, D]) if second_norm else None
        ones = m.sb("ones", [P, P])
        ones_row = m.sb("ones_row", [P, E * J])
        xin = m.sb("xin", [P, NT, D])
        rn = m.sb("rn", [P, 2, TB, D]) if second_norm else None
        xnT = m.sb("xnT", [P, 2, TB, KC, P])
        logits = m.sb("logits", [P, NT, E])
        xall = m.sb("xall", [P, NT, D])
        norm = BatchNorm(m, consts, "ln")
        again = BatchNorm(m, consts, "again") if second_norm else None
        top = m.sb("top", [P, choices, NT])
        ex = m.sb("ex", [P, NT, E])
        total = m.sb("total", [P, NT])
        eq = m.sb("eq", [P, NT, E])
        key = m.sb("key", [P, NT, E])
        least_key = m.sb("least_key", [P, NT])
        chosen = m.sb("chosen", [P, E, J])
        earlier = m.sb("earlier", [P, E, J])
        incl = m.sb("incl", [P, E, J])
        excl = m.sb("excl", [P, E, J])
        totals = m.sb("totals", [P, E, J])
        cnt = m.sb("cnt", [P, E])
        ntiles = m.sb("ntiles", [P, E])
        end = m.sb("end", [P, E])
        adj = m.sb("adj", [P, E])
        slotf = m.sb("slotf", [P, J])
        past = m.sb("past", [P, MAX_TILES, E])
        expf = m.sb("expf", [P, MAX_TILES])
        flag = m.sb("flag", [P, NT])

        ps_x = m.psum("ps_x", [P, 2, TB, KC, P])
        ps_l = m.psum("ps_l", [P, 512])
        ps_e = m.psum("ps_e", [P, 512])
        ps_t = m.psum("ps_t", [P, 512])

        weights_in = m.sem("weights_in")
        loaded = [m.sem("loaded0"), m.sem("loaded1")]
        norm_stored = m.sem("norm_stored")
        xn_ready = Tally(m.sem("xn_ready"), 1)
        rn_step = Tally(m.sem("rn_step"), 2)
        rn_ready = Tally(m.sem("rn_ready"), 1)
        xnT_ready = Tally(m.sem("xnT_ready"), 1, 2)
        xnT_copied = Tally(m.sem("xnT_copied"), 1)
        logits_ready = Tally(m.sem("logits_ready"), 1)
        step_done = m.sem("step_done")
        exponent_in = m.sem("exponent_in")
        exponent_out = m.sem("exponent_out")
        chosen_ready = m.sem("chosen_ready")
        counted = m.sem("counted")
        slots_ready = m.sem("slots_ready")
        scattered = w["scattered"].sem
        all_scattered = w["scattered"].target(J)
        ident = consts["ident"]
        gate = w["gate"]
        nweights = 5 + (2 if second_norm else 0)
        passed = m.sem("passed")
        block = m.block()

        def logits_out(b, t):
            return ps_l[:, 0:NT * E].rearrange("p (n e) -> p n e", e=E)[:, b * TB + t, :]

        @block.sync
        def _(sp):
            for b in range(B):
                if b >= 2:
                    sp.wait_ge(loaded[b % 2], 16 * (b // 2))
                sp.dma_start(xin[:, b * TB:(b + 1) * TB], rows(x_src, b)).then_inc(loaded[b % 2], 16)
                if b == 1:
                    sp.dma_start(wr[:], w["router"]).then_inc(weights_in, 16)
                    sp.dma_start(eidx[:], w["eidx"]).then_inc(weights_in, 16)
                    sp.dma_start(before[:], w["before"]).then_inc(weights_in, 16)
                    sp.dma_start(tidx[:], w["tidx"]).then_inc(weights_in, 16)
                    sp.dma_start(least[:], w["least"]).then_inc(weights_in, 16)
                    if second_norm:
                        sp.dma_start(gamma[:], w["gamma"].broadcast_to([P, D])).then_inc(weights_in, 16)
                        sp.dma_start(beta[:], w["beta"].broadcast_to([P, D])).then_inc(weights_in, 16)
            if xn_dst is not None:
                for b in range(B):
                    xn_ready.wait(sp, b, 1)
                    sp.dma_start(xn_dst[b * TB:(b + 1) * TB].rearrange("n p d -> p n d"),
                                 xall[:, b * TB:(b + 1) * TB]).then_inc(norm_stored, 16)
                sp.wait_ge(norm_stored, 16 * B)

        @block.gpsimd
        def _(pool):
            def turn(b, par, first=False, last=False, before_last=False):
                if not last:
                    norm.on_pool(pool, b + 1, 1 - par)
                if second_norm:
                    again.on_pool(pool, b, par)

            norm.on_pool(pool, 0, 0)
            batches(pool, turn)
            xn_ready.wait(pool, B - 1, 1)
            pool.wait_ge(slots_ready, 1)
            for c in range(choices):
                for n in range(NT):
                    j = c * NT + n
                    pool.indirect_dma_start(
                        out=sorted_dst, out_offset=bass.IndirectOffsetOnAxis(ap=routing.slot[:, j:j + 1], axis=0),
                        in_=xall[:, n, :], in_offset=None).then_inc(scattered, 16)
            pool.wait_ge(scattered, all_scattered)

        @block.tensor
        def _(pe):
            pe.sem_inc(xnT_ready.sem, 2)
            pe.wait_ge(weights_in, 16 * nweights)

            def logits_of(b, par):
                xnT_copied.wait(pe, b, 1)
                for t in range(TB):
                    for k in range(KC):
                        last_m = pe.matmul(logits_out(b, t), xnT[:, par, t, k, :], wr[:, k, :],
                                           start=(k == 0), stop=(k == KC - 1))
                last_m.then_inc(logits_ready.sem, 1)

            def turn(b, par, first):
                (rn_ready if second_norm else xn_ready).wait(pe, b, 1)
                for t in range(TB):
                    src = rn[:, par, t] if second_norm else xall[:, b * TB + t]
                    for k in range(KC):
                        last_t = pe.transpose(ps_x[:, par, t, k, :], src[:, k * P:(k + 1) * P], ident[:])
                last_t.then_inc(xnT_ready.sem, 1)
                if not first:
                    logits_of(b - 1, 1 - par)

            for b in range(B):
                turn(b, b % 2, first=(b == 0))
            logits_of(B - 1, 1)
            pe.wait_ge(chosen_ready, 1)
            flat = chosen[:].rearrange("p e j -> p (e j)")
            pe.matmul(ps_e[:, 0:E * J], before[:], flat, start=True, stop=True)
            pe.matmul(ps_t[:, 0:E * J], ones[:], flat, start=True, stop=True).then_inc(counted, 1)

        @block.scalar
        def _(act):
            def turn(b, par, first=False, last=False, before_last=False):
                xnT_ready.wait(act, b, 1)
                act.activation(xnT[:, par], ps_x[:, par], ACT.Copy).then_inc(xnT_copied.sem, 1)

            batches(act, turn)
            act.wait_ge(exponent_in, 1)
            act.activation(ex[:], logits[:], ACT.Exp).then_inc(exponent_out, 1)

        @block.vector
        def _(dve):
            done = [0]

            def step(ins):
                done[0] += 1
                ins.then_inc(step_done, 1)
                dve.wait_ge(step_done, done[0])

            step(dve.memset(ones[:], 1.0))
            step(dve.memset(ones_row[:], 1.0))

            def tile_of(x, b):
                return lambda t: x[:, b * TB + t]

            def statistics(b, par):
                dve.wait_ge(loaded[par], load_times(b, par, 1))
                dve.sem_inc(passed, 1)
                norm.statistics(dve, tile_of(xin, b), b, par)

            def second(b, par):
                mine = rn[:, par]
                xnT_ready.wait_apart(dve, b, -1, passed)
                again.apply(dve, lambda t: rn[:, par, t], tile_of(xall, b), b, par).then_inc(rn_step.sem, 1)
                rn_step.wait(dve, b, 1)
                dve.tensor_tensor(mine, mine, gamma[:].unsqueeze(1).broadcast_to([P, TB, D]),
                                  ALU.mult).then_inc(rn_step.sem, 1)
                rn_step.wait(dve, b, 2)
                dve.tensor_tensor(mine, mine, beta[:].unsqueeze(1).broadcast_to([P, TB, D]),
                                  ALU.add).then_inc(rn_ready.sem, 1)

            def turn(b, par, first=False, last=False, before_last=False):
                if not last:
                    statistics(b + 1, 1 - par)
                norm.apply(dve, tile_of(xall, b), tile_of(xin, b), b, par).then_inc(xn_ready.sem, 1)
                if second_norm:
                    if not first:
                        second(b - 1, 1 - par)
                    xn_ready.wait_apart(dve, b, 1, passed)
                    again.statistics(dve, tile_of(xall, b), b, par)

            statistics(0, 0)
            if second_norm:
                dve.wait_ge(weights_in, 16 * nweights)
            batches(dve, turn)
            if second_norm:
                second(B - 1, 1)
            dve.wait_ge(weights_in, 16 * nweights)
            logits_ready.wait(dve, B - 1, 1)
            step(dve.tensor_copy(logits[:], ps_l[:, 0:NT * E].rearrange("p (n e) -> p n e", e=E)))

            def over_experts(x):
                return x.unsqueeze(2).broadcast_to([P, NT, E])

            step(dve.tensor_reduce(total[:], logits[:], AX.X, ALU.max))
            dve.tensor_tensor(logits[:], logits[:], over_experts(total[:]), ALU.subtract).then_inc(exponent_in, 1)
            dve.wait_ge(exponent_out, 1)
            step(dve.tensor_reduce(total[:], ex[:], AX.X, ALU.add))
            step(dve.reciprocal(total[:], total[:]))
            step(dve.tensor_tensor(ex[:], ex[:], over_experts(total[:]), ALU.mult))
            eids = eidx[:].unsqueeze(1).broadcast_to([P, NT, E])
            for c in range(choices):
                step(dve.tensor_reduce(top[:, c], ex[:], AX.X, ALU.max))
                step(dve.tensor_tensor(eq[:], ex[:], over_experts(top[:, c]), ALU.is_equal))
                step(dve.scalar_tensor_tensor(key[:], eq[:], -2.0 * E, eids, ALU.mult, ALU.add))
                step(dve.tensor_reduce(least_key[:], key[:], AX.X, ALU.min))
                mine = chosen[:, :, c * NT:(c + 1) * NT].rearrange("p e n -> p n e")
                step(dve.tensor_tensor(mine, key[:], over_experts(least_key[:]), ALU.is_equal))
                if c < choices - 1:
                    step(dve.scalar_tensor_tensor(ex[:], mine, -4.0, ex[:], ALU.mult, ALU.add))
                if none_expert:
                    step(dve.tensor_scalar(flag[:], chosen[:, E - 1, c * NT:(c + 1) * NT], -alpha, alpha,
                                           ALU.mult, ALU.add))
                    step(dve.tensor_tensor(top[:, c], top[:, c], flag[:], ALU.mult))
            step(dve.tensor_scalar(routing.weight[:], top[:], gate, None, ALU.mult))
            dve.sem_inc(chosen_ready, 1)
            dve.wait_ge(counted, 1)
            flat = "p e j -> p (e j)"
            step(dve.tensor_copy(totals[:].rearrange(flat), ps_t[:, 0:E * J]))
            step(dve.tensor_tensor_scan(incl[:].rearrange(flat), ones_row[:], totals[:].rearrange(flat), 0.0,
                                        ALU.mult, ALU.add))
            step(dve.tensor_tensor(excl[:], incl[:], totals[:], ALU.subtract))
            step(dve.tensor_tensor(earlier[:].rearrange(flat), ps_e[:, 0:E * J], excl[:].rearrange(flat), ALU.add))
            step(dve.tensor_tensor(cnt[:], incl[:, :, J - 1], excl[:, :, 0], ALU.subtract))
            step(dve.tensor_scalar(ntiles[:], cnt[:], 1.0 / P, 0.5 - 0.5 / P, ALU.mult, ALU.add))
            step(dve.tensor_scalar(ntiles[:], ntiles[:], MAGIC, None, ALU.add))
            step(dve.tensor_scalar(ntiles[:], ntiles[:], MAGIC, None, ALU.subtract))
            step(dve.tensor_tensor_scan(end[:], ones_row[:, 0:E], ntiles[:], 0.0, ALU.mult, ALU.add))
            step(dve.tensor_tensor(adj[:], end[:], ntiles[:], ALU.subtract))
            step(dve.scalar_tensor_tensor(adj[:], adj[:], float(P), excl[:, :, 0], ALU.mult, ALU.subtract))
            step(dve.tensor_tensor(earlier[:], earlier[:], adj[:].unsqueeze(2).broadcast_to([P, E, J]), ALU.add))
            step(dve.tensor_tensor(earlier[:], earlier[:], chosen[:], ALU.mult))
            step(dve.tensor_reduce(slotf[:], earlier[:].rearrange("p e j -> p j e"), AX.X, ALU.add))
            step(dve.tensor_copy(routing.slot[:], slotf[:]))
            dve.sem_inc(slots_ready, 1)
            ne = experts - 1
            step(dve.tensor_tensor(past[:, :, 0:ne], tidx[:].unsqueeze(2).broadcast_to([P, MAX_TILES, ne]),
                                   end[:, 0:ne].unsqueeze(1).broadcast_to([P, MAX_TILES, ne]), ALU.is_ge))
            step(dve.tensor_reduce(expf[:], past[:, :, 0:ne], AX.X, ALU.add))
            step(dve.tensor_tensor(expf[:], expf[:], least[:], ALU.max))
            step(dve.tensor_copy(routing.expert[:], expf[:]))


def experts_phase(nc, name, x_rows, y_rows, w, routing, n_sorted, n_shared, F, kind):
    FC = F // P
    HC = FC // 2
    HW = HC * P
    mats = 2 if kind == "swiglu" else 1
    up_cols = mats * KC * HW
    down_cols = FC * D + (FC if kind == "relu" else 0)
    ntiles = n_sorted + n_shared
    sets = 3 if n_shared else 2
    with ExitStack() as ctx:
        m = Space(nc, ctx, name)
        wup = m.sb("wup", [P, sets, 2, up_cols])
        wdown = m.sb("wdown", [P, sets, down_cols])
        b2 = m.sb("b2", [P, 2, D])
        x = m.sb("x", [P, 2, D])
        xT = m.sb("xT", [P, 2, KC, P])
        act_out = m.sb("act_out", [P, 2, HW])
        hT = m.sb("hT", [P, 2, FC * P])
        y = m.sb("y", [P, 2, D])
        ps_a = m.psum("ps_a", [P, 2, 512])
        ps_b = m.psum("ps_b", [P, 2, 512])
        ps_x = m.psum("ps_x", [P, 512])
        ps_y = m.psum("ps_y", [P, 2, 512])

        up_in = [[m.sem(f"up_in{half}{par}") for par in range(2)] for half in range(2)]
        down_in = [m.sem("down_in0"), m.sem("down_in1")]
        shared_in = m.sem("shared_in")
        x_in = [m.sem("x_in0"), m.sem("x_in1")]
        stored = [m.sem("stored0"), m.sem("stored1")]
        xT_ready = Tally(m.sem("xT_ready"), 1)
        xT_copied = Tally(m.sem("xT_copied"), 1)
        up_ready = Tally(m.sem("up_ready"), 2)
        act_ready = Tally(m.sem("act_ready"), 2)
        h_ready = Tally(m.sem("h_ready"), 2, 2)
        y_ready = Tally(m.sem("y_ready"), 1, 2)
        y_copied = Tally(m.sem("y_copied"), 1, 2)
        per = 2 if kind == "relu" else 1
        block = m.block()

        def turns(engine, turn):
            turn(0, 0, first=True)
            with engine.Fori(0, (n_sorted - 3) // 2) as pair:
                turn(2 * pair + 1, 1)
                turn(2 * pair + 2, 0)
            turn(n_sorted - 2, 1)
            turn(n_sorted - 1, 0, last=not n_shared, next_shared=True)
            if n_shared:
                turn(n_sorted, 1, shared=True, next_shared=True)
                with engine.Fori(0, n_shared // 2 - 1) as pair:
                    turn(2 * pair + (n_sorted + 1), 0, shared=True, next_shared=True)
                    turn(2 * pair + (n_sorted + 2), 1, shared=True, next_shared=True)
                turn(ntiles - 1, 0, last=True, shared=True)

        @block.sync
        def _(sp):
            def load(i, par, shared):
                reused = not isinstance(i, int) or i >= 2
                if reused:
                    xT_ready.wait(sp, i, -1)
                sp.dma_start(x[:, par], x_rows[i]).then_inc(x_in[par], 16)
                if shared:
                    return
                e = sp.value_load(routing.expert[0:1, i:i + 1] if isinstance(i, int)
                                  else routing.expert[0:1, bass.ds(i, 1)], min_val=0, max_val=E - 1)
                for half in range(2):
                    if reused:
                        up_ready.wait(sp, i, half - 3)
                    sp.dma_start(wup[:, par, half], w["experts"][e][:, half * up_cols:(half + 1) * up_cols]
                                 ).then_inc(up_in[half][par], 16)
                if reused:
                    y_ready.wait(sp, i, -1)
                sp.dma_start(wdown[:, par], w["experts"][e][:, 2 * up_cols:]).then_inc(down_in[par], 16)
                if kind == "relu":
                    if reused:
                        y_copied.wait(sp, i, -1)
                    sp.dma_start(b2[:, par], w["b2"][e].broadcast_to([P, D])).then_inc(down_in[par], 16)

            def turn(i, par, first=False, last=False, shared=False, next_shared=False):
                if first:
                    load(0, 0, False)
                if not last:
                    load(i + 1, 1 - par, next_shared)
                if n_shared and isinstance(i, int) and i == n_sorted - 2:
                    sp.dma_start(wup[:, 2], w["experts"][E - 1][:, 0:2 * up_cols].rearrange("p (h n) -> p h n", h=2)
                                 ).then_inc(shared_in, 16)
                    sp.dma_start(wdown[:, 2], w["experts"][E - 1][:, 2 * up_cols:]).then_inc(shared_in, 16)

            turns(sp, turn)

        @block.tensor
        def _(pe):
            pe.sem_inc(y_ready.sem, 2)

            def turn_x(i, par):
                pe.wait_ge(x_in[par], tile_times(i, par, 1))
                for k in range(KC):
                    last = pe.transpose(ps_x[:, k * P:(k + 1) * P], x[:, par, k * P:(k + 1) * P], w["ident"][:])
                last.then_inc(xT_ready.sem, 1)

            def up(i, par, half, shared):
                if half == 0:
                    xT_copied.wait(pe, i, 1)
                if not shared:
                    pe.wait_ge(up_in[half][par], tile_times(i, par, 1))
                elif half == 0:
                    pe.wait_ge(shared_in, 32)
                wset = 2 if shared else par
                h_ready.wait(pe, i, half - 1)
                for n, bank in enumerate((ps_a, ps_b)[:mats]):
                    for f in range(HC):
                        for k in range(KC):
                            at = (n * KC + k) * HW + f * P
                            last = pe.matmul(bank[:, half, f * P:(f + 1) * P], wup[:, wset, half, at:at + P],
                                             xT[:, par, k, :], start=(k == 0), stop=(k == KC - 1))
                last.then_inc(up_ready.sem, 1)

            def down(i, par, shared):
                if not shared:
                    pe.wait_ge(down_in[par], tile_times(i, par, per))
                h_ready.wait(pe, i, 2)
                y_copied.wait(pe, i, -1)
                wset = 2 if shared else par
                for f in range(FC):
                    last = pe.matmul(ps_y[:, par, 0:D], hT[:, par, f * P:(f + 1) * P],
                                     wdown[:, wset, f * D:(f + 1) * D], start=(f == 0), stop=(f == FC - 1))
                last.then_inc(y_ready.sem, 1)

            def turn(i, par, first=False, last=False, shared=False, next_shared=False):
                if first:
                    turn_x(0, 0)
                up(i, par, 0, shared)
                if not first:
                    down(i - 1, 1 - par, shared and not (isinstance(i, int) and i == n_sorted))
                if not last:
                    turn_x(i + 1, 1 - par)
                up(i, par, 1, shared)

            turns(pe, turn)
            down(ntiles - 1, 0, bool(n_shared))

        @block.scalar
        def _(act):
            act.sem_inc(y_copied.sem, 2)
            act.sem_inc(stored[0], 16)
            act.sem_inc(stored[1], 16)

            def copy_x(i, par):
                xT_ready.wait(act, i, 1)
                act.activation(xT[:, par].rearrange("p k n -> p (k n)"), ps_x[:, 0:D],
                               ACT.Copy).then_inc(xT_copied.sem, 1)

            def activate(i, par, half):
                if kind == "relu":
                    act.wait_ge(down_in[par], tile_times(i, par, per))
                up_ready.wait(act, i, half + 1)
                if kind == "swiglu":
                    act.activation(act_out[:, half], ps_a[:, half, 0:HW], ACT.Silu).then_inc(act_ready.sem, 1)
                if kind == "gelu":
                    act.activation(hT[:, par, half * HW:(half + 1) * HW], ps_a[:, half, 0:HW],
                                   ACT.Gelu).then_inc(h_ready.sem, 1)
                if kind == "relu":
                    for f in range(HC):
                        ff = half * HC + f
                        bias = wdown[:, par, FC * D + ff:FC * D + ff + 1]
                        last = act.activation(hT[:, par, ff * P:(ff + 1) * P], ps_a[:, half, f * P:(f + 1) * P],
                                              ACT.Relu, bias=bias)
                    last.then_inc(h_ready.sem, 1)

            def store(i, par):
                if kind != "relu":
                    y_ready.wait(act, i, 1)
                    act.wait_ge(stored[par], tile_times(i, par, 1))
                    act.activation(y[:, par], ps_y[:, par, 0:D], ACT.Copy).then_inc(y_copied.sem, 1)
                y_copied.wait(act, i, 1)
                act.dma_start(y_rows[i], y[:, par]).then_inc(stored[par], 16)

            def turn(i, par, first=False, last=False, shared=False, next_shared=False):
                if first:
                    if kind != "swiglu":
                        act.sem_inc(h_ready.sem, 2)
                    copy_x(0, 0)
                activate(i, par, 0)
                if not last:
                    copy_x(i + 1, 1 - par)
                if not first:
                    store(i - 1, 1 - par)
                activate(i, par, 1)

            turns(act, turn)
            store(ntiles - 1, 0)
            act.wait_ge(stored[0], 16 * ((ntiles + 1) // 2) + 16)
            act.wait_ge(stored[1], 16 * (ntiles // 2) + 16)

        @block.vector
        def _(dve):
            if kind == "swiglu":
                dve.sem_inc(h_ready.sem, 2)

                def multiply(i, par, half):
                    act_ready.wait(dve, i, half + 1)
                    dve.tensor_tensor(hT[:, par, half * HW:(half + 1) * HW], ps_b[:, half, 0:HW], act_out[:, half],
                                      ALU.mult).then_inc(h_ready.sem, 1)

                def turn(i, par, first=False, last=False, shared=False, next_shared=False):
                    multiply(i, par, 0)
                    multiply(i, par, 1)

                turns(dve, turn)
            if kind == "relu":
                def add_bias(i, par):
                    y_ready.wait(dve, i, 1)
                    dve.wait_ge(stored[par], tile_times(i, par, 1))
                    dve.tensor_tensor(y[:, par], ps_y[:, par, 0:D], b2[:, par], ALU.add).then_inc(y_copied.sem, 1)

                def turn(i, par, first=False, last=False, shared=False, next_shared=False):
                    add_bias(i, par)

                turns(dve, turn)


def combine_phase(nc, name, x_src, x_dst, y_sorted, y_shared, consts, routing, choices, gate_col, gathers):
    QT = NT // 4
    with ExitStack() as ctx:
        m = Space(nc, ctx, name)
        x = m.sb("x", [P, NT, D])
        y = m.sb("y", [P, choices, NT, D])
        ysh = m.sb("ysh", [P, NT, D]) if y_shared is not None else None
        x_in = [m.sem(f"x_in{q}") for q in range(4)]
        gathered = [g.sem for g in gathers]
        all_gathered = [g.target(QT * choices) for g in gathers]
        step_done = m.sem("step_done")
        sum_ready = m.sem("sum_ready")
        stored = m.sem("stored")
        nx = 2 if y_shared is not None else 1
        block = m.block()
        xs = x_src.rearrange("b (t p) d -> p (b t) d", p=P)
        xd = x_dst.rearrange("b (t p) d -> p (b t) d", p=P)
        part = [slice(q * QT, (q + 1) * QT) for q in range(4)]

        @block.sync
        def _(sp):
            for q in range(4):
                sp.dma_start(x[:, part[q]], xs[:, part[q]]).then_inc(x_in[q], 16)
                if y_shared is not None:
                    sp.dma_start(ysh[:, part[q]], y_shared.rearrange("n p d -> p n d")[:, part[q]]).then_inc(x_in[q], 16)
            for q in range(4):
                sp.wait_ge(sum_ready, q + 1)
                sp.dma_start(xd[:, part[q]], x[:, part[q]]).then_inc(stored, 16)
            sp.wait_ge(stored, 64)

        @block.gpsimd
        def _(pool):
            for q in range(4):
                for n in range(q * QT, (q + 1) * QT):
                    for c in range(choices):
                        j = c * NT + n
                        pool.indirect_dma_start(
                            out=y[:, c, n, :], out_offset=None, in_=y_sorted,
                            in_offset=bass.IndirectOffsetOnAxis(ap=routing.slot[:, j:j + 1], axis=0),
                        ).then_inc(gathered[q], 16)

        @block.vector
        def _(dve):
            done = [0]

            def step(ins):
                done[0] += 1
                ins.then_inc(step_done, 1)
                dve.wait_ge(step_done, done[0])

            for q in range(4):
                dve.wait_ge(x_in[q], 16 * nx)
                if y_shared is not None:
                    step(dve.scalar_tensor_tensor(x[:, part[q]], ysh[:, part[q]], consts["gates"][:, gate_col:gate_col + 1],
                                                  x[:, part[q]], ALU.mult, ALU.add))
                dve.wait_ge(gathered[q], all_gathered[q])
                for c in range(choices):
                    for n in range(q * QT, (q + 1) * QT):
                        last = dve.scalar_tensor_tensor(x[:, n, :], y[:, c, n, :], routing.weight[:, c, n:n + 1],
                                                        x[:, n, :], ALU.mult, ALU.add)
                    if c < choices - 1:
                        step(last)
                last.then_inc(sum_ready, 1)


def moe(nc, m, name, x_src, x_dst, consts, w, scratch, choices, F, kind, gate_col, alpha=1.0, shared=False,
        second_norm=False):
    n_sorted = sorted_tiles(choices)
    with ExitStack() as ctx:
        routing = Routing(Space(nc, ctx, name + "_routing"), choices)
        xs, ys = scratch["x_sorted"], scratch["y_sorted"]
        xn = xs[n_sorted:n_sorted + NT] if shared else None
        flat = "n p d -> (n p) d"
        w = dict(w, gate=consts["gates"][:, gate_col:gate_col + 1], ident=consts["ident"], eidx=scratch["eidx"],
                 before=scratch["before"], tidx=scratch["tidx"], scattered=scratch["scattered"])
        route_phase(nc, name + "_route", x_src, xn, xs.rearrange(flat), consts, w, routing, choices, n_sorted,
                    E - 1 if shared else E, alpha, shared, second_norm)
        experts_phase(nc, name + "_experts", xs, ys, w, routing, n_sorted, NT if shared else 0, F, kind)
        combine_phase(nc, name + "_sum", x_src, x_dst, ys.rearrange(flat),
                      ys[n_sorted:n_sorted + NT] if shared else None, consts, routing, choices, gate_col,
                      scratch["gathers"])


def setup_phase(nc, consts, ident_dram, g_dram, x_sorted):
    with ExitStack() as ctx:
        m = Space(nc, ctx, "setup")
        zeros = m.sb("zeros", [P, D])
        const_in = m.sem("const_in")
        zeros_set = m.sem("zeros_set")
        zeros_out = m.sem("zeros_out")
        set_done = m.sem("set_done")
        block = m.block()

        @block.sync
        def _(sp):
            sp.dma_start(consts["ident"][:], ident_dram).then_inc(const_in, 16)
            sp.dma_start(consts["raw_gates"][:], g_dram.broadcast_to([P, 2 * LAYERS])).then_inc(const_in, 16)
            sp.wait_ge(zeros_set, 1)
            sp.dma_start(x_sorted.rearrange("n p d -> p n d"),
                         zeros[:].unsqueeze(1).broadcast_to([P, MAX_TILES, D])).then_inc(zeros_out, 16)
            sp.wait_ge(zeros_out, 16)

        @block.gpsimd
        def _(pool):
            pool.memset(consts["minus_half"][:], -0.5).then_inc(set_done, 1)
            pool.wait_ge(set_done, 1)

        @block.vector
        def _(dve):
            dve.memset(zeros[:], 0.0).then_inc(zeros_set, 1)

        @block.scalar
        def _(act):
            act.wait_ge(const_in, 32)
            act.activation(consts["gates"][:], consts["raw_gates"][:], ACT.Tanh)


def program(nc, t, out, upto):
    with ExitStack() as ctx:
        m = Space(nc, ctx, "all")
        consts = {
            "ident": m.sb("ident", [P, P]),
            "raw_gates": m.sb("raw_gates", [P, 2 * LAYERS]),
            "gates": m.sb("gates", [P, 2 * LAYERS]),
            "minus_half": m.sb("minus_half", [P, TB * H]),
        }
        def dram(name, shape):
            return nc.dram_tensor(name, shape, F32).ap()

        scratch = {
            "x_sorted": dram("x_sorted", [MAX_TILES, P, D]), "y_sorted": dram("y_sorted", [MAX_TILES, P, D]),
            "scattered": Running(m, "scattered"), "gathers": [Running(m, f"gathered{q}") for q in range(4)],
            "eidx": t["eidx"], "before": t["before"], "tidx": t["tidx"],
        }
        bounce = {
            "q": nc.dram_tensor("q_parts", [PARTS, DH, H, S], BF16).ap(),
            "k": nc.dram_tensor("k_parts", [PARTS, DH, H, S], BF16).ap(),
            "m": nc.dram_tensor("m_parts", [PARTS, H, S], BF16).ap(),
        }
        setup_phase(nc, consts, t["ident"], t["gates"], scratch["x_sorted"])
        xs = [t["x"]] + [dram(f"x_after_{i}", [B, S, D]) for i in range(upto - 1)] + [out]
        steps = [
            lambda a, b: attention_phase(nc, "a0", a, b, t["ctx"], consts,
                                         {k: t["a0_" + k] for k in ("wq", "wk", "wv", "wo")}, 0, DH ** -0.5, bounce,
                                         (t["mask"], t["maskT"])),
            lambda a, b: quantised_ffn_phase(nc, "f0", a, b, consts,
                                             {"gate": t["f0_gate"], "up": t["f0_up"], "down": t["f0_down"]}, 4),
            lambda a, b: mlstm_phase(nc, "m1", a, b, t["ctx"], consts,
                                     {k: t["m1_" + k] for k in ("gates", "ib", "fb", "ow", "sel", "lower")}, 1, 8,
                                     False),
            lambda a, b: moe(nc, m, "f1", a, b, consts,
                             {"router": t["f1_router"], "experts": t["f1_experts"], "least": t["f1_least"]}, scratch,
                             1, 1024, "swiglu", 5, alpha=2.0, shared=True),
            lambda a, b: attention_phase(nc, "a2", a, b, t["ctx"], consts,
                                         {k: t["a2_" + k] for k in ("wq", "wk", "wv", "wo", "bq", "bk", "bv", "bo")},
                                         2, D ** -0.5, bounce),
            lambda a, b: moe(nc, m, "f2", a, b, consts,
                             {"router": t["f2_router"], "experts": t["f2_experts"], "b2": t["f2_b2"],
                              "least": t["least"]}, scratch, 1, 1024, "relu", 6),
            lambda a, b: mlstm_phase(nc, "m3", a, b, t["ctx"], consts,
                                     {k: t["m3_" + k] for k in ("gates", "ib", "fb", "ow", "sel", "lower")}, 3, 4,
                                     True),
            lambda a, b: moe(nc, m, "f3", a, b, consts,
                             {"router": t["f3_router"], "experts": t["f3_experts"], "least": t["least"],
                              "gamma": t["f3_gamma"], "beta": t["f3_beta"]}, scratch, 2, 512, "gelu", 7,
                             second_norm=True),
        ]
        for i, step in enumerate(steps[:upto]):
            step(xs[i], xs[i + 1])


LAYERS = 4
UPTO = 8


def _chunks(w):
    return w.reshape(-1, P, w.shape[-1]).transpose(1, 0, 2)


def _by_row(w):
    return w.reshape(-1, H // KC, KC, DH).transpose(0, 2, 3, 1).reshape(-1, D)


def _experts(up, down, bias=None):
    parts = []
    for half in range(2):
        for m in up:
            f = m.shape[2] // 2
            parts.append(np.stack([_chunks(w[:, half * f:(half + 1) * f]).reshape(P, -1) for w in m]))
    parts.append(np.stack([_chunks(w).reshape(P, -1) for w in down]))
    if bias is not None:
        parts.append(np.stack([_chunks(w[:, None]).reshape(P, -1) for w in bias]))
    return np.concatenate(parts, axis=2)


def _mlstm(prefix, wi, bi, wf, bf, scale):
    nh = len(bi)
    gates = np.zeros((wi.shape[1], 64), np.float32)
    gates[:, 0:nh] = wi.T
    gates[:, FG_ROW:FG_ROW + nh] = wf.T
    t, s = np.arange(P)[:, None], np.arange(P)[None, :]
    return {
        prefix + "gates": _chunks(gates), prefix + "ib": bi[:, None], prefix + "fb": bf[:, None],
        prefix + "ow": scale[None, :],
        prefix + "sel": np.tile(np.repeat(np.eye(PART_ROWS, nh, dtype=np.float32), P, axis=1), (3, 1)),
        prefix + "lower": np.where(t > s, np.float32(-1e30), np.float32(0)),
    }


def kernel(**inputs):
    import concourse.bacc as bacc
    from concourse.bass_utils import run_bass_kernel_spmd

    v = {k: np.asarray(a) for k, a in inputs.items()}
    laid = {
        "x": v["x"], "ctx": v["ctx_1024"], "mask": v["mask_BxSxS2_ff0"],
        "maskT": v["mask_BxSxS2_ff0"].transpose(0, 2, 1),
        "ident": np.eye(P, dtype=np.float32),
        "gates": np.concatenate([v["g_xattn"], v["g_ffn"]])[None, :],
        "a0_wq": _chunks(_by_row(v["L0_xattn_Wq"])), "a0_wk": _chunks(_by_row(v["L0_xattn_Wk"])),
        "a0_wv": _chunks(v["L0_xattn_Wv"]), "a0_wo": _chunks(v["L0_xattn_Wo"]),
        "f0_gate": _chunks(v["L0_ffn_w_gate"].T), "f0_up": _chunks(v["L0_ffn_w_up"].T),
        "f0_down": _chunks(v["L0_ffn_w_down"].T),
        **_mlstm("m1_", v["L1_xattn_igate_w"], v["L1_xattn_igate_b"], v["L1_xattn_fgate_w"],
                 v["L1_xattn_fgate_b"], v["L1_xattn_out_w"]),
    }
    rows_of = np.arange(P)
    laid.update({
        "eidx": np.broadcast_to(np.arange(E, dtype=np.float32), (P, E)),
        "before": (rows_of[:, None] < rows_of[None, :]).astype(np.float32),
        "tidx": np.broadcast_to(np.arange(MAX_TILES, dtype=np.float32), (P, MAX_TILES)),
        "least": np.zeros((P, MAX_TILES), np.float32),
        "f1_least": np.broadcast_to(np.where(np.arange(MAX_TILES) < sorted_tiles(1), 0, E - 1).astype(np.float32),
                                    (P, MAX_TILES)),
        "f1_router": _chunks(v["L1_ffn_Wr"]),
        "f1_experts": _experts([np.concatenate([v["L1_ffn_Wg"], v["L1_ffn_Wg_s"][None]]),
                                np.concatenate([v["L1_ffn_Wu"], v["L1_ffn_Wu_s"][None]])],
                               np.concatenate([v["L1_ffn_Wd"], v["L1_ffn_Wd_s"][None]])),
        "a2_wq": _chunks(_by_row(v["L2_xattn_wq"])), "a2_wk": _chunks(_by_row(v["L2_xattn_wk"])),
        "a2_wv": _chunks(v["L2_xattn_wv"]), "a2_wo": _chunks(v["L2_xattn_wo"]),
        "a2_bq": _by_row(v["L2_xattn_bq"]).reshape(KC, P).T, "a2_bk": _by_row(v["L2_xattn_bk"]).reshape(KC, P).T,
        "a2_bv": v["L2_xattn_bv"][None, :], "a2_bo": v["L2_xattn_bo"][None, :],
        "f2_router": _chunks(v["L2_ffn_gate_w"].T),
        "f2_experts": _experts([v["L2_ffn_w1"]], v["L2_ffn_w2"], v["L2_ffn_b1"]),
        "f2_b2": v["L2_ffn_b2"][:, None, :],
        **_mlstm("m3_", v["L3_xattn_w_igate"], v["L3_xattn_b_igate"], v["L3_xattn_w_fgate"],
                 v["L3_xattn_b_fgate"], v["L3_xattn_ln_weight"]),
        "f3_router": _chunks(v["L3_ffn_gate_w"].T),
        "f3_gamma": v["L3_ffn_ln_gamma"][None, :], "f3_beta": v["L3_ffn_ln_beta"][None, :],
        "f3_experts": _experts([v["L3_ffn_w1"].transpose(0, 2, 1)], v["L3_ffn_w2"].transpose(0, 2, 1)),
    })
    nc = bacc.Bacc("TRN2", target_bir_lowering=False, num_devices=1)
    arrays, tensors = {}, {}
    for name, a in laid.items():
        arrays[f"in_{name}"] = np.ascontiguousarray(a)
        tensors[name] = nc.dram_tensor(f"in_{name}", a.shape, mybir.dt.from_np(a.dtype), kind="ExternalInput").ap()
    out = nc.dram_tensor("out_x", [B, S, D], F32, kind="ExternalOutput").ap()
    program(nc, tensors, out, UPTO)
    result = run_bass_kernel_spmd(nc, [arrays], core_ids=[0])
    return result.results[0]["out_x"]
```
